# Optimizing a Trainium2 kernel written in Bass

```python
import numpy as np
import jax
import jax.numpy as jnp

def _softmax(x, axis=-1):
    return jax.nn.softmax(x, axis=axis)

def _gelu(x):
    return jax.nn.gelu(x, approximate=True)

def _silu(x):
    return jax.nn.silu(x)

def _sigmoid(x):
    return jax.nn.sigmoid(x)

def _layernorm(x, axis=-1, eps=1e-05):
    m = jnp.mean(x, axis=axis, keepdims=True)
    v = jnp.var(x, axis=axis, keepdims=True)
    return (x - m) / jnp.sqrt(v + eps)

def _scatter_add(tgt, idx, src, axis=0):
    return tgt.at[idx].add(src)

def _segment_sum(src, seg, n):
    return jax.ops.segment_sum(src, seg, n)
kernel_name = 'mk_perceiver_d2_seqx_r8_cc2c13'

def setup_inputs(seed: int=0):
    np.random.seed(seed)
    _w = jnp.asarray

    def _rec_inputs():
        import jax
        import jax.numpy as jnp
        _rk = jax.random.key(seed)
        x = -0.000125 + 0.9999 * jax.random.normal(jax.random.fold_in(_rk, 1), (8, 64, 256), jnp.float32)
        _lenS = 64 - jax.random.randint(jax.random.fold_in(_rk, 7), (8,), 0, max(1, 64 // 4) + 1, jnp.int32)
        _lenS2 = 1601 - jax.random.randint(jax.random.fold_in(_rk, 8), (8,), 0, max(1, 1601 // 4) + 1, jnp.int32)
        _ctx_2048P = jax.random.normal(jax.random.fold_in(_rk, 11), (8, 16, 256), jnp.float32)
        _ctx_2048c = jax.random.dirichlet(jax.random.fold_in(_rk, 511), 0.3 * jnp.ones((16,), jnp.float32), (8, 1601))
        _ctx_2048t = jnp.einsum('bsk,bkd->bsd', _ctx_2048c, _ctx_2048P)
        _ctx_2048t = _ctx_2048t * jax.lax.rsqrt(jnp.mean(jnp.square(_ctx_2048t)) + 1e-12) * 0.953939
        ctx_2048 = -0.000514642 + 1.00011 * (_ctx_2048t + 0.3 * jax.random.normal(jax.random.fold_in(_rk, 611), (8, 1601, 256), jnp.float32))
        _validS = jnp.arange(64)[None, :] < _lenS[:, None]
        _validS2 = jnp.arange(1601)[None, :] < _lenS2[:, None]
        _causal = jnp.tril(jnp.ones((64, 64), dtype=bool))
        mask_BxS2_bk0 = jnp.logical_not(jnp.broadcast_to(_validS2[:, :], (8, 1601)))
        return (x, ctx_2048, mask_BxS2_bk0)
    x, ctx_2048, mask_BxS2_bk0 = _rec_inputs()

    def _L0_xattn_setup():
        import jax, jax.numpy as jnp
        import numpy as np
        H = 256
        NH = 16
        HD = H // NH
        EPS = 1e-06

        def rmsnorm(x, w, eps=EPS):
            var = jnp.mean(x * x, axis=-1, keepdims=True)
            return x * jax.lax.rsqrt(var + eps) * w
        key = jax.random.key(seed)
        ks = jax.random.split(key, 9)
        B, L, M = (4, 512, 32)
        s = 1.0 / np.sqrt(H)
        return {'hidden_states': jax.random.normal(ks[0], (B, L, H), dtype=jnp.float32), 'memory_tokens': jax.random.normal(ks[1], (B, M, H), dtype=jnp.float32), 'memory_mask': jax.random.randint(ks[2], (B, M), 0, 2).astype(bool), 'norm_w': jnp.ones((H,), dtype=jnp.float32), 'wq': jax.random.normal(ks[3], (H, H), dtype=jnp.float32) * s, 'wk': jax.random.normal(ks[4], (H, H), dtype=jnp.float32) * s, 'wv': jax.random.normal(ks[5], (H, H), dtype=jnp.float32) * s, 'wo': jax.random.normal(ks[6], (H, H), dtype=jnp.float32) * s, 'wg': jax.random.normal(ks[7], (H, H), dtype=jnp.float32) * s}
    _L0_xattn_all = _L0_xattn_setup()
    _L0_xattn_in = {k: v for k, v in _L0_xattn_all.items() if k in ('norm_w', 'wq', 'wk', 'wv', 'wo', 'wg')}
    del _L0_xattn_all

    def _L0_attn_setup():
        import jax, jax.numpy as jnp
        import numpy as np
        key = jax.random.key(seed)
        ks = jax.random.split(key, 5)
        B, S, D = (1, 512, 256)
        H, Dh = (16, 128)
        scale = 1.0 / np.sqrt(D).astype(np.float32)
        return {'x': jax.random.normal(ks[0], (B, S, D), dtype=jnp.float32), 'W_K': jax.random.normal(ks[1], (H, Dh, D), dtype=jnp.float32) * scale, 'W_Q': jax.random.normal(ks[2], (H, Dh, D), dtype=jnp.float32) * scale, 'W_V': jax.random.normal(ks[3], (H, Dh, D), dtype=jnp.float32) * scale, 'W_O': jax.random.normal(ks[4], (D, H * Dh), dtype=jnp.float32) * scale}
    _L0_attn_all = _L0_attn_setup()
    _L0_attn_in = {k: v for k, v in _L0_attn_all.items() if k in ('W_K', 'W_Q', 'W_V', 'W_O')}
    del _L0_attn_all

    def _L0_ffn_setup():
        import jax, jax.numpy as jnp
        import numpy as np
        TOP_K = 8
        NUM_GROUPS = 8
        key = jax.random.key(seed)
        ks = jax.random.split(key, 6)
        T_B, T_S, H, I, E, G = (1, 256, 256, 96, 32, NUM_GROUPS)
        hidden_states = jax.random.normal(ks[0], (T_B, T_S, H), dtype=jnp.float32)
        gate_weight = jax.random.normal(ks[1], (E, H), dtype=jnp.float32) * 0.02
        gate_up_proj = jax.random.normal(ks[2], (E, 2 * I, H), dtype=jnp.float32) * 0.02
        down_proj = jax.random.normal(ks[3], (E, H, I), dtype=jnp.float32) * 0.02
        merge_groups = jax.random.randint(ks[4], (E,), 0, G, dtype=jnp.int64)
        merge_groups = merge_groups.at[:G].set(jnp.arange(G, dtype=jnp.int64))
        dominant_experts = jax.random.randint(ks[5], (G,), 0, E, dtype=jnp.int64)
        return {'hidden_states': hidden_states, 'gate_weight': gate_weight, 'gate_up_proj': gate_up_proj, 'down_proj': down_proj, 'merge_groups': merge_groups, 'dominant_experts': dominant_experts}
    _L0_ffn_all = _L0_ffn_setup()
    _L0_ffn_in = {k: v for k, v in _L0_ffn_all.items() if k in ('gate_weight', 'gate_up_proj', 'down_proj', 'merge_groups', 'dominant_experts')}
    del _L0_ffn_all

    def _L1_xattn_setup():
        import jax, jax.numpy as jnp
        import numpy as np
        DIM = 256
        NHEADS = 32
        HEAD_DIM = DIM // NHEADS
        EPS = 1e-06

        def _rmsnorm(t):
            return t * jax.lax.rsqrt(jnp.mean(t * t, axis=-1, keepdims=True) + EPS)
        key = jax.random.key(seed)
        kx, kc, kq, kk, kv = jax.random.split(key, 5)
        x = jax.random.normal(kx, (2, 512, DIM), dtype=jnp.float32)
        context = jax.random.normal(kc, (2, 64, DIM), dtype=jnp.float32)
        std = 0.02
        Wq = jax.random.normal(kq, (DIM, DIM), dtype=jnp.float32) * std
        Wk = jax.random.normal(kk, (DIM, DIM), dtype=jnp.float32) * std
        Wv = jax.random.normal(kv, (DIM, DIM), dtype=jnp.float32) * std
        return {'x': x, 'context': context, 'Wq': Wq, 'Wk': Wk, 'Wv': Wv}
    _L1_xattn_all = _L1_xattn_setup()
    _L1_xattn_in = {k: v for k, v in _L1_xattn_all.items() if k in ('Wq', 'Wk', 'Wv')}
    del _L1_xattn_all

    def _L1_attn_setup():
        import jax, jax.numpy as jnp
        import numpy as np
        N_EMBED = 256
        N_HEAD = 16
        HEAD_DIM = N_EMBED // N_HEAD
        BATCH, SEQ = (2, 256)

        def _rotate_half(t):
            d = t.shape[-1] // 2
            x1, x2 = (t[..., :d], t[..., d:])
            return jnp.concatenate([-x2, x1], axis=-1)
        key = jax.random.key(seed)
        k1, k2, k3 = jax.random.split(key, 3)
        x = jax.random.normal(k1, (BATCH, SEQ, N_EMBED), dtype=jnp.float32)
        w_attn = jax.random.normal(k2, (N_EMBED, (N_HEAD + 2) * HEAD_DIM), dtype=jnp.float32) * N_EMBED ** (-0.5)
        w_out = jax.random.normal(k3, (N_EMBED, N_EMBED), dtype=jnp.float32) * N_EMBED ** (-0.5)
        return {'x': x, 'w_attn': w_attn, 'w_out': w_out}
    _L1_attn_all = _L1_attn_setup()
    _L1_attn_in = {k: v for k, v in _L1_attn_all.items() if k in ('w_attn', 'w_out')}
    del _L1_attn_all

    def _L1_ffn_setup():
        import jax, jax.numpy as jnp
        import numpy as np
        TOPK = 2
        NORM_TOPK = True
        SCALE = 1.0
        EPS = 1e-09
        key = jax.random.key(seed)
        ks = jax.random.split(key, 9)
        h, i, E = (256, 128, 16)
        std = 0.02
        return {'x': jax.random.normal(ks[0], (1, 256, h), jnp.float32), 'Wr': jax.random.normal(ks[1], (E, h), jnp.float32) * std, 'bias': jnp.zeros((E,), jnp.float32), 'Wg': jax.random.normal(ks[2], (E, h, i), jnp.float32) * std, 'Wu': jax.random.normal(ks[3], (E, h, i), jnp.float32) * std, 'Wd': jax.random.normal(ks[4], (E, i, h), jnp.float32) * std, 'sWg': jax.random.normal(ks[5], (h, i), jnp.float32) * std, 'sWu': jax.random.normal(ks[6], (h, i), jnp.float32) * std, 'sWd': jax.random.normal(ks[7], (i, h), jnp.float32) * std}
    _L1_ffn_all = _L1_ffn_setup()
    _L1_ffn_in = {k: v for k, v in _L1_ffn_all.items() if k in ('Wr', 'bias', 'Wg', 'Wu', 'Wd', 'sWg', 'sWu', 'sWd')}
    del _L1_ffn_all
    return {'x': x, 'ctx_2048': ctx_2048, 'mask_BxS2_bk0': mask_BxS2_bk0, 'L0_xattn_norm_w': _L0_xattn_in['norm_w'], 'L0_xattn_wq': _L0_xattn_in['wq'], 'L0_xattn_wk': _L0_xattn_in['wk'], 'L0_xattn_wv': _L0_xattn_in['wv'], 'L0_xattn_wo': _L0_xattn_in['wo'], 'L0_xattn_wg': _L0_xattn_in['wg'], 'L0_attn_W_K': _L0_attn_in['W_K'], 'L0_attn_W_Q': _L0_attn_in['W_Q'], 'L0_attn_W_V': _L0_attn_in['W_V'], 'L0_attn_W_O': _L0_attn_in['W_O'], 'L0_ffn_gate_weight': _L0_ffn_in['gate_weight'], 'L0_ffn_gate_up_proj': _L0_ffn_in['gate_up_proj'], 'L0_ffn_down_proj': _L0_ffn_in['down_proj'], 'L0_ffn_merge_groups': _L0_ffn_in['merge_groups'], 'L0_ffn_dominant_experts': _L0_ffn_in['dominant_experts'], 'L1_xattn_Wq': _L1_xattn_in['Wq'], 'L1_xattn_Wk': _L1_xattn_in['Wk'], 'L1_xattn_Wv': _L1_xattn_in['Wv'], 'L1_attn_w_attn': _L1_attn_in['w_attn'], 'L1_attn_w_out': _L1_attn_in['w_out'], 'L1_ffn_Wr': _L1_ffn_in['Wr'], 'L1_ffn_bias': _L1_ffn_in['bias'], 'L1_ffn_Wg': _L1_ffn_in['Wg'], 'L1_ffn_Wu': _L1_ffn_in['Wu'], 'L1_ffn_Wd': _L1_ffn_in['Wd'], 'L1_ffn_sWg': _L1_ffn_in['sWg'], 'L1_ffn_sWu': _L1_ffn_in['sWu'], 'L1_ffn_sWd': _L1_ffn_in['sWd']}

def reference(x, ctx_2048, mask_BxS2_bk0, L0_xattn_norm_w, L0_xattn_wq, L0_xattn_wk, L0_xattn_wv, L0_xattn_wo, L0_xattn_wg, L0_attn_W_K, L0_attn_W_Q, L0_attn_W_V, L0_attn_W_O, L0_ffn_gate_weight, L0_ffn_gate_up_proj, L0_ffn_down_proj, L0_ffn_merge_groups, L0_ffn_dominant_experts, L1_xattn_Wq, L1_xattn_Wk, L1_xattn_Wv, L1_attn_w_attn, L1_attn_w_out, L1_ffn_Wr, L1_ffn_bias, L1_ffn_Wg, L1_ffn_Wu, L1_ffn_Wd, L1_ffn_sWg, L1_ffn_sWu, L1_ffn_sWd):
    import jax
    import jax.numpy as jnp

    def _L0_xattn_ref(hidden_states, memory_tokens, memory_mask, norm_w, wq, wk, wv, wo, wg):
        import jax, jax.numpy as jnp
        import numpy as np
        H = 256
        NH = 16
        HD = H // NH
        EPS = 1e-06

        def rmsnorm(x, w, eps=EPS):
            var = jnp.mean(x * x, axis=-1, keepdims=True)
            return x * jax.lax.rsqrt(var + eps) * w
        B, L, C = hidden_states.shape
        M = memory_tokens.shape[1]
        scale = HD ** (-0.5)
        x = rmsnorm(hidden_states, norm_w)
        q = (x @ wq.T).reshape(B, L, NH, HD)
        k = (memory_tokens @ wk.T).reshape(B, M, NH, HD)
        v = (memory_tokens @ wv.T).reshape(B, M, NH, HD)
        attn = jnp.einsum('blhd,bmhd->bhlm', q, k) * scale
        attn = jnp.where(memory_mask[:, None, None, :], attn, -jnp.inf)
        attn = jax.nn.softmax(attn, axis=-1)
        attn = jnp.nan_to_num(attn, nan=0.0)
        out = jnp.einsum('bhlm,bmhd->blhd', attn, v).reshape(B, L, C)
        out = out @ wo.T
        gate = jax.nn.sigmoid(x @ wg.T)
        return gate * out

    def _L0_attn_ref(x, W_K, W_Q, W_V, W_O):
        import jax, jax.numpy as jnp
        import numpy as np
        b, pos, d_model = x.shape
        d_head = W_K.shape[1]
        k = jnp.einsum('ihd,bpd->biph', W_K, x)
        q = jnp.einsum('ihd,bpd->biph', W_Q, x)
        v = jnp.einsum('ihd,bpd->biph', W_V, x)
        scores = jnp.einsum('biph,biqh->biqp', k, q)
        mask = jnp.tril(jnp.ones((pos, pos), dtype=x.dtype))
        masked = scores * mask - jnp.float32(10000000000.0) * (1.0 - mask)
        attn = jax.nn.softmax(masked / jnp.sqrt(jnp.float32(d_head)), axis=-1)
        z = jnp.einsum('biqp,biph->biqh', attn, v)
        z_flat = jnp.transpose(z, (0, 2, 1, 3)).reshape(b, pos, -1)
        out = jnp.einsum('df,bqf->bqd', W_O, z_flat)
        return out

    def _L0_ffn_ref(hidden_states, gate_weight, gate_up_proj, down_proj, merge_groups, dominant_experts):
        import jax, jax.numpy as jnp
        import numpy as np
        TOP_K = 8
        NUM_GROUPS = 8
        B, S, H = hidden_states.shape
        G = dominant_experts.shape[0]
        x = hidden_states.reshape(-1, H)
        logits = jnp.einsum('th,eh->te', x, gate_weight)
        probs = jax.nn.softmax(logits.astype(jnp.float32), axis=-1).astype(logits.dtype)
        top_val, top_idx = jax.lax.top_k(probs, TOP_K)
        top_val = top_val / jnp.sum(top_val, axis=-1, keepdims=True)
        sel_group = merge_groups[top_idx]
        onehot = jax.nn.one_hot(sel_group, G, dtype=top_val.dtype)
        w_tg = jnp.einsum('tk,tkg->tg', top_val, onehot)
        gu = gate_up_proj[dominant_experts]
        dn = down_proj[dominant_experts]
        h = jnp.einsum('th,goh->tgo', x, gu)
        gate, up = jnp.split(h, 2, axis=-1)
        act = jax.nn.silu(gate) * up
        y = jnp.einsum('tgi,ghi->tgh', act, dn)
        out = jnp.einsum('tg,tgh->th', w_tg, y)
        return out.reshape(B, S, H)

    def _L1_xattn_ref(x, context, Wq, Wk, Wv):
        import jax, jax.numpy as jnp
        import numpy as np
        DIM = 256
        NHEADS = 32
        HEAD_DIM = DIM // NHEADS
        EPS = 1e-06

        def _rmsnorm(t):
            return t * jax.lax.rsqrt(jnp.mean(t * t, axis=-1, keepdims=True) + EPS)
        b, n, _ = x.shape
        m = context.shape[1]
        q = x @ Wq.T
        k_raw = context @ Wk.T
        v_raw = context @ Wv.T
        q = q.reshape(b, n, NHEADS, HEAD_DIM).transpose(0, 2, 1, 3)
        kv = jnp.concatenate([k_raw, v_raw], axis=-1)
        kv = kv.reshape(b, m, NHEADS, HEAD_DIM, 2)
        k = kv[..., 0].transpose(0, 2, 1, 3)
        v = kv[..., 1].transpose(0, 2, 1, 3)
        q = _rmsnorm(q)
        k = _rmsnorm(k)
        scale = HEAD_DIM ** (-0.5)
        scores = jnp.einsum('bhnd,bhmd->bhnm', q, k) * scale
        attn = jax.nn.softmax(scores, axis=-1)
        out = jnp.einsum('bhnm,bhmd->bhnd', attn, v)
        return out.transpose(0, 2, 1, 3).reshape(b, n, NHEADS * HEAD_DIM)

    def _L1_attn_ref(x, w_attn, w_out):
        import jax, jax.numpy as jnp
        import numpy as np
        N_EMBED = 256
        N_HEAD = 16
        HEAD_DIM = N_EMBED // N_HEAD
        BATCH, SEQ = (2, 256)

        def _rotate_half(t):
            d = t.shape[-1] // 2
            x1, x2 = (t[..., :d], t[..., d:])
            return jnp.concatenate([-x2, x1], axis=-1)
        B, T, E = x.shape
        H, hd = (N_HEAD, HEAD_DIM)
        qkv = x @ w_attn
        q = qkv[..., :H * hd].reshape(B, T, H, hd).transpose(0, 2, 1, 3)
        k = qkv[..., H * hd:(H + 1) * hd].reshape(B, T, 1, hd).transpose(0, 2, 1, 3)
        v = qkv[..., (H + 1) * hd:].reshape(B, T, 1, hd).transpose(0, 2, 1, 3)
        pos = 10000.0 ** ((-2.0 * jnp.arange(0, hd, 2, dtype=jnp.float32) - 1.0) / hd)
        angles = jnp.arange(T, dtype=jnp.float32)[:, None] * pos[None, :]
        rot = jnp.concatenate([angles, angles], axis=-1)
        cos, sin = (jnp.cos(rot), jnp.sin(rot))
        q = q * cos + _rotate_half(q) * sin
        k = k * cos + _rotate_half(k) * sin
        scores = jnp.matmul(q, jnp.swapaxes(k, -1, -2)) * hd ** (-0.5)
        attn = jax.nn.softmax(scores, axis=-1)
        out = jnp.matmul(attn, v)
        out = out.transpose(0, 2, 1, 3).reshape(B, T, E)
        return out @ w_out

    def _L1_ffn_ref(x, Wr, bias, Wg, Wu, Wd, sWg, sWu, sWd):
        import jax, jax.numpy as jnp
        import numpy as np
        TOPK = 2
        NORM_TOPK = True
        SCALE = 1.0
        EPS = 1e-09
        b, s, h = x.shape
        E = Wr.shape[0]
        xt = x.reshape(b * s, h)
        logits = xt @ Wr.T + bias
        probs = jax.nn.softmax(logits, axis=-1)
        topk_val, topk_idx = jax.lax.top_k(probs, TOPK)
        if NORM_TOPK:
            w = topk_val / (jnp.sum(topk_val, axis=-1, keepdims=True) + EPS)
        else:
            w = topk_val
        w = w * SCALE
        g = jnp.einsum('th,ehi->tei', xt, Wg)
        u = jnp.einsum('th,ehi->tei', xt, Wu)
        y = jnp.einsum('tei,eih->teh', jax.nn.silu(g) * u, Wd)
        oh = jax.nn.one_hot(topk_idx, E, dtype=x.dtype)
        routed = jnp.einsum('tke,tk,teh->th', oh, w, y)
        shared = jax.nn.silu(xt @ sWg) * (xt @ sWu) @ sWd
        return (routed + shared).reshape(b, s, h)
    x = x + _L0_xattn_ref(_layernorm(x, axis=-1), ctx_2048, mask_BxS2_bk0, L0_xattn_norm_w, L0_xattn_wq, L0_xattn_wk, L0_xattn_wv, L0_xattn_wo, L0_xattn_wg)
    x = x + _L0_attn_ref(_layernorm(x, axis=-1), L0_attn_W_K, L0_attn_W_Q, L0_attn_W_V, L0_attn_W_O)
    x = x + _L0_ffn_ref(_layernorm(x, axis=-1), L0_ffn_gate_weight, L0_ffn_gate_up_proj, L0_ffn_down_proj, L0_ffn_merge_groups, L0_ffn_dominant_experts)
    x = x + _L1_xattn_ref(_layernorm(x, axis=-1), ctx_2048, L1_xattn_Wq, L1_xattn_Wk, L1_xattn_Wv)
    x = x + _L1_attn_ref(_layernorm(x, axis=-1), L1_attn_w_attn, L1_attn_w_out)
    x = x + _L1_ffn_ref(_layernorm(x, axis=-1), L1_ffn_Wr, L1_ffn_bias, L1_ffn_Wg, L1_ffn_Wu, L1_ffn_Wd, L1_ffn_sWg, L1_ffn_sWu, L1_ffn_sWd)
    return x

_drawn_inputs = setup_inputs


def setup_inputs(seed=0):
    import zlib

    import numpy as np

    out = dict(_drawn_inputs(seed))
    spreads = {'L0_xattn_norm_w': (1.0, 0.2), 'L1_ffn_bias': (0.0, 0.8)}
    factors = {'L0_ffn_gate_weight': 8.0,
     'L0_ffn_gate_up_proj': 8.0,
     'L0_ffn_down_proj': 8.0,
     'L1_ffn_Wr': 8.0,
     'L1_ffn_Wg': 8.0,
     'L1_ffn_Wu': 8.0,
     'L1_ffn_Wd': 8.0,
     'L1_ffn_sWg': 8.0,
     'L1_ffn_sWu': 8.0,
     'L1_ffn_sWd': 8.0}
    for name, (base, spread) in spreads.items():
        noise = np.random.default_rng([zlib.crc32(name.encode()), seed]).standard_normal(out[name].shape)
        drawn = base * np.exp(spread * noise) if base else spread * noise
        out[name] = jnp.asarray(drawn.astype(out[name].dtype))
    for name, factor in factors.items():
        out[name] = (out[name] * factor).astype(out[name].dtype)
    return out
```

```python
from contextlib import ExitStack

import concourse.bass as bass
import numpy as np
from concourse import mybir

ALU = mybir.AluOpType
ACT = mybir.ActivationFunctionType
AX = mybir.AxisListType
F32 = mybir.dt.float32
U8 = mybir.dt.uint8
BF16 = mybir.dt.bfloat16
I32 = mybir.dt.int32

P = 128
B, S, D = 8, 64, 256
T = B * S
TT = T // P
DC = D // P
S2 = 1601
KT = -(-S2 // P)
S2P = KT * P
NT = B * KT
H0, HD0 = 16, 16
G0 = H0 // 2
HA, HDA = 16, 128
E0, G, I0 = 32, 8, 96
H1, HD1 = 32, 8
G1 = H1 // 2
HB, HDB = 16, 16
QKV = (HB + 2) * HDB
E1, I1 = 16, 128
NX = E1 + 1
KCH = [(c, min(4, KT - c)) for c in range(0, KT, 4)]
NEG = -1e30
LN_EPS, RMS_EPS = 1e-5, 1e-6



def constants():
    p = np.arange(P)[:, None]
    f = np.arange(P)[None, :]
    same = p // S == f // S
    pos = (np.arange(P) % S).astype(np.float32)
    freq = (np.float32(10000.0) ** ((-2.0 * np.arange(0, HDB, 2, dtype=np.float32) - 1.0) / HDB)).astype(np.float32)
    ang = pos[:, None] * freq[None, :]
    ang = np.concatenate([ang, ang], 1).astype(np.float32)
    sin = np.sin(ang)
    sin[:, :HDB // 2] *= -1
    parts = {
        "ident": (p == f),
        "head16": (p // HD0 == np.arange(P // HD0)[None, :]),
        "head8": (p // HD1 == np.arange(P // HD1)[None, :]),
        "mean8": (p // HD1 == f // HD1) / HD1,
        "fold": (p % S == np.arange(S)[None, :]),
        "place": np.stack([(p % S + S * k == f) for k in range(2)], 1),
        "own16": (np.arange(2 * HD0)[None, :] // HD0 == p // S),
        "own8": (np.arange(2 * HD1)[None, :] // HD1 == p // S),
        "causal": np.where(same & (f <= p), 0.0, -1e10),
        "block": np.where(same, 0.0, NEG),
        "cos": np.cos(ang),
        "sin": sin,
        "before": (p < f),
        "count": np.arange(NT + 1)[None, :] * np.ones((P, 1)),
        "tile": np.concatenate([p, p // KT], 1),
        "group": np.ones((P, 1)) * np.arange(G)[None, :],
    }
    at, cols, n = {}, [], 0
    for k, v in parts.items():
        v = np.asarray(v, np.float32).reshape(P, -1)
        at[k] = (n, n + v.shape[1])
        n += v.shape[1]
        cols.append(v)
    return np.ascontiguousarray(np.concatenate(cols, 1)), at


CONST, CONST_AT = constants()


class Chain:

    def __init__(self, eng, sem):
        self.eng, self.sem, self.n, self.loops = eng, sem, 0, []

    def value(self):
        v = self.n
        for var, per in self.loops:
            v = v + var * per
        return v

    def __call__(self, ins):
        ins.then_inc(self.sem, 1)
        self.n += 1
        self.eng.wait_ge(self.sem, self.value())

    def enter(self, var, per):
        self.loops.append((var, per))
        return self.n

    def leave(self, began, count):
        _, per = self.loops.pop()
        assert self.n - began == per, (self.n - began, per)
        self.n = began + per * count


def build(nc, a, out, stages=(1, 2, 3, 4, 5, 6)):
    with ExitStack() as ctx:
        def sb(name, shape, dt=F32):
            return ctx.enter_context(nc.sbuf_tensor(name, shape, dt))

        def sem(name):
            return ctx.enter_context(nc.semaphore(name))

        bank = [ctx.enter_context(nc.psum_tensor(f"bank{i}", [P, 512], F32)) for i in range(8)]

        cst = sb("cst", [P, CONST.shape[1]])

        def const(name):
            lo, hi = CONST_AT[name]
            return cst[:, lo:hi]

        ident = const("ident")
        x = sb("x_sb", [P, TT, D])
        xn = sb("xn", [P, TT, D])
        xnT = sb("xnT", [P, DC, T])
        stats = sb("stats", [P, TT, 6])
        mv = sb("mv", [P, TT, 2])
        lnv = sb("lnv", [P, TT])
        rstd = sb("rstd", [P, TT])
        ms = sb("ms", [P, TT])
        eps = sb("eps", [P, 2])
        w0 = sb("w0", [P, 5, DC, D])
        w1 = sb("w1", [P, 3, DC, D])
        normw = sb("normw", [P, DC])

        consts_loaded = sem("consts_loaded")
        x_loaded = sem("x_loaded")
        w0_loaded = sem("w0_loaded")
        eps_ready = sem("eps_ready")
        var_ready = sem("var_ready")
        rstd_ready = sem("rstd_ready")
        sumsq_ready = sem("sumsq_ready")
        rrms_ready = sem("rrms_ready")
        xn_ready = sem("xn_ready")
        xn_turned = sem("xn_turned")
        xnT_act = sem("xnT_act")
        xnT_dve = sem("xnT_dve")
        act_chain = sem("act_chain")
        dve_chain = sem("dve_chain")

        scratch = sb("scratch", [P, TT, D])
        gate = sb("gate", [P, TT, D])
        q0T = sb("q0T", [P, DC, T])
        q0bd = sb("q0bd", [P, DC, 8, S])
        ctx_tile = sb("ctx_tile", [P, DC, P])
        mask_tiles = sb("mask_tiles", [B * KT, P], U8)
        mask_tile = sb("mask_tile", [1, P], U8)
        tile_any = sb("tile_any", [P, 1])
        tile_at = sb("tile_at", [P, 1])
        tile_hot = sb("tile_hot", [P, NT + 1])
        plan = sb("plan", [1, 2 * (NT + 1) + 1], I32)
        tile_bias = sb("tile_bias", [1, 4, P], BF16)
        ones_row = sb("ones_row", [1, P], BF16)
        k0T = sb("k0T", [P, DC, P])
        v0 = sb("v0", [P, G0, 2 * HD0 + 1])
        probs0 = sb("probs0", [P, G0, P])
        probs0T = sb("probs0T", [P, G0, P])
        m_run = sb("m_run", [P, B, G0])
        m_new = sb("m_new", [P, G0])
        m_tile = sb("m_tile", [P, G0])
        m_step = sb("m_step", [P, G0])
        alpha = sb("alpha", [P, G0])
        o_run = sb("o_run", [P, B, G0, 2 * HD0 + 1])
        l_inv = sb("l_inv", [P, B, G0])
        o0T = sb("o0T", [P, DC, T])

        q0_projected = sem("q0_projected")
        gate_projected = sem("gate_projected")
        gate_exp = sem("gate_exp")
        q0T_ready = sem("q0T_ready")
        ones_ready = sem("ones_ready")
        mask_loaded = sem("mask_loaded")
        any_ready = sem("any_ready")
        any_turned = sem("any_turned")
        tile_at_ready = sem("tile_at_ready")
        tile_hot_ready = sem("tile_hot_ready")
        plan_turned = sem("plan_turned")
        plan_ready = sem("plan_ready")
        tile_chain = sem("tile_chain")
        ctx_loaded = sem("ctx_loaded")
        bias_ready = sem("bias_ready")
        mask_tile_loaded = sem("mask_tile_loaded")
        kv_projected = sem("kv_projected")
        k0_ready = sem("k0_ready")
        v0_ready = sem("v0_ready")
        q0bd_ready = sem("q0bd_ready")
        scored = sem("scored")
        shifted = sem("shifted")
        exped = sem("exped")
        alpha_ready = sem("alpha_ready")
        turned = sem("turned")
        pT_act = sem("pT_act")
        pT_dve = sem("pT_dve")
        attended = sem("attended")
        o_norm_ready = sem("o_norm_ready")
        o_folded = sem("o_folded")
        o0T_ready = sem("o0T_ready")
        out0_projected = sem("out0_projected")

        wa = [sb(f"wa{k}", [P, 8 * D]) for k in range(2)]
        kaT = sb("kaT", [P, 2, T])
        qaT = sb("qaT", [P, 2, T])
        va = sb("va", [P, TT, 2 * HDA])
        pa = sb("pa", [P, 2, TT, P])
        paT = sb("paT", [P, 2, TT, P])
        zaT = sb("zaT", [P, 2, T])
        maxa = sb("maxa", [P, 2, TT])
        suma = sb("suma", [P, 2, TT])
        wa_loaded = [sem(f"wa_loaded{k}") for k in range(2)]
        kqa_projected = sem("kqa_projected")
        va_projected = sem("va_projected")
        kqa_ready = sem("kqa_ready")
        va_ready = sem("va_ready")
        a_scored = sem("a_scored")
        a_maxed = sem("a_maxed")
        a_exped = sem("a_exped")
        a_normed = sem("a_normed")
        a_summed = sem("a_summed")
        a_turned = sem("a_turned")
        paT_ready = sem("paT_ready")
        a_mixed = sem("a_mixed")
        zaT_ready = sem("zaT_ready")
        a_out = sem("a_out")
        a_added = sem("a_added")

        ctxb = sb("ctxb", [P, KT, DC, P])
        v1 = sb("v1", [P, KT, G1, 4 * HD1])
        o_norm = v1[:].rearrange("p t g j -> p (t g j)")[:, 0:B * D].rearrange("p (b g j) -> p b g j", b=B, g=G0)
        q1T = sb("q1T", [P, DC, T])
        q1bd = sb("q1bd", [P, DC, 16, S])
        sq1, r1 = kaT, qaT
        k1T = sb("k1T", [P, DC, S2P])
        p1 = wa
        acc1 = zaT[:, 0, :]
        rden1 = sb("rden1", [P, G1])
        on1 = sb("on1", [P, G1, 2 * HD1])
        o1T = sb("o1T", [P, DC, T])
        w1_loaded = sem("w1_loaded")
        ctxb_loaded = sem("ctxb_loaded")
        q1_projected = sem("q1_projected")
        q1_squared = sem("q1_squared")
        q1_copied = sem("q1_copied")
        q1_meaned = sem("q1_meaned")
        q1_r = sem("q1_r")
        q1bd_ready = sem("q1bd_ready")
        k1_projected = sem("k1_projected")
        k1_squared = sem("k1_squared")
        k1_copied = sem("k1_copied")
        k1_meaned = sem("k1_meaned")
        k1_r = sem("k1_r")
        k1_ready = sem("k1_ready")
        v1_projected = sem("v1_projected")
        v1_ready = sem("v1_ready")
        s1_scored = sem("s1_scored")
        p1_ready = sem("p1_ready")
        p1_used = sem("p1_used")
        acc1_copied = sem("acc1_copied")
        acc1_turned = sem("acc1_turned")
        on1_ready = sem("on1_ready")
        o1_folded = sem("o1_folded")
        o1T_ready = sem("o1T_ready")
        o1_turned = sem("o1_turned")
        r1_ln = sem("r1_ln")
        v1_copied = sem("v1_copied")

        wqkv = sb("wqkv", [P, DC, QKV])
        wout = sb("wout", [P, DC, D])
        NR = HB + 1
        flat = ctxb[:].rearrange("p t c k -> p (t c k)")
        rot, rot2 = (flat[:, k * TT * NR * HDB:(k + 1) * TT * NR * HDB].rearrange("p (t h d) -> p t h d", t=TT, h=NR)
                     for k in range(2))
        krep = sb("krep", [P, TT, 8, HDB])
        vb = sb("vb", [P, TT, HDB])
        qbT, kbd, ob, obT = q0T, [probs0, probs0T], scratch, o0T
        wb_loaded = sem("wb_loaded")
        qkv_projected = sem("qkv_projected")
        rotated = sem("rotated")
        qk_turned = sem("qk_turned")
        qbT_ready = sem("qbT_ready")
        kbd_ready = sem("kbd_ready")
        b_scored = sem("b_scored")
        b_maxed = sem("b_maxed")
        b_exped = sem("b_exped")
        b_normed = sem("b_normed")
        b_turned = sem("b_turned")
        pbT_ready = sem("pbT_ready")
        b_mixed = sem("b_mixed")
        ob_ready = sem("ob_ready")
        ob_turned = sem("ob_turned")
        obT_ready = sem("obT_ready")
        b_out = sem("b_out")
        b_added = sem("b_added")
        b_summed = sem("b_summed")

        NB = 4
        wgu = [sb(f"wgu{k}", [P, DC, 2, P]) for k in range(NB)]
        wdn = [sb(f"wdn{k}", [P, D]) for k in range(NB)]
        hid = [kaT[:, 0, :], kaT[:, 1, :], qaT[:, 0, :], qaT[:, 1, :]]
        wr0 = sb("wr0", [P, DC, E0])
        wr1 = sb("wr1", [P, DC, E1])
        bias1 = sb("bias1", [P, E1])
        merge_i = sb("merge_i", [E0, 1], I32)
        merge_f = sb("merge_f", [E0, 1])
        onehot = sb("onehot", [E0, G])
        dom = sb("dom", [1, G], I32)
        pr = sb("pr", [P, TT, E0])
        rep = sb("rep", [P, TT, E0])
        mx8 = sb("mx8", [P, TT, 8])
        pick = sb("pick", [P, TT, 8])
        rmax = sb("rmax", [P, TT])
        selT = sb("selT", [E0, T])
        we = sb("we", [P, TT, NX])
        router_loaded = sem("router_loaded")
        we_loaded = [sem(f"we_loaded{k}") for k in range(NB)]
        r_scored = sem("r_scored")
        r_shifted = sem("r_shifted")
        r_exped = sem("r_exped")
        sel_ready = sem("sel_ready")
        sel_turned = sem("sel_turned")
        selT_ready = sem("selT_ready")
        w_summed = sem("w_summed")
        e_projected = sem("e_projected")
        silu_ready = sem("silu_ready")
        hid_ready = sem("hid_ready")
        e_down = sem("e_down")
        e_added = sem("e_added")
        we_ready = sem("we_ready")
        stored = sem("stored")
        dve_done = sem("dve_done")

        COUNT_AT = 2 * (NT + 1)
        LN_AT = {st: k for k, st in enumerate(stages)}
        N1 = G if 3 in stages else 0
        R1 = 1 if 3 in stages else 0
        block = ctx.enter_context(nc.Block())
        xd = a["x"].rearrange("b s d -> (b s) d").rearrange("(t p) d -> p t d", p=P)
        od = out.rearrange("b s d -> (b s) d").rearrange("(t p) d -> p t d", p=P)

        @block.sync
        def _(sp):
            sp.dma_start(x[:], xd).then_inc(x_loaded, 16)
            sp.dma_start(cst[:], a["const"]).then_inc(consts_loaded, 16)
            sp.dma_start(w0[:], a["w0"]).then_inc(w0_loaded, 16)
            sp.dma_start(normw[:], a["norm_w"]).then_inc(w0_loaded, 16)
            sp.dma_start(mask_tiles[:], a["mask"]).then_inc(mask_loaded, 16)

            def l0_xattn():
                def load(i):
                    n = sp.value_load(plan[0:1, bass.ds(i, 1)], min_val=0, max_val=NT - 1)
                    sp.dma_start(ctx_tile[:], a["ctxT"][bass.ds(n, 1), :, :, :].rearrange("n p c k -> p (n c) k"))\
                      .then_inc(ctx_loaded, 16)
                    sp.dma_start(mask_tile[:], a["mask"][bass.ds(n, 1), :]).then_inc(mask_tile_loaded, 16)
                sp.wait_ge(plan_ready, 1)
                n_tiles = sp.value_load(plan[0:1, COUNT_AT:COUNT_AT + 1], min_val=1, max_val=NT)
                load(0)
                with sp.Fori(0, n_tiles) as i:
                    sp.wait_ge(bias_ready, i + 1)
                    sp.wait_ge(kv_projected, i + 1)
                    load(i + 1)

            def l0_attn():
                def load(n, k):
                    sp.dma_start(wa[k][:], a["wa"][bass.ds(n, 1), :, :].rearrange("n p f -> p (n f)")).then_inc(wa_loaded[k], 16)
                for k in range(2):
                    load(k, k)
                with sp.Fori(0, HA // 4 - 1) as i:
                    for k in range(2):
                        n = i * 2 + k
                        sp.wait_ge(a_out, n + 1)
                        load(n + 2, k)

            def load_expert(gu, dn, width, index, k):
                sp.dma_start(wgu[k][:, :, :, 0:width], gu[bass.ds(index, 1), :, :, :, :].rearrange("n p c u i -> p (n c) u i"))\
                  .then_inc(we_loaded[k], 16)
                sp.dma_start(wdn[k][0:width, :], dn[bass.ds(index, 1), :, :].rearrange("n p f -> p (n f)"))\
                  .then_inc(we_loaded[k], 16)

            def l0_ffn():
                def load(n, k):
                    e = sp.value_load(dom[0:1, bass.ds(n, 1)], min_val=0, max_val=E0 - 1)
                    load_expert(a["gu0"], a["dn0"], I0, e, k)
                for k in range(NB):
                    load(k, k)
                with sp.Fori(0, G // NB - 1) as i:
                    for k in range(NB):
                        n = i * NB + k
                        sp.wait_ge(e_down, n + 1)
                        load(n + NB, k)

            def l1_xattn():
                sp.dma_start(w1[:], a["w1"]).then_inc(w1_loaded, 16)
                with sp.Fori(0, B) as b:
                    sp.wait_ge(v1_ready, b + 1)
                    sp.dma_start(ctxb[:], a["ctxT"][bass.ds(b * KT, KT), :, :, :].rearrange("t p c k -> p t (c k)"))\
                      .then_inc(ctxb_loaded, 16)

            def l1_attn():
                sp.dma_start(wqkv[:], a["wqkv"]).then_inc(wb_loaded, 16)
                sp.dma_start(wout[:], a["wout"]).then_inc(wb_loaded, 16)

            def l1_ffn():
                for k in range(NB):
                    if N1:
                        sp.wait_ge(e_down, N1 - NB + k + 1)
                    load_expert(a["gu1"], a["dn1"], I1, k, k)
                with sp.Fori(0, E1 // NB - 1) as i:
                    for k in range(NB):
                        n = i * NB + k
                        sp.wait_ge(e_down, N1 + n + 1)
                        load_expert(a["gu1"], a["dn1"], I1, n + NB, k)
                sp.wait_ge(e_down, N1 + E1 - NB + 1)
                load_expert(a["gu1"], a["dn1"], I1, E1, 0)

            sp.dma_start(wr0[:], a["wr0"]).then_inc(router_loaded, 16)
            sp.dma_start(wr1[:], a["wr1"]).then_inc(router_loaded, 16)
            sp.dma_start(bias1[:], a["bias1"].broadcast_to([P, E1])).then_inc(router_loaded, 16)
            sp.dma_start(merge_i[:], a["merge"]).then_inc(router_loaded, 16)
            sp.dma_start(dom[:], a["dom"]).then_inc(router_loaded, 16)
            if 1 in stages:
                l0_xattn()
            if 2 in stages:
                l0_attn()
            if 3 in stages:
                sp.wait_ge(router_loaded, 80)
                l0_ffn()
            if 4 in stages:
                l1_xattn()
            if 5 in stages:
                l1_attn()
            if 6 in stages:
                l1_ffn()
            sp.wait_ge(dve_done, 1)
            sp.dma_start(od, x[:]).then_inc(stored, 16)
            sp.wait_ge(mask_loaded, 16)
            sp.wait_ge(router_loaded, 80)
            sp.wait_ge(w0_loaded, 32)
            sp.wait_ge(stored, 16)

        @block.tensor
        def _(pe):
            def layernorm(stage):
                s = LN_AT[stage]
                for i in range(TT):
                    pe.wait_ge(xn_ready, TT * s + i + 1)
                    for c in range(DC):
                        mm = pe.transpose(bank[c][:, i * P:(i + 1) * P], xn[:, i, c * P:(c + 1) * P], ident)
                mm.then_inc(xn_turned, 1)
                pe.wait_ge(xnT_act, s + 1)
                pe.wait_ge(xnT_dve, s + 1)

            def l0_xattn():
                pe.wait_ge(w0_loaded, 32)
                for m in range(DC):
                    for c in range(DC):
                        mm = pe.matmul(bank[2 + m][:], w0[:, 0, c, m * P:(m + 1) * P], xnT[:, c, :],
                                       start=(c == 0), stop=(c == DC - 1))
                mm.then_inc(q0_projected, 1)
                for i in range(TT):
                    for c in range(DC):
                        mm = pe.matmul(bank[4 + i][:, 0:D], xnT[:, c, i * P:(i + 1) * P], w0[:, 1, c, :],
                                       start=(c == 0), stop=(c == DC - 1))
                mm.then_inc(gate_projected, 1)
                pe.wait_ge(any_ready, 1)
                pe.matmul(bank[0][0:NT, 0:1], const("before")[0:NT, 0:NT], tile_any[0:NT, :], start=True, stop=True)\
                  .then_inc(any_turned, 1)
                pe.wait_ge(tile_hot_ready, 1)
                for k in range(2):
                    pe.matmul(bank[1][0:1, k * (NT + 1):(k + 1) * (NT + 1)], const("tile")[0:NT, k:k + 1], tile_hot[0:NT, :],
                              start=True, stop=True)
                pe.matmul(bank[1][0:1, COUNT_AT:COUNT_AT + 1], tile_any[0:NT, :], tile_any[0:NT, :], start=True, stop=True)\
                  .then_inc(plan_turned, 1)
                pe.wait_ge(ones_ready, 1)
                pe.wait_ge(gate_exp, 1)
                pe.wait_ge(plan_ready, 1)
                n_tiles = pe.value_load(plan[0:1, COUNT_AT:COUNT_AT + 1], min_val=1, max_val=NT)

                def project(i):
                    pe.wait_ge(ctx_loaded, 16 * (i + 1))
                    for m in range(DC):
                        for c in range(DC):
                            pe.matmul(bank[0][:, m * P:(m + 1) * P], w0[:, 2, c, m * P:(m + 1) * P],
                                      ctx_tile[:, c, :], start=(c == 0), stop=(c == DC - 1))
                    for c in range(DC):
                        mm = pe.matmul(bank[1][:, 0:D], ctx_tile[:, c, :], w0[:, 3, c, :],
                                       start=(c == 0), stop=(c == DC - 1))
                    mm.then_inc(kv_projected, 1)

                def scores(i):
                    pe.wait_ge(q0bd_ready, i + 1)
                    pe.wait_ge(bias_ready, i + 1)
                    pe.wait_ge(k0_ready, i + 1)
                    for m in range(DC):
                        pe.matmul(bank[2 + m][:], ones_row[:], tile_bias[:].rearrange("p g k -> p (g k)"),
                                  start=True, stop=False, skip_group_check=True)
                        for g in range(4):
                            mm = pe.matmul(bank[2 + m][:, g * P:(g + 1) * P],
                                           q0bd[:, m, 2 * g:2 * g + 2, :].rearrange("p h q -> p (h q)"),
                                           k0T[:, m, :], start=False, stop=True, skip_group_check=True)
                    mm.then_inc(scored, 1)

                project(0)
                scores(0)
                with pe.Fori(0, n_tiles) as i:
                    pe.wait_ge(v0_ready, i + 1)
                    project(i + 1)
                    pe.wait_ge(exped, i + 1)
                    for g in range(G0):
                        mm = pe.transpose(bank[4 + g // 4][:, (g % 4) * P:(g % 4 + 1) * P], probs0[:, g, :], ident)
                    mm.then_inc(turned, 1)
                    scores(i + 1)
                    pe.wait_ge(pT_act, i + 1)
                    pe.wait_ge(pT_dve, i + 1)
                    for g in range(G0):
                        w = 2 * HD0 + 1
                        mm = pe.matmul(bank[6][:, g * w:(g + 1) * w], probs0T[:, g, :], v0[:, g, :], start=True, stop=True)
                    mm.then_inc(attended, 1)
                pe.wait_ge(o_norm_ready, 1)
                for c in range(DC):
                    for b in range(B):
                        mm = pe.matmul(bank[c][:, b * S:(b + 1) * S],
                                       o_norm[:, b, 4 * c:4 * c + 4, :].rearrange("p g j -> p (g j)"), const("fold"),
                                       start=True, stop=True)
                mm.then_inc(o_folded, 1)
                pe.wait_ge(o0T_ready, 2)
                for i in range(TT):
                    for c in range(DC):
                        mm = pe.matmul(bank[4 + i][:, 0:D], o0T[:, c, i * P:(i + 1) * P], w0[:, 4, c, :],
                                       start=(c == 0), stop=(c == DC - 1))
                mm.then_inc(out0_projected, 1)

            def l0_attn():
                with pe.Fori(0, HA // 4) as i:
                    for k in range(2):
                        n = i * 2 + k
                        w = wa[k]
                        pe.wait_ge(wa_loaded[k], 16 * (i + 1))
                        for u in range(2):
                            for j in range(2):
                                for c in range(DC):
                                    o = ((u * 2 + j) * DC + c) * HDA
                                    mm = pe.matmul(bank[3 * u + j][:], w[:, o:o + HDA], xnT[:, c, :],
                                                   start=(c == 0), stop=(c == DC - 1))
                            mm.then_inc(kqa_projected, 1)
                        pe.wait_ge(a_added, n + 1)
                        for t in range(TT):
                            for c in range(DC):
                                o = 4 * D + c * D
                                mm = pe.matmul(bank[2 + 3 * (t // 2)][:, (t % 2) * D:(t % 2 + 1) * D],
                                               xnT[:, c, t * P:(t + 1) * P], w[:, o:o + D], start=(c == 0), stop=(c == DC - 1))
                        mm.then_inc(va_projected, 1)
                        for u in range(2):
                            pe.wait_ge(kqa_ready, 2 * n + u + 1)
                            for t in range(TT):
                                mm = pe.matmul(bank[6 + u][:, t * P:(t + 1) * P], qaT[:, u, t * P:(t + 1) * P],
                                               kaT[:, u, t * P:(t + 1) * P], start=True, stop=True)
                            mm.then_inc(a_scored, 1)
                        for u in range(2):
                            pe.wait_ge(a_normed, 2 * n + u + 1)
                            for t in range(TT):
                                mm = pe.transpose(bank[3 * u][:, t * P:(t + 1) * P], pa[:, u, t, :], ident)
                            mm.then_inc(a_turned, 1)
                        pe.wait_ge(va_ready, n + 1)
                        for u in range(2):
                            pe.wait_ge(paT_ready, 2 * n + u + 1)
                            for t in range(TT):
                                mm = pe.matmul(bank[1 + 3 * u][:, t * P:(t + 1) * P], va[:, t, u * HDA:(u + 1) * HDA],
                                               paT[:, u, t, :], start=True, stop=True)
                            mm.then_inc(a_mixed, 1)
                        pe.wait_ge(zaT_ready, 2 * n + 2)
                        for t in range(TT):
                            for u in range(2):
                                o = 6 * D + u * D
                                mm = pe.matmul(bank[2 + 3 * (t // 2)][:, (t % 2) * D:(t % 2 + 1) * D],
                                               zaT[:, u, t * P:(t + 1) * P], w[:, o:o + D], start=(u == 0), stop=(u == 1))
                        mm.then_inc(a_out, 1)

            def router(r, w, ne):
                for t in range(TT):
                    for c in range(DC):
                        mm = pe.matmul(bank[7][:, t * ne:(t + 1) * ne], xnT[:, c, t * P:(t + 1) * P], w[:, c, :],
                                       start=(c == 0), stop=(c == DC - 1))
                mm.then_inc(r_scored, 1)

            def up(k, n, width, loaded):
                pe.wait_ge(we_loaded[k], loaded)
                for j in range(2):
                    for c in range(DC):
                        mm = pe.matmul(bank[2 * (k % 2) + j][0:width, :], wgu[k][:, c, j, 0:width], xnT[:, c, :],
                                       start=(c == 0), stop=(c == DC - 1))
                mm.then_inc(e_projected, 1)

            def down(k, n, width):
                pe.wait_ge(hid_ready, n + 1)
                for t in range(TT):
                    mm = pe.matmul(bank[4 + 2 * (k % 2) + t // 2][:, (t % 2) * D:(t % 2 + 1) * D],
                                   hid[k][0:width, t * P:(t + 1) * P], wdn[k][0:width, :], start=True, stop=True)
                mm.then_inc(e_down, 1)

            def experts(n0, first, count, width, one_more):
                with pe.Fori(0, count // NB) as i:
                    for k in range(0, NB, 2):
                        n = n0 + i * NB + k
                        up(k, n, width, 32 * (first + i + 1))
                        up(k + 1, n + 1, width, 32 * (first + i + 1))
                        pe.wait_ge(e_added, n + 1)
                        down(k, n, width)
                        down(k + 1, n + 1, width)
                if one_more:
                    n = n0 + count
                    up(0, n, width, 32 * (first + count // NB + 1))
                    pe.wait_ge(e_added, n + 1)
                    down(0, n, width)

            def l0_ffn():
                pe.wait_ge(router_loaded, 80)
                router(0, wr0, E0)
                pe.wait_ge(sel_ready, 1)
                for t in range(TT):
                    mm = pe.transpose(bank[6][0:E0, t * P:(t + 1) * P], pr[:, t, :], ident)
                mm.then_inc(sel_turned, 1)
                pe.wait_ge(selT_ready, 1)
                for t in range(TT):
                    mm = pe.matmul(bank[5][:, t * G:(t + 1) * G], selT[:, t * P:(t + 1) * P], onehot[:], start=True, stop=True)
                mm.then_inc(w_summed, 1)
                pe.wait_ge(we_ready, 1)
                experts(0, 0, G, I0, False)

            def l1_ffn():
                pe.wait_ge(router_loaded, 80)
                router(1, wr1, E1)
                pe.wait_ge(we_ready, R1 + 1)
                experts(N1, N1 // NB, E1, I1, True)

            def l1_xattn():
                pe.wait_ge(w1_loaded, 16)
                for m in range(DC):
                    for c in range(DC):
                        mm = pe.matmul(bank[2 + m][:], w1[:, 0, c, m * P:(m + 1) * P], xnT[:, c, :],
                                       start=(c == 0), stop=(c == DC - 1))
                mm.then_inc(q1_projected, 1)
                pe.wait_ge(q1_squared, 1)
                for m in range(DC):
                    mm = pe.matmul(bank[4 + m][:], const("mean8"), sq1[:, m, :], start=True, stop=True)
                mm.then_inc(q1_meaned, 1)
                pe.wait_ge(q1_copied, 1)
                pe.wait_ge(q1_r, 1)

                def scores(b, t):
                    keys = min(P, S2 - t * P)
                    for m in range(DC):
                        if t:
                            pe.wait_ge(p1_ready, b * 2 * KT + 2 * t + m - 1)
                        for h in range(2):
                            mm = pe.matmul(bank[4 + 2 * m + h][0:keys, :], k1T[:, m, t * P:t * P + keys],
                                           q1bd[:, m, 8 * h:8 * h + 8, :].rearrange("p h q -> p (h q)"), start=True, stop=True)
                        mm.then_inc(s1_scored, 1)

                def mix(b, t):
                    keys = min(P, S2 - t * P)
                    pe.wait_ge(p1_ready, b * 2 * KT + 2 * t + 2)
                    for g in range(G1):
                        j, s = g % 4, g // 4
                        mm = pe.matmul(bank[3][32 * j:32 * j + 32, s * P:(s + 1) * P], v1[0:keys, t, g, :],
                                       p1[t % 2][0:keys, g * P:(g + 1) * P], start=(t == 0 and s == 0), stop=(t == KT - 1),
                                       skip_group_check=True)
                    mm.then_inc(p1_used, 1)

                with pe.Fori(0, B) as b:
                    pe.wait_ge(o1T_ready, b + 1)
                    pe.wait_ge(ctxb_loaded, 16 * (b + 1))
                    for j, (t0, nt) in enumerate(KCH):
                        n = b * len(KCH) + j
                        for m in range(DC):
                            for c in range(DC):
                                mm = pe.matmul(bank[m][:, 0:nt * P], w1[:, 1, c, m * P:(m + 1) * P], ctxb[:, t0:t0 + nt, c, :],
                                               start=(c == 0), stop=(c == DC - 1))
                        mm.then_inc(k1_projected, 1)
                        for t in range(t0, t0 + nt):
                            if t >= 1:
                                pe.wait_ge(v1_copied, b * KT + t)
                            for c in range(DC):
                                mm = pe.matmul(bank[3][:, 0:D], ctxb[:, t, c, :], w1[:, 2, c, :],
                                               start=(c == 0), stop=(c == DC - 1))
                            mm.then_inc(v1_projected, 1)
                        pe.wait_ge(k1_squared, n + 1)
                        pe.wait_ge(k1_copied, n + 1)
                        for m in range(DC):
                            mm = pe.matmul(bank[4 + m][:, 0:nt * P], const("mean8"), sq1[:, m, 0:nt * P], start=True, stop=True)
                        mm.then_inc(k1_meaned, 1)
                    pe.wait_ge(v1_copied, b * KT + KT)
                    pe.wait_ge(k1_ready, (b + 1) * len(KCH) + 1)
                    pe.wait_ge(q1bd_ready, b + 1)
                    scores(b, 0)
                    for t in range(KT):
                        if t + 1 < KT:
                            scores(b, t + 1)
                        mix(b, t)
                    pe.wait_ge(acc1_copied, b + 1)
                    for s in range(4):
                        mm = pe.transpose(bank[0][:, s * P:(s + 1) * P], acc1[:, s * P:(s + 1) * P], ident)
                    mm.then_inc(acc1_turned, 1)
                    pe.wait_ge(on1_ready, b + 1)
                    for c in range(DC):
                        mm = pe.matmul(bank[1][:, c * S:(c + 1) * S],
                                       on1[:, 8 * c:8 * c + 8, :].rearrange("p g j -> p (g j)"), const("fold"),
                                       start=True, stop=True)
                    mm.then_inc(o1_folded, 1)
                pe.wait_ge(o1T_ready, B + 1)
                for c in range(DC):
                    for i in range(TT):
                        mm = pe.transpose(bank[i][:, c * P:(c + 1) * P], o1T[:, c, i * P:(i + 1) * P], ident)
                mm.then_inc(o1_turned, 1)

            def l1_attn():
                pe.wait_ge(wb_loaded, 32)
                for t in range(TT):
                    for c in range(DC):
                        mm = pe.matmul(bank[2 + t][:, 0:QKV], xnT[:, c, t * P:(t + 1) * P], wqkv[:, c, :],
                                       start=(c == 0), stop=(c == DC - 1))
                    mm.then_inc(qkv_projected, 1)

                def turn_qk(t):
                    pe.wait_ge(rotated, t + 1)
                    if t >= 1:
                        pe.wait_ge(qbT_ready, t)
                        pe.wait_ge(kbd_ready, t)
                    qk = rot[:, t, 0:HB, :].rearrange("p h d -> p (h d)")
                    for m in range(DC):
                        pe.transpose(bank[0][:, m * P:(m + 1) * P], qk[:, m * P:(m + 1) * P], ident)
                    pe.transpose(bank[0][:, 2 * P:3 * P], krep[:, t, :, :].rearrange("p h d -> p (h d)"), ident)\
                      .then_inc(qk_turned, 1)

                def scores(j):
                    t, m, h = j // 4, j // 2 % 2, j % 2
                    if j % 4 == 0:
                        pe.wait_ge(qbT_ready, t + 1)
                        pe.wait_ge(kbd_ready, t + 1)
                    if j >= 2:
                        pe.wait_ge(b_maxed, j - 1)
                    pe.matmul(bank[6 + j % 2][:], qbT[:, m, t * P:(t + 1) * P],
                              kbd[t % 2][:, 4 * h:4 * h + 4, :].rearrange("p h k -> p (h k)"), start=True, stop=True)\
                      .then_inc(b_scored, 1)

                def mix(j):
                    t = j // 4
                    pe.wait_ge(b_normed, j + 1)
                    if j >= 1:
                        pe.wait_ge(pbT_ready, j)
                    for h in range(4):
                        mm = pe.transpose(bank[1][:, h * P:(h + 1) * P], pa[:, j % 2, h, :], ident)
                    mm.then_inc(b_turned, 1)
                    pe.wait_ge(pbT_ready, j + 1)
                    if j >= 4 and j % 4 == 0:
                        pe.wait_ge(ob_ready, t)
                    for h in range(4):
                        k = (j % 4 * 4 + h) * HDB
                        mm = pe.matmul(bank[2][:, k:k + HDB], paT[:, j % 2, h, :], vb[:, t, :], start=True, stop=True)
                    mm.then_inc(b_mixed, 1)

                def project(t):
                    pe.wait_ge(ob_ready, t + 1)
                    if t >= 1:
                        pe.wait_ge(b_added, t)
                    for c in range(DC):
                        mm = pe.transpose(bank[3][:, c * P:(c + 1) * P], ob[:, t, c * P:(c + 1) * P], ident)
                    mm.then_inc(ob_turned, 1)
                    pe.wait_ge(obT_ready, t + 1)
                    for c in range(DC):
                        mm = pe.matmul(bank[4][:, 0:D], obT[:, c, t * P:(t + 1) * P], wout[:, c, :],
                                       start=(c == 0), stop=(c == DC - 1))
                    mm.then_inc(b_out, 1)

                pe.wait_ge(rotated, TT)
                turn_qk(0)
                for j in range(4 * TT + 1):
                    if j < 4 * TT:
                        scores(j)
                    if j % 4 == 1 and j // 4 + 1 < TT:
                        turn_qk(j // 4 + 1)
                    if j >= 1:
                        mix(j - 1)
                    if j >= 4 and j % 4 == 0:
                        project(j // 4 - 1)

            pe.wait_ge(consts_loaded, 16)
            if 1 in stages:
                layernorm(1)
                l0_xattn()
            if 2 in stages:
                layernorm(2)
                l0_attn()
            if 3 in stages:
                layernorm(3)
                l0_ffn()
            if 4 in stages:
                layernorm(4)
                l1_xattn()
            if 5 in stages:
                layernorm(5)
                l1_attn()
            if 6 in stages:
                layernorm(6)
                l1_ffn()

        @block.scalar
        def _(act):
            chain = Chain(act, act_chain)

            def rsqrt(dst, src, bias, scale=1.0):
                chain(act.activation(lnv[:], src, ACT.Ln, bias=bias, scale=scale))
                return act.activation(dst, lnv[:], ACT.Exp, scale=-0.5)

            def layernorm(stage):
                s = LN_AT[stage]
                act.wait_ge(var_ready, s + 1)
                rsqrt(rstd[:], mv[:, :, 1], eps[:, 0:1]).then_inc(rstd_ready, 1)
                if stage == 1:
                    act.wait_ge(sumsq_ready, 1)
                    rsqrt(rstd[:], ms[:], eps[:, 1:2], 1.0 / D).then_inc(rrms_ready, 1)
                act.wait_ge(xn_turned, s + 1)
                if stage == 1:
                    act.wait_ge(w0_loaded, 32)
                    act.activation(xnT[:, 0, :], bank[0][:], ACT.Copy, scale=normw[:, 0:1]).then_inc(xnT_act, 1)
                else:
                    act.activation(xnT[:, 0, :], bank[0][:], ACT.Copy).then_inc(xnT_act, 1)

            def l0_xattn():
                act.wait_ge(q0_projected, 1)
                for m in range(DC):
                    act.activation(q0T[:, m, :], bank[2 + m][:], ACT.Copy, scale=HD0 ** -0.5).then_inc(q0T_ready, 1)
                act.wait_ge(gate_projected, 1)
                for i in range(TT):
                    e = act.activation(gate[:, i, :], bank[4 + i][:, 0:D], ACT.Exp, scale=-1.0)
                e.then_inc(gate_exp, 1)
                act.wait_ge(plan_ready, 1)
                n_tiles = act.value_load(plan[0:1, COUNT_AT:COUNT_AT + 1], min_val=1, max_val=NT)

                def copy_k(i):
                    act.wait_ge(kv_projected, i + 1)
                    act.activation(k0T[:].rearrange("p m k -> p (m k)"), bank[0][:, 0:D], ACT.Copy).then_inc(k0_ready, 1)

                copy_k(0)
                with act.Fori(0, n_tiles) as i:
                    act.wait_ge(shifted, i + 1)
                    act.activation(probs0[:], probs0[:], ACT.Exp).then_inc(exped, 1)
                    act.activation(alpha[:], m_step[:], ACT.Exp).then_inc(alpha_ready, 1)
                    copy_k(i + 1)
                    act.wait_ge(turned, i + 1)
                    act.activation(probs0T[:, 0:4, :].rearrange("p g k -> p (g k)"), bank[4][:], ACT.Copy).then_inc(pT_act, 1)
                act.wait_ge(o_folded, 1)
                act.activation(o0T[:, 0, :], bank[0][:], ACT.Copy).then_inc(o0T_ready, 1)

            def l0_attn():
                with act.Fori(0, HA // 4) as i:
                    for k in range(2):
                        n = i * 2 + k
                        for u in range(2):
                            act.wait_ge(kqa_projected, 2 * n + u + 1)
                            act.activation(kaT[:, u, :], bank[3 * u][:], ACT.Copy)
                            act.activation(qaT[:, u, :], bank[3 * u + 1][:], ACT.Copy).then_inc(kqa_ready, 1)
                        for u in range(2):
                            act.wait_ge(a_maxed, 2 * n + u + 1)
                            for t in range(TT):
                                e = act.activation(pa[:, u, t, :], pa[:, u, t, :], ACT.Exp, bias=maxa[:, u, t:t + 1],
                                                   scale=HDA ** -0.5, accum_out=suma[:, u, t:t + 1])
                            e.then_inc(a_exped, 1)
                        for u in range(2):
                            act.wait_ge(a_turned, 2 * n + u + 1)
                            act.activation(paT[:, u, :, :].rearrange("p t q -> p (t q)"), bank[3 * u][:], ACT.Copy).then_inc(paT_ready, 1)

            def router(r):
                act.wait_ge(r_shifted, r * R1 + 1)
                ne = (E0, E1)[r]
                act.activation(pr[:, :, 0:ne], pr[:, :, 0:ne], ACT.Exp).then_inc(r_exped, 1)

            def experts(n0, count, width, one_more):
                def silu(k, n):
                    act.wait_ge(e_projected, n + 1)
                    act.activation(hid[k][0:width, :], bank[2 * (k % 2)][0:width, :], ACT.Silu).then_inc(silu_ready, 1)
                with act.Fori(0, count // NB) as i:
                    for k in range(NB):
                        silu(k, n0 + i * NB + k)
                if one_more:
                    silu(0, n0 + count)

            def l1_xattn():
                def mean_rsqrt(nt):
                    for m in range(DC):
                        act.activation(r1[:, m, 0:nt], bank[4 + m][:, 0:nt], ACT.Ln, bias=eps[:, 1:2]).then_inc(r1_ln, 1)

                act.wait_ge(q1_projected, 1)
                for m in range(DC):
                    e = act.activation(sq1[:, m, :], bank[2 + m][:], ACT.Square)
                e.then_inc(q1_squared, 1)
                act.wait_ge(q1_meaned, 1)
                mean_rsqrt(512)
                act.wait_ge(r1_ln, 2)
                act.activation(r1[:], r1[:], ACT.Exp, scale=-0.5).then_inc(q1_r, 1)
                with act.Fori(0, B) as b:
                    for j, (t0, nt) in enumerate(KCH):
                        n = b * len(KCH) + j
                        act.wait_ge(k1_projected, n + 1)
                        for m in range(DC):
                            e = act.activation(sq1[:, m, 0:nt * P], bank[m][:, 0:nt * P], ACT.Square)
                        e.then_inc(k1_squared, 1)
                        act.wait_ge(k1_meaned, n + 1)
                        act.wait_ge(k1_ready, n + 1)
                        mean_rsqrt(nt * P)
                        act.wait_ge(r1_ln, 2 * n + 4)
                        act.activation(r1[:, :, 0:nt * P], r1[:, :, 0:nt * P], ACT.Exp, scale=-0.5).then_inc(k1_r, 1)
                    for t in range(KT):
                        keys = min(P, S2 - t * P)
                        if t >= 2:
                            act.wait_ge(p1_used, b * KT + t - 1)
                        for m in range(DC):
                            act.wait_ge(s1_scored, b * 2 * KT + 2 * t + m + 1)
                            for h in range(2):
                                e = act.activation(p1[t % 2][0:keys, m * 1024 + h * 512:m * 1024 + (h + 1) * 512],
                                                   bank[4 + 2 * m + h][0:keys, :], ACT.Exp, scale=HD1 ** -0.5)
                            e.then_inc(p1_ready, 1)

            def l1_attn():
                for j in range(4 * TT + 1):
                    if j < 4 * TT:
                        t = j // 4
                        if j % 4 == 0:
                            act.wait_ge(qk_turned, t + 1)
                            act.activation(qbT[:, :, t * P:(t + 1) * P], bank[0][:, 0:D].rearrange("p (m q) -> p m q", m=DC), ACT.Copy)\
                               .then_inc(qbT_ready, 1)
                        act.wait_ge(b_maxed, j + 1)
                        for h in range(4):
                            e = act.activation(pa[:, j % 2, h, :], pa[:, j % 2, h, :], ACT.Exp, bias=maxa[:, j % 2, h:h + 1],
                                               scale=HDB ** -0.5, accum_out=suma[:, j % 2, h:h + 1])
                        e.then_inc(b_exped, 1)
                    if j >= 1:
                        act.wait_ge(b_turned, j)
                        act.activation(paT[:, (j - 1) % 2, :, :].rearrange("p t q -> p (t q)"), bank[1][:], ACT.Copy).then_inc(pbT_ready, 1)

            act.preload_act_table_set("natural_log_exp_and_others")
            act.wait_ge(eps_ready, 2)
            if 1 in stages:
                layernorm(1)
                l0_xattn()
            if 2 in stages:
                layernorm(2)
                l0_attn()
            if 3 in stages:
                layernorm(3)
                router(0)
                experts(0, G, I0, False)
            if 4 in stages:
                layernorm(4)
                l1_xattn()
            if 5 in stages:
                layernorm(5)
                l1_attn()
            if 6 in stages:
                layernorm(6)
                router(1)
                experts(N1, E1, I1, True)

        @block.gpsimd
        def _(pool):
            def l0_xattn():
                pool.wait_ge(consts_loaded, 16)
                pool.wait_ge(q0T_ready, 2)
                pool.wait_ge(plan_ready, 1)
                n_tiles = pool.value_load(plan[0:1, COUNT_AT:COUNT_AT + 1], min_val=1, max_val=NT)

                def queries(i):
                    b = pool.value_load(plan[0:1, bass.ds(i + NT + 1, 1)], min_val=0, max_val=B - 1)
                    for m in range(DC):
                        ins = pool.tensor_tensor(q0bd[:, m, :, :], const("head16").unsqueeze(2).broadcast_to([P, 8, S]),
                                                 q0T[:, m, bass.ds(b * S, S)].unsqueeze(1).broadcast_to([P, 8, S]), ALU.mult)
                    ins.then_inc(q0bd_ready, 1)
                queries(0)
                with pool.Fori(0, n_tiles) as i:
                    pool.wait_ge(scored, i + 1)
                    queries(i + 1)

            if 1 in stages:
                l0_xattn()

        @block.vector
        def _(v):
            chain = Chain(v, dve_chain)

            def layernorm(stage):
                s = LN_AT[stage]
                for i in range(TT):
                    ins = v.bn_stats(stats[:, i, :], x[:, i, :])
                chain(ins)
                for i in range(TT):
                    ins = v.bn_aggr(mv[:, i, :], stats[:, i, :])
                ins.then_inc(var_ready, 1)
                v.wait_ge(var_ready, s + 1)
                v.wait_ge(rstd_ready, s + 1)
                if stage == 1:
                    for i in range(TT):
                        chain(v.tensor_scalar(xn[:, i, :], x[:, i, :], mv[:, i, 0:1], rstd[:, i:i + 1],
                                              ALU.subtract, ALU.mult))
                    for i in range(TT):
                        ins = v.tensor_tensor_reduce(scratch[:, i, :], xn[:, i, :], xn[:, i, :], 1.0, 0.0,
                                                     ALU.mult, ALU.add, ms[:, i:i + 1])
                    ins.then_inc(sumsq_ready, 1)
                    v.wait_ge(rrms_ready, 1)
                    for i in range(TT):
                        v.tensor_scalar(xn[:, i, :], xn[:, i, :], rstd[:, i:i + 1], None, ALU.mult).then_inc(xn_ready, 1)
                    v.wait_ge(w0_loaded, 32)
                    v.wait_ge(xn_turned, 1)
                    v.tensor_scalar(xnT[:, 1, :], bank[1][:], normw[:, 1:2], None, ALU.mult).then_inc(xnT_dve, 1)
                else:
                    for i in range(TT):
                        v.tensor_scalar(xn[:, i, :], x[:, i, :], mv[:, i, 0:1], rstd[:, i:i + 1],
                                        ALU.subtract, ALU.mult).then_inc(xn_ready, 1)
                    v.wait_ge(xn_turned, s + 1)
                    v.tensor_copy(xnT[:, 1, :], bank[1][:]).then_inc(xnT_dve, 1)

            def l0_xattn():
                v.memset(ones_row[:], 1.0).then_inc(ones_ready, 1)
                v.wait_ge(mask_loaded, 16)
                v.tensor_reduce(tile_any[0:B * KT, :], mask_tiles[:], AX.X, ALU.max).then_inc(any_ready, 1)
                v.wait_ge(any_turned, 1)
                v.tensor_copy(tile_at[0:NT, :], bank[0][0:NT, 0:1]).then_inc(tile_at_ready, 1)
                v.wait_ge(tile_at_ready, 1)
                v.wait_ge(any_ready, 1)
                v.tensor_scalar(tile_hot[0:NT, :], const("count")[0:NT, :], tile_at[0:NT, 0:1], tile_any[0:NT, 0:1],
                                ALU.is_equal, ALU.mult).then_inc(tile_hot_ready, 1)
                v.wait_ge(plan_turned, 1)
                v.tensor_copy(plan[:, 0:COUNT_AT], bank[1][0:1, 0:COUNT_AT])
                v.tensor_scalar(plan[:, COUNT_AT:], bank[1][0:1, COUNT_AT:COUNT_AT + 1], 1.0, None, ALU.max).then_inc(plan_ready, 1)
                v.wait_ge(gate_exp, 1)
                chain(v.tensor_scalar(gate[:], gate[:], 1.0, None, ALU.add))
                chain(v.reciprocal(gate[:], gate[:]))
                v.memset(m_run[:], NEG)
                v.memset(v0[:, :, 2 * HD0:], 1.0)
                chain(v.memset(o_run[:], 0.0))
                v.wait_ge(plan_ready, 1)
                n_tiles = v.value_load(plan[0:1, COUNT_AT:COUNT_AT + 1], min_val=1, max_val=NT)
                steps = Chain(v, tile_chain)

                def batch_of(i):
                    return v.value_load(plan[0:1, bass.ds(i + NT + 1, 1)], min_val=0, max_val=B - 1)

                def mask_bias(i):
                    v.wait_ge(mask_tile_loaded, 16 * (i + 1))
                    v.tensor_scalar(tile_bias[:], mask_tile[:].unsqueeze(1).broadcast_to([1, 4, P]),
                                    1.0, -NEG, ALU.subtract, ALU.mult).then_inc(bias_ready, 1)

                def copy_v(i):
                    v.wait_ge(kv_projected, i + 1)
                    v.tensor_copy(v0[:, :, 0:2 * HD0], bank[1][:, 0:D].rearrange("p (g j) -> p g j", g=G0)).then_inc(v0_ready, 1)

                def shift(i, b):
                    m_old = m_run[:, bass.ds(b, 1), :].rearrange("p o g -> p (o g)")
                    v.wait_ge(scored, i + 1)
                    for m in range(DC):
                        ins = v.tensor_reduce(m_tile[:, 4 * m:4 * m + 4], bank[2 + m][:].rearrange("p (g k) -> p g k", g=4),
                                              AX.X, ALU.max)
                    steps(ins)
                    steps(v.tensor_tensor(m_new[:], m_old, m_tile[:], ALU.max))
                    steps(v.tensor_tensor(m_step[:], m_old, m_new[:], ALU.subtract))
                    v.tensor_tensor(m_old, m_old, m_tile[:], ALU.max)
                    for m in range(DC):
                        ins = v.tensor_tensor(probs0[:, 4 * m:4 * m + 4, :], bank[2 + m][:].rearrange("p (g k) -> p g k", g=4),
                                              m_new[:, 4 * m:4 * m + 4].unsqueeze(2).broadcast_to([P, 4, P]), ALU.subtract)
                    ins.then_inc(shifted, 1)
                    v.wait_ge(shifted, i + 1)

                mask_bias(0)
                copy_v(0)
                shift(0, batch_of(0))
                with v.Fori(0, n_tiles) as i:
                    PER_TILE = 5
                    began = steps.enter(i, PER_TILE)
                    b = batch_of(i)
                    o = o_run[:, bass.ds(b, 1), :, :].rearrange("p o g j -> p (o g) j")
                    mask_bias(i + 1)
                    v.wait_ge(alpha_ready, i + 1)
                    steps(v.tensor_tensor(o, o, alpha[:].unsqueeze(2).broadcast_to([P, G0, 2 * HD0 + 1]), ALU.mult))
                    v.wait_ge(turned, i + 1)
                    v.tensor_copy(probs0T[:, 4:8, :].rearrange("p g k -> p (g k)"), bank[5][:]).then_inc(pT_dve, 1)
                    shift(i + 1, batch_of(i + 1))
                    v.wait_ge(attended, i + 1)
                    steps(v.tensor_tensor(o, o, bank[6][:, 0:G0 * (2 * HD0 + 1)].rearrange("p (g j) -> p g j", g=G0), ALU.add))
                    copy_v(i + 1)
                    steps.leave(began, 1)
                chain(v.tensor_scalar(l_inv[:], o_run[:, :, :, 2 * HD0], 1e-30, None, ALU.max))
                chain(v.reciprocal(l_inv[:], l_inv[:]))
                chain(v.tensor_scalar(m_run[:], m_run[:], 0.1 * NEG, None, ALU.is_gt))
                chain(v.tensor_tensor(l_inv[:], l_inv[:], m_run[:], ALU.mult))
                flat_o = o_norm.rearrange("p b g j -> p (b g) j")
                chain(v.tensor_tensor(flat_o, o_run[:].rearrange("p b g j -> p (b g) j")[:, :, 0:2 * HD0],
                                      l_inv[:].rearrange("p b g -> p (b g)").unsqueeze(2).broadcast_to([P, B * G0, 2 * HD0]), ALU.mult))
                v.tensor_tensor(flat_o, flat_o, const("own16").unsqueeze(1).broadcast_to([P, B * G0, 2 * HD0]), ALU.mult)\
                 .then_inc(o_norm_ready, 1)
                v.wait_ge(o_folded, 1)
                v.tensor_copy(o0T[:, 1, :], bank[1][:]).then_inc(o0T_ready, 1)
                v.wait_ge(out0_projected, 1)
                for i in range(TT):
                    ins = v.tensor_tensor(scratch[:, i, :], bank[4 + i][:, 0:D], gate[:, i, :], ALU.mult)
                chain(ins)
                chain(v.tensor_tensor(x[:], x[:], scratch[:], ALU.add))

            def l0_attn():
                PER_PAIR = 4
                with v.Fori(0, HA // 4) as i:
                    began = chain.enter(i, 2 * PER_PAIR)
                    for k in range(2):
                        n = i * 2 + k
                        v.wait_ge(va_projected, n + 1)
                        for j in range(2):
                            ins = v.tensor_copy(va[:, 2 * j:2 * j + 2, :].rearrange("p t f -> p (t f)"), bank[2 + 3 * j][:])
                        ins.then_inc(va_ready, 1)
                        for u in range(2):
                            v.wait_ge(a_scored, 2 * n + u + 1)
                            chain(v.tensor_tensor(pa[:, u, :, :], bank[6 + u][:].rearrange("p (t k) -> p t k", t=TT),
                                                  const("causal").unsqueeze(1).broadcast_to([P, TT, P]), ALU.add))
                            chain(v.tensor_reduce(maxa[:, u, :], pa[:, u, :, :], AX.X, ALU.max))
                            v.tensor_scalar(maxa[:, u, :], maxa[:, u, :], -HDA ** -0.5, None, ALU.mult).then_inc(a_maxed, 1)
                        for u in range(2):
                            v.wait_ge(a_exped, 2 * n + u + 1)
                            v.reciprocal(suma[:, u, :], suma[:, u, :]).then_inc(a_summed, 1)
                            v.wait_ge(a_summed, 2 * n + u + 1)
                            v.tensor_tensor(pa[:, u, :, :], pa[:, u, :, :],
                                            suma[:, u, :].unsqueeze(2).broadcast_to([P, TT, P]), ALU.mult).then_inc(a_normed, 1)
                        for u in range(2):
                            v.wait_ge(a_mixed, 2 * n + u + 1)
                            v.tensor_copy(zaT[:, u, :], bank[1 + 3 * u][:]).then_inc(zaT_ready, 1)
                        v.wait_ge(a_out, n + 1)
                        for j in range(2):
                            ins = v.tensor_tensor(x[:, 2 * j:2 * j + 2, :], x[:, 2 * j:2 * j + 2, :],
                                                  bank[2 + 3 * j][:].rearrange("p (t f) -> p t f", t=2), ALU.add)
                        ins.then_inc(a_added, 1)
                        v.wait_ge(a_added, n + 2)
                    chain.leave(began, HA // 4)

            def l1_xattn():
                chain(v.memset(v1[:, :, :, 2 * HD1:], 1.0))
                v.wait_ge(q1_squared, 1)
                for m in range(DC):
                    ins = v.tensor_copy(q1T[:, m, :], bank[2 + m][:])
                ins.then_inc(q1_copied, 1)
                v.wait_ge(q1_copied, 1)
                v.wait_ge(q1_r, 1)
                chain(v.tensor_tensor(q1T[:], q1T[:], r1[:], ALU.mult))
                PER_BATCH = 4
                with v.Fori(0, B) as b:
                    began = chain.enter(b, PER_BATCH)
                    for m in range(DC):
                        ins = v.tensor_tensor(q1bd[:, m, :, :], const("head8").unsqueeze(2).broadcast_to([P, 16, S]),
                                              q1T[:, m, bass.ds(b * S, S)].unsqueeze(1).broadcast_to([P, 16, S]), ALU.mult)
                    ins.then_inc(q1bd_ready, 1)
                    for j, (t0, nt) in enumerate(KCH):
                        n = b * len(KCH) + j
                        v.wait_ge(k1_squared, n + 1)
                        k = k1T[:, :, t0 * P:(t0 + nt) * P]
                        for m in range(DC):
                            ins = v.tensor_copy(k[:, m, :], bank[m][:, 0:nt * P])
                        ins.then_inc(k1_copied, 1)
                        for t in range(t0, t0 + nt):
                            v.wait_ge(v1_projected, b * KT + t + 1)
                            v.tensor_copy(v1[:, t, :, 0:2 * HD1], bank[3][:, 0:D].rearrange("p (g j) -> p g j", g=G1)).then_inc(v1_copied, 1)
                        v.wait_ge(k1_copied, n + 1)
                        v.wait_ge(k1_r, n + 1)
                        v.tensor_tensor(k, k, r1[:, :, 0:nt * P], ALU.mult).then_inc(k1_ready, 1)
                    v.wait_ge(v1_copied, b * KT + KT)
                    v.sem_inc(v1_ready, 1)
                    v.wait_ge(p1_used, b * KT + KT)
                    v.tensor_copy(acc1, bank[3][:]).then_inc(acc1_copied, 1)
                    v.wait_ge(acc1_turned, b + 1)
                    o = bank[0][:].rearrange("p (g r) -> p g r", g=G1)
                    chain(v.reciprocal(rden1[:], o[:, :, 2 * HD1]))
                    chain(v.tensor_tensor(on1[:], o[:, :, 0:2 * HD1], rden1[:].unsqueeze(2).broadcast_to([P, G1, 2 * HD1]), ALU.mult))
                    chain(v.tensor_tensor(on1[:], on1[:], const("own8").unsqueeze(1).broadcast_to([P, G1, 2 * HD1]), ALU.mult))
                    v.sem_inc(on1_ready, 1)
                    v.wait_ge(o1_folded, b + 1)
                    chain(v.tensor_copy(o1T[:, :, bass.ds(b * S, S)], bank[1][:, 0:DC * S].rearrange("p (c q) -> p c q", c=DC)))
                    v.sem_inc(o1T_ready, 1)
                    chain.leave(began, B)
                v.wait_ge(o1_turned, 1)
                for i in range(TT):
                    ins = v.tensor_tensor(x[:, i, :], x[:, i, :], bank[i][:, 0:D], ALU.add)
                chain(ins)

            def l1_attn():
                for t in range(TT):
                    v.wait_ge(qkv_projected, t + 1)
                    z = bank[2 + t][:, 0:NR * HDB].rearrange("p (h d) -> p h d", h=NR)
                    hd = HDB // 2
                    cos, sin = const("cos"), const("sin")
                    v.tensor_tensor(rot[:, t, :, :], z, cos.unsqueeze(1).broadcast_to([P, NR, HDB]), ALU.mult)
                    v.tensor_tensor(rot2[:, t, :, 0:hd], z[:, :, hd:], sin[:, 0:hd].unsqueeze(1).broadcast_to([P, NR, hd]), ALU.mult)
                    v.tensor_tensor(rot2[:, t, :, hd:], z[:, :, 0:hd], sin[:, hd:].unsqueeze(1).broadcast_to([P, NR, hd]), ALU.mult)
                    chain(v.tensor_copy(vb[:, t, :], bank[2 + t][:, NR * HDB:QKV]))
                    chain(v.tensor_tensor(rot[:, t, :, :], rot[:, t, :, :], rot2[:, t, :, :], ALU.add))
                    v.tensor_copy(krep[:, t, :, :], rot[:, t, HB:NR, :].broadcast_to([P, 8, HDB])).then_inc(rotated, 1)
                for j in range(4 * TT + 1):
                    t = j // 4
                    if j < 4 * TT:
                        if j % 4 == 0:
                            v.wait_ge(qk_turned, t + 1)
                            v.wait_ge(qbT_ready, t + 1)
                            v.tensor_tensor(kbd[t % 2][:], const("head16").unsqueeze(2).broadcast_to([P, 8, P]),
                                            bank[0][:, 2 * P:3 * P].unsqueeze(1).broadcast_to([P, 8, P]), ALU.mult).then_inc(kbd_ready, 1)
                        v.wait_ge(b_scored, j + 1)
                        if j >= 2:
                            v.wait_ge(b_turned, j - 1)
                        chain(v.tensor_tensor(pa[:, j % 2, :, :], bank[6 + j % 2][:].rearrange("p (h k) -> p h k", h=4),
                                              const("block").unsqueeze(1).broadcast_to([P, 4, P]), ALU.add))
                        chain(v.tensor_reduce(maxa[:, j % 2, :], pa[:, j % 2, :, :], AX.X, ALU.max))
                        v.tensor_scalar(maxa[:, j % 2, :], maxa[:, j % 2, :], -HDB ** -0.5, None, ALU.mult).then_inc(b_maxed, 1)
                        v.wait_ge(b_exped, j + 1)
                        v.reciprocal(suma[:, j % 2, :], suma[:, j % 2, :]).then_inc(b_summed, 1)
                        v.wait_ge(b_summed, j + 1)
                        v.tensor_tensor(pa[:, j % 2, :, :], pa[:, j % 2, :, :],
                                        suma[:, j % 2, :].unsqueeze(2).broadcast_to([P, 4, P]), ALU.mult).then_inc(b_normed, 1)
                    if j >= 4 and j % 4 == 0:
                        t = j // 4 - 1
                        v.wait_ge(b_mixed, j)
                        v.tensor_copy(ob[:, t, :], bank[2][:, 0:D]).then_inc(ob_ready, 1)
                        v.wait_ge(ob_turned, t + 1)
                        v.tensor_copy(obT[:, :, t * P:(t + 1) * P], bank[3][:, 0:D].rearrange("p (c q) -> p c q", c=DC)).then_inc(obT_ready, 1)
                        v.wait_ge(b_out, t + 1)
                        v.tensor_tensor(x[:, t, :], x[:, t, :], bank[4][:, 0:D], ALU.add).then_inc(b_added, 1)
                v.wait_ge(b_added, TT)

            def softmax_rows(r, ne):
                v.wait_ge(r_scored, r * R1 + 1)
                p = pr[:, :, 0:ne]
                logits = bank[7][:, 0:TT * ne].rearrange("p (t e) -> p t e", t=TT)
                if r == 1:
                    chain(v.tensor_tensor(p, logits, bias1[:].unsqueeze(1).broadcast_to([P, TT, E1]), ALU.add))
                    logits = p
                chain(v.tensor_reduce(rmax[:], logits, AX.X, ALU.max))
                v.tensor_tensor(p, logits, rmax[:].unsqueeze(2).broadcast_to([P, TT, ne]), ALU.subtract).then_inc(r_shifted, 1)
                v.wait_ge(r_exped, r * R1 + 1)
                chain(v.tensor_reduce(rmax[:], p, AX.X, ALU.add))
                chain(v.reciprocal(rmax[:], rmax[:]))
                chain(v.tensor_tensor(p, p, rmax[:].unsqueeze(2).broadcast_to([P, TT, ne]), ALU.mult))
                for t in range(TT):
                    ins = v.max(mx8[:, t, :], pr[:, t, 0:ne])
                chain(ins)

            def router0():
                chain(v.tensor_copy(merge_f[:], merge_i[:]))
                chain(v.tensor_scalar(onehot[:], const("group")[0:E0, :], merge_f[:, 0:1], None, ALU.is_equal))
                softmax_rows(0, E0)
                for t in range(TT):
                    ins = v.match_replace(rep[:, t, :], mx8[:, t, :], pr[:, t, :], 0.0)
                chain(ins)
                chain(v.tensor_tensor(pr[:], pr[:], rep[:], ALU.subtract))
                chain(v.tensor_reduce(rmax[:], mx8[:], AX.X, ALU.add))
                chain(v.reciprocal(rmax[:], rmax[:]))
                v.tensor_tensor(pr[:], pr[:], rmax[:].unsqueeze(2).broadcast_to([P, TT, E0]), ALU.mult).then_inc(sel_ready, 1)
                v.wait_ge(sel_turned, 1)
                v.tensor_copy(selT[:], bank[6][0:E0, :]).then_inc(selT_ready, 1)
                v.wait_ge(w_summed, 1)
                v.tensor_copy(we[:, :, 0:G], bank[5][:, 0:TT * G].rearrange("p (t g) -> p t g", t=TT)).then_inc(we_ready, 1)
                v.wait_ge(we_ready, 1)

            def router1():
                chain(v.memset(pr[:, :, E1:E1 + 8], -1.0))
                chain(v.memset(pick[:], -1.0))
                softmax_rows(1, E1)
                chain(v.tensor_copy(pick[:, :, 0:2], mx8[:, :, 0:2]))
                for t in range(TT):
                    ins = v.match_replace(rep[:, t, 0:E1 + 8], pick[:, t, :], pr[:, t, 0:E1 + 8], 0.0)
                chain(ins)
                chain(v.tensor_tensor(we[:, :, 0:E1], pr[:, :, 0:E1], rep[:, :, 0:E1], ALU.subtract))
                chain(v.tensor_reduce(rmax[:], mx8[:, :, 0:2], AX.X, ALU.add))
                chain(v.tensor_scalar(rmax[:], rmax[:], 1e-9, None, ALU.add))
                chain(v.reciprocal(rmax[:], rmax[:]))
                chain(v.tensor_tensor(we[:, :, 0:E1], we[:, :, 0:E1], rmax[:].unsqueeze(2).broadcast_to([P, TT, E1]), ALU.mult))
                v.memset(we[:, :, E1:NX], 1.0).then_inc(we_ready, 1)
                v.wait_ge(we_ready, R1 + 1)

            def experts(n0, count, width, one_more):
                def hidden(k, n):
                    v.wait_ge(silu_ready, n + 1)
                    v.tensor_tensor(hid[k][0:width, :], hid[k][0:width, :], bank[2 * (k % 2) + 1][0:width, :], ALU.mult)\
                     .then_inc(hid_ready, 1)

                def add(k, n, e):
                    v.wait_ge(e_down, n + 1)
                    for t in range(TT):
                        ins = v.scalar_tensor_tensor(x[:, t, :], bank[4 + 2 * (k % 2) + t // 2][:, (t % 2) * D:(t % 2 + 1) * D],
                                                     we[:, t, bass.ds(e, 1)], x[:, t, :], ALU.mult, ALU.add)
                    ins.then_inc(e_added, 1)
                    v.wait_ge(e_added, n + 2)
                with v.Fori(0, count // NB) as i:
                    for k in range(0, NB, 2):
                        n = n0 + i * NB + k
                        hidden(k, n)
                        hidden(k + 1, n + 1)
                        add(k, n, i * NB + k)
                        add(k + 1, n + 1, i * NB + k + 1)
                if one_more:
                    hidden(0, n0 + count)
                    add(0, n0 + count, count)

            for free in (v1_ready, a_added, e_added, o1T_ready, k1_ready):
                v.sem_inc(free, 1)
            v.memset(eps[:, 0:1], LN_EPS).then_inc(eps_ready, 1)
            v.memset(eps[:, 1:2], RMS_EPS).then_inc(eps_ready, 1)
            v.wait_ge(x_loaded, 16)
            v.wait_ge(consts_loaded, 16)
            if 1 in stages:
                layernorm(1)
                l0_xattn()
            if 2 in stages:
                layernorm(2)
                l0_attn()
            if 3 in stages:
                layernorm(3)
                v.wait_ge(router_loaded, 80)
                router0()
                experts(0, G, I0, False)
            if 4 in stages:
                layernorm(4)
                l1_xattn()
            if 5 in stages:
                layernorm(5)
                l1_attn()
            if 6 in stages:
                layernorm(6)
                v.wait_ge(router_loaded, 80)
                router1()
                experts(N1, E1, I1, True)
            v.sem_inc(dve_done, 1)



def layout(inputs):
    f = {k: np.asarray(v) for k, v in inputs.items()}

    def wide(w):
        return w.reshape(DC, P, -1).transpose(1, 0, 2)

    ctxT = np.zeros((B, D, S2P), np.float32)
    ctxT[:, :, :S2] = f["ctx_2048"].transpose(0, 2, 1)
    mask = np.zeros((B, S2P), bool)
    mask[:, :S2] = f["mask_BxS2_bk0"]
    kv1 = np.concatenate([f["L1_xattn_Wk"], f["L1_xattn_Wv"]], 0)
    r = {
        "x": f["x"],
        "const": CONST,
        "w0": np.stack([wide(f[f"L0_xattn_{n}"].T) for n in ("wq", "wg", "wk", "wv", "wo")], 1),
        "norm_w": f["L0_xattn_norm_w"].reshape(DC, P).T,
        "wa": np.concatenate([
            np.stack([f["L0_attn_W_K"], f["L0_attn_W_Q"]], 1).reshape(HA // 2, 2, 2, HDA, DC, P)
              .transpose(0, 5, 1, 2, 4, 3).reshape(HA // 2, P, -1),
            f["L0_attn_W_V"].reshape(HA // 2, 2 * HDA, DC, P).transpose(0, 3, 2, 1).reshape(HA // 2, P, -1),
            f["L0_attn_W_O"].reshape(D, HA // 2, 2, HDA).transpose(1, 3, 2, 0).reshape(HA // 2, P, -1)], 2),
        "w1": np.stack([wide(w.T) for w in (f["L1_xattn_Wq"], kv1[0::2], kv1[1::2])], 1),
        "wqkv": wide(f["L1_attn_w_attn"]),
        "wout": wide(f["L1_attn_w_out"]),
        "gu0": f["L0_ffn_gate_up_proj"].reshape(E0, 2, I0, DC, P).transpose(0, 4, 3, 1, 2),
        "dn0": f["L0_ffn_down_proj"].transpose(0, 2, 1),
        "wr0": wide(f["L0_ffn_gate_weight"].T),
        "merge": f["L0_ffn_merge_groups"].reshape(E0, 1),
        "dom": f["L0_ffn_dominant_experts"].reshape(1, G),
        "gu1": np.stack([np.concatenate([f["L1_ffn_W" + n], f["L1_ffn_sW" + n][None]], 0) for n in "gu"], 1)
                 .reshape(NX, 2, DC, P, I1).transpose(0, 3, 2, 1, 4),
        "dn1": np.concatenate([f["L1_ffn_Wd"], f["L1_ffn_sWd"][None]], 0),
        "wr1": wide(f["L1_ffn_Wr"].T),
        "bias1": f["L1_ffn_bias"].reshape(1, E1),
        "mask": mask.reshape(B * KT, P),
        "ctxT": ctxT.reshape(B, DC, P, KT, P).transpose(0, 3, 2, 1, 4).reshape(B * KT, P, DC, P),
    }
    return {k: np.ascontiguousarray(v) for k, v in r.items()}


def kernel(**inputs):
    import concourse.bacc as _bacc
    from concourse.bass_utils import run_bass_kernel_spmd as _run

    nc = _bacc.Bacc("TRN2", target_bir_lowering=False, num_devices=1)
    arrays = layout(inputs)
    aps = {k: nc.dram_tensor(f"in_{k}", v.shape, mybir.dt.from_np(v.dtype), kind="ExternalInput").ap()
           for k, v in arrays.items()}
    out = nc.dram_tensor("out_x", (B, S, D), F32, kind="ExternalOutput").ap()
    build(nc, aps, out)
    r = _run(nc, [{f"in_{k}": v for k, v in arrays.items()}], core_ids=[0])
    return r.results[0]["out_x"]
```

```python
from contextlib import ExitStack

import concourse.bass as bass
import numpy as np
from concourse import mybir

ALU = mybir.AluOpType
ACT = mybir.ActivationFunctionType
AX = mybir.AxisListType
F32 = mybir.dt.float32
U8 = mybir.dt.uint8
BF16 = mybir.dt.bfloat16
F16 = mybir.dt.float16
I32 = mybir.dt.int32

P = 128
B, S, D = 8, 64, 256
T = B * S
TT = T // P
DC = D // P
S2 = 1601
KT = -(-S2 // P)
S2P = KT * P
NT = B * KT
H0, HD0 = 16, 16
G0 = H0 // 2
HA, HDA = 16, 128
E0, G, I0 = 32, 8, 96
H1, HD1 = 32, 8
G1 = H1 // 2
HB, HDB = 16, 16
QKV = (HB + 2) * HDB
E1, I1 = 16, 128
NX = E1 + 1
NCH = 4
CHUNK = [KT * j // NCH + (KT * j % NCH > 0) for j in range(NCH + 1)]
NEG = -1e30
LN_EPS, RMS_EPS = 1e-5, 1e-6



def constants():
    p = np.arange(P)[:, None]
    f = np.arange(P)[None, :]
    same = p // S == f // S
    pos = (np.arange(P) % S).astype(np.float32)
    freq = (np.float32(10000.0) ** ((-2.0 * np.arange(0, HDB, 2, dtype=np.float32) - 1.0) / HDB)).astype(np.float32)
    ang = pos[:, None] * freq[None, :]
    ang = np.concatenate([ang, ang], 1).astype(np.float32)
    sin = np.sin(ang)
    sin[:, :HDB // 2] *= -1
    parts = {
        "ident": (p == f),
        "head16": (p // HD0 == np.arange(P // HD0)[None, :]),
        "head8s": (p % S // HD1 == np.arange(S // HD1)[None, :]),
        "mean8": (p // HD1 == f // HD1) / HD1,
        "fold": (p % S == np.arange(S)[None, :]),
        "place": np.stack([(p % S + S * k == f) for k in range(2)], 1),
        "own16": (np.arange(2 * HD0)[None, :] // HD0 == p // S),
        "own8": (np.arange(2 * HD1)[None, :] // HD1 == p // S),
        "causal": np.where(same & (f <= p), 0.0, -1e10),
        "block": np.where(same, 0.0, NEG),
        "cos": np.cos(ang),
        "sin": sin,
        "before": (p < f),
        "count": np.arange(NT + 1)[None, :] * np.ones((P, 1)),
        "tile": np.concatenate([p, p // KT], 1),
        "group": np.ones((P, 1)) * np.arange(G)[None, :],
    }
    at, cols, n = {}, [], 0
    for k, v in parts.items():
        v = np.asarray(v, np.float32).reshape(P, -1)
        at[k] = (n, n + v.shape[1])
        n += v.shape[1]
        cols.append(v)
    return np.ascontiguousarray(np.concatenate(cols, 1)), at


CONST, CONST_AT = constants()


class Chain:

    def __init__(self, eng, sem):
        self.eng, self.sem, self.n, self.loops = eng, sem, 0, []

    def value(self):
        v = self.n
        for var, per in self.loops:
            v = v + var * per
        return v

    def __call__(self, ins):
        ins.then_inc(self.sem, 1)
        self.n += 1
        self.eng.wait_ge(self.sem, self.value())

    def enter(self, var, per):
        self.loops.append((var, per))
        return self.n

    def leave(self, began, count):
        _, per = self.loops.pop()
        assert self.n - began == per, (self.n - began, per)
        self.n = began + per * count


def build(nc, a, out, stages=(1, 2, 3, 4, 5, 6)):
    with ExitStack() as ctx:
        def sb(name, shape, dt=F32):
            return ctx.enter_context(nc.sbuf_tensor(name, shape, dt))

        def sem(name):
            return ctx.enter_context(nc.semaphore(name))

        pair = [ctx.enter_context(nc.psum_tensor(f"banks{2 * i}", [P, 1024], F32)) for i in range(4)]
        bank = [pair[i // 2][:, i % 2 * 512:(i % 2 + 1) * 512] for i in range(8)]

        cst = sb("cst", [P, CONST.shape[1]])

        def const(name):
            lo, hi = CONST_AT[name]
            return cst[:, lo:hi]

        ident = const("ident")
        x = sb("x_sb", [P, TT, D])
        xn = sb("xn", [P, TT, D])
        xnT = sb("xnT", [P, DC, T])
        stats = sb("stats", [P, TT, 6])
        mv = sb("mv", [P, TT, 2])
        lnv = sb("lnv", [P, TT])
        rstd = sb("rstd", [P, TT])
        ms = sb("ms", [P, TT])
        eps = sb("eps", [P, 2])
        w0 = sb("w0", [P, 5, DC, D])
        w1 = sb("w1", [P, 3, DC, D])
        normw = sb("normw", [P, DC])

        consts_loaded = sem("consts_loaded")
        x_loaded = sem("x_loaded")
        w0_loaded = sem("w0_loaded")
        eps_ready = sem("eps_ready")
        var_ready = sem("var_ready")
        rstd_ready = sem("rstd_ready")
        sumsq_ready = sem("sumsq_ready")
        rrms_ready = sem("rrms_ready")
        xn_ready = sem("xn_ready")
        xn_turned = sem("xn_turned")
        xnT_act = sem("xnT_act")
        xnT_dve = sem("xnT_dve")
        act_chain = sem("act_chain")
        dve_chain = sem("dve_chain")

        scratch = sb("scratch", [P, TT, D])
        gate = sb("gate", [P, TT, D])
        q0T = sb("q0T", [P, DC, T])
        q0bd = sb("q0bd", [P, DC, 8, S])
        ctx_tile = sb("ctx_tile", [P, DC, P])
        mask_tiles = sb("mask_tiles", [B * KT, P], U8)
        mask_tile = sb("mask_tile", [1, P], U8)
        tile_any = sb("tile_any", [P, 1])
        tile_at = sb("tile_at", [P, 1])
        tile_hot = sb("tile_hot", [P, NT + 1])
        plan = sb("plan", [1, 2 * (NT + 1) + 1], I32)
        tile_bias = sb("tile_bias", [1, 4, P], BF16)
        ones_row = sb("ones_row", [1, P], BF16)
        k0T = sb("k0T", [P, DC, P])
        v0 = sb("v0", [P, G0, 2 * HD0 + 1])
        probs0 = sb("probs0", [P, G0, P])
        probs0T = sb("probs0T", [P, G0, P])
        m_run = sb("m_run", [P, B, G0])
        m_new = sb("m_new", [P, G0])
        m_tile = sb("m_tile", [P, G0])
        m_step = sb("m_step", [P, G0])
        alpha = sb("alpha", [P, G0])
        o_run = sb("o_run", [P, B, G0, 2 * HD0 + 1])
        l_inv = sb("l_inv", [P, B, G0])
        o0T = sb("o0T", [P, DC, T])

        q0_projected = sem("q0_projected")
        gate_projected = sem("gate_projected")
        gate_exp = sem("gate_exp")
        q0T_ready = sem("q0T_ready")
        ones_ready = sem("ones_ready")
        mask_loaded = sem("mask_loaded")
        any_ready = sem("any_ready")
        any_turned = sem("any_turned")
        tile_at_ready = sem("tile_at_ready")
        tile_hot_ready = sem("tile_hot_ready")
        plan_turned = sem("plan_turned")
        plan_ready = sem("plan_ready")
        tile_chain = sem("tile_chain")
        ctx_loaded = sem("ctx_loaded")
        bias_ready = sem("bias_ready")
        mask_tile_loaded = sem("mask_tile_loaded")
        kv_projected = sem("kv_projected")
        k0_ready = sem("k0_ready")
        v0_ready = sem("v0_ready")
        q0bd_ready = sem("q0bd_ready")
        scored = sem("scored")
        shifted = sem("shifted")
        exped = sem("exped")
        alpha_ready = sem("alpha_ready")
        turned = sem("turned")
        pT_act = sem("pT_act")
        pT_dve = sem("pT_dve")
        attended = sem("attended")
        o_norm_ready = sem("o_norm_ready")
        o_folded = sem("o_folded")
        o0T_ready = sem("o0T_ready")
        out0_projected = sem("out0_projected")

        wa = [sb(f"wa{k}", [P, 8 * D]) for k in range(2)]
        kaT = sb("kaT", [P, 2, T])
        qaT = sb("qaT", [P, 2, T])
        va = sb("va", [P, TT, 2 * HDA])
        pa = sb("pa", [P, 2, TT, P])
        paT = sb("paT", [P, 2, TT, P])
        zaT = sb("zaT", [P, 2, T])
        maxa = sb("maxa", [P, 2, TT])
        suma = sb("suma", [P, 2, TT])
        wa_loaded = [sem(f"wa_loaded{k}") for k in range(2)]
        kqa_projected = sem("kqa_projected")
        va_projected = sem("va_projected")
        kqa_ready = sem("kqa_ready")
        va_ready = sem("va_ready")
        a_scored = sem("a_scored")
        a_maxed = sem("a_maxed")
        a_exped = sem("a_exped")
        a_normed = sem("a_normed")
        a_summed = sem("a_summed")
        a_turned = sem("a_turned")
        paT_ready = sem("paT_ready")
        a_mixed = sem("a_mixed")
        zaT_ready = sem("zaT_ready")
        a_out = sem("a_out")
        a_added = sem("a_added")

        ctxc = [sb(f"ctxc{k}", [P, 4, DC, P]) for k in range(2)]
        v1 = sb("v1", [P, 2, 4, G1, 4 * HD1])
        o_norm = v1[:].rearrange("p u t g j -> p (u t g j)")[:, 0:B * D].rearrange("p (b g j) -> p b g j", b=B, g=G0)
        q1T = sb("q1T", [P, DC, T])
        q1s = [sb(f"q1s{k}", [P, DC, 2, T], F16) for k in range(2)]
        q1bd = [sb(f"q1bd{k}", [P, DC, 2, 8, S], F16) for k in range(2)]
        k1s = [sb(f"k1s{k}", [P, DC, 2, 4 * P], F16) for k in range(2)]
        k1f = paT[:].rearrange("p u t k -> p u (t k)")
        sq1, r1 = kaT, qaT
        p1 = wa
        acc1 = zaT[:, 0, :]
        rden1 = sb("rden1", [P, G1])
        on1 = sb("on1", [P, G1, 2 * HD1])
        o1T = sb("o1T", [P, DC, T])
        w1_loaded = sem("w1_loaded")
        ctxc_loaded = [sem(f"ctxc_loaded{k}") for k in range(2)]
        q1_projected = sem("q1_projected")
        q1_squared = sem("q1_squared")
        q1_copied = sem("q1_copied")
        q1_meaned = sem("q1_meaned")
        q1_r = sem("q1_r")
        q1bd_ready = sem("q1bd_ready")
        q1_split = sem("q1_split")
        k1_projected = sem("k1_projected")
        k1_copied = sem("k1_copied")
        k1_squared = sem("k1_squared")
        k1_meaned = sem("k1_meaned")
        r1_ready = sem("r1_ready")
        k1_normed = sem("k1_normed")
        k1_high = sem("k1_high")
        k1_ready = sem("k1_ready")
        v1_projected = sem("v1_projected")
        s1_scored = sem("s1_scored")
        p1_ready = sem("p1_ready")
        p1_used = sem("p1_used")
        acc1_copied = sem("acc1_copied")
        acc1_turned = sem("acc1_turned")
        on1_ready = sem("on1_ready")
        o1_folded = sem("o1_folded")
        o1T_ready = sem("o1T_ready")
        o1_turned = sem("o1_turned")
        r1_ln = sem("r1_ln")
        v1_copied = sem("v1_copied")
        q1bd_low = sem("q1bd_low")

        wqkv = sb("wqkv", [P, DC, QKV])
        wout = sb("wout", [P, DC, D])
        NR = HB + 1
        flat = v1[:].rearrange("p u t g j -> p (u t g j)")
        rot, rot2 = (flat[:, k * TT * NR * HDB:(k + 1) * TT * NR * HDB].rearrange("p (t h d) -> p t h d", t=TT, h=NR)
                     for k in range(2))
        krep = sb("krep", [P, TT, 8, HDB])
        vb = sb("vb", [P, TT, HDB])
        qbT, kbd, ob, obT = q0T, [probs0, probs0T], scratch, o0T
        wb_loaded = sem("wb_loaded")
        qkv_projected = sem("qkv_projected")
        rotated = sem("rotated")
        qk_turned = sem("qk_turned")
        qbT_ready = sem("qbT_ready")
        kbd_ready = sem("kbd_ready")
        b_scored = sem("b_scored")
        b_maxed = sem("b_maxed")
        b_exped = sem("b_exped")
        b_normed = sem("b_normed")
        b_turned = sem("b_turned")
        pbT_ready = sem("pbT_ready")
        b_mixed = sem("b_mixed")
        ob_ready = sem("ob_ready")
        ob_turned = sem("ob_turned")
        obT_ready = sem("obT_ready")
        b_out = sem("b_out")
        b_added = sem("b_added")
        b_summed = sem("b_summed")

        NB = 4
        wgu = [sb(f"wgu{k}", [P, DC, 2, P]) for k in range(NB)]
        wdn = [sb(f"wdn{k}", [P, D]) for k in range(NB)]
        hid = [kaT[:, 0, :], kaT[:, 1, :], qaT[:, 0, :], qaT[:, 1, :]]
        wr0 = sb("wr0", [P, DC, E0])
        wr1 = sb("wr1", [P, DC, E1])
        bias1 = sb("bias1", [P, E1])
        merge_i = sb("merge_i", [E0, 1], I32)
        merge_f = sb("merge_f", [E0, 1])
        onehot = sb("onehot", [E0, G])
        dom = sb("dom", [1, G], I32)
        pr = sb("pr", [P, TT, E0])
        rep = sb("rep", [P, TT, E0])
        mx8 = sb("mx8", [P, TT, 8])
        pick = sb("pick", [P, TT, 8])
        rmax = sb("rmax", [P, TT])
        selT = sb("selT", [E0, T])
        we = sb("we", [P, TT, NX])
        router_loaded = sem("router_loaded")
        we_loaded = [sem(f"we_loaded{k}") for k in range(NB)]
        r_scored = sem("r_scored")
        r_shifted = sem("r_shifted")
        r_exped = sem("r_exped")
        sel_ready = sem("sel_ready")
        sel_turned = sem("sel_turned")
        selT_ready = sem("selT_ready")
        w_summed = sem("w_summed")
        e_projected = sem("e_projected")
        silu_ready = sem("silu_ready")
        hid_ready = sem("hid_ready")
        e_down = sem("e_down")
        e_added = sem("e_added")
        we_ready = sem("we_ready")
        stored = sem("stored")
        dve_done = sem("dve_done")

        COUNT_AT = 2 * (NT + 1)
        LN_AT = {st: k for k, st in enumerate(stages)}
        N1 = G if 3 in stages else 0
        R1 = 1 if 3 in stages else 0
        block = ctx.enter_context(nc.Block())
        xd = a["x"].rearrange("b s d -> (b s) d").rearrange("(t p) d -> p t d", p=P)
        od = out.rearrange("b s d -> (b s) d").rearrange("(t p) d -> p t d", p=P)

        @block.sync
        def _(sp):
            sp.dma_start(x[:], xd).then_inc(x_loaded, 16)
            sp.dma_start(cst[:], a["const"]).then_inc(consts_loaded, 16)
            sp.dma_start(w0[:], a["w0"]).then_inc(w0_loaded, 16)
            sp.dma_start(normw[:], a["norm_w"]).then_inc(w0_loaded, 16)
            sp.dma_start(mask_tiles[:], a["mask"]).then_inc(mask_loaded, 16)

            def l0_xattn():
                def load(i):
                    n = sp.value_load(plan[0:1, bass.ds(i, 1)], min_val=0, max_val=NT - 1)
                    sp.dma_start(ctx_tile[:], a["ctxT"][bass.ds(n, 1), :, :, :].rearrange("n p c k -> p (n c) k"))\
                      .then_inc(ctx_loaded, 16)
                    sp.dma_start(mask_tile[:], a["mask"][bass.ds(n, 1), :]).then_inc(mask_tile_loaded, 16)
                sp.wait_ge(plan_ready, 1)
                n_tiles = sp.value_load(plan[0:1, COUNT_AT:COUNT_AT + 1], min_val=1, max_val=NT)
                load(0)
                with sp.Fori(0, n_tiles) as i:
                    sp.wait_ge(bias_ready, i + 1)
                    sp.wait_ge(kv_projected, i + 1)
                    load(i + 1)

            def l0_attn():
                def load(n, k):
                    sp.dma_start(wa[k][:], a["wa"][bass.ds(n, 1), :, :].rearrange("n p f -> p (n f)")).then_inc(wa_loaded[k], 16)
                for k in range(2):
                    load(k, k)
                with sp.Fori(0, HA // 4 - 1) as i:
                    for k in range(2):
                        n = i * 2 + k
                        sp.wait_ge(a_out, n + 1)
                        load(n + 2, k)

            def load_expert(gu, dn, width, index, k):
                sp.dma_start(wgu[k][:, :, :, 0:width], gu[bass.ds(index, 1), :, :, :, :].rearrange("n p c u i -> p (n c) u i"))\
                  .then_inc(we_loaded[k], 16)
                sp.dma_start(wdn[k][0:width, :], dn[bass.ds(index, 1), :, :].rearrange("n p f -> p (n f)"))\
                  .then_inc(we_loaded[k], 16)

            def l0_ffn():
                def load(n, k):
                    e = sp.value_load(dom[0:1, bass.ds(n, 1)], min_val=0, max_val=E0 - 1)
                    load_expert(a["gu0"], a["dn0"], I0, e, k)
                for k in range(NB):
                    load(k, k)
                with sp.Fori(0, G // NB - 1) as i:
                    for k in range(NB):
                        n = i * NB + k
                        sp.wait_ge(e_down, n + 1)
                        load(n + NB, k)

            def l1_xattn():
                sp.dma_start(w1[:], a["w1"]).then_inc(w1_loaded, 16)
                def load(first, n, k):
                    sp.dma_start(ctxc[k][:, 0:n, :, :].rearrange("p t c k -> p t (c k)"),
                                 a["ctxT"][bass.ds(first, n), :, :, :].rearrange("t p c k -> p t (c k)")).then_inc(ctxc_loaded[k], 16)
                for j in range(2):
                    load(CHUNK[j], CHUNK[j + 1] - CHUNK[j], j)
                with sp.Fori(0, B) as b:
                    for j in range(NCH):
                        jj = (j + 2) % NCH
                        bb = b if j + 2 < NCH else (b + 1) % B
                        sp.wait_ge(v1_projected, b * KT + CHUNK[j + 1])
                        load(bb * KT + CHUNK[jj], CHUNK[jj + 1] - CHUNK[jj], j % 2)

            def l1_attn():
                sp.dma_start(wqkv[:], a["wqkv"]).then_inc(wb_loaded, 16)
                sp.dma_start(wout[:], a["wout"]).then_inc(wb_loaded, 16)

            def l1_ffn():
                for k in range(NB):
                    if N1:
                        sp.wait_ge(e_down, N1 - NB + k + 1)
                    load_expert(a["gu1"], a["dn1"], I1, k, k)
                with sp.Fori(0, E1 // NB - 1) as i:
                    for k in range(NB):
                        n = i * NB + k
                        sp.wait_ge(e_down, N1 + n + 1)
                        load_expert(a["gu1"], a["dn1"], I1, n + NB, k)
                sp.wait_ge(e_down, N1 + E1 - NB + 1)
                load_expert(a["gu1"], a["dn1"], I1, E1, 0)

            sp.dma_start(wr0[:], a["wr0"]).then_inc(router_loaded, 16)
            sp.dma_start(wr1[:], a["wr1"]).then_inc(router_loaded, 16)
            sp.dma_start(bias1[:], a["bias1"].broadcast_to([P, E1])).then_inc(router_loaded, 16)
            sp.dma_start(merge_i[:], a["merge"]).then_inc(router_loaded, 16)
            sp.dma_start(dom[:], a["dom"]).then_inc(router_loaded, 16)
            if 1 in stages:
                l0_xattn()
            if 2 in stages:
                l0_attn()
            if 3 in stages:
                sp.wait_ge(router_loaded, 80)
                l0_ffn()
            if 4 in stages:
                l1_xattn()
            if 5 in stages:
                l1_attn()
            if 6 in stages:
                l1_ffn()
            sp.wait_ge(dve_done, 1)
            sp.dma_start(od, x[:]).then_inc(stored, 16)
            sp.wait_ge(mask_loaded, 16)
            sp.wait_ge(router_loaded, 80)
            sp.wait_ge(w0_loaded, 32)
            sp.wait_ge(stored, 16)

        @block.tensor
        def _(pe):
            def layernorm(stage):
                s = LN_AT[stage]
                for i in range(TT):
                    pe.wait_ge(xn_ready, TT * s + i + 1)
                    for c in range(DC):
                        mm = pe.transpose(bank[c][:, i * P:(i + 1) * P], xn[:, i, c * P:(c + 1) * P], ident)
                mm.then_inc(xn_turned, 1)
                pe.wait_ge(xnT_act, s + 1)
                pe.wait_ge(xnT_dve, s + 1)

            def l0_xattn():
                pe.wait_ge(w0_loaded, 32)
                for m in range(DC):
                    for c in range(DC):
                        mm = pe.matmul(bank[2 + m], w0[:, 0, c, m * P:(m + 1) * P], xnT[:, c, :],
                                       start=(c == 0), stop=(c == DC - 1))
                mm.then_inc(q0_projected, 1)
                for i in range(TT):
                    for c in range(DC):
                        mm = pe.matmul(bank[4 + i][:, 0:D], xnT[:, c, i * P:(i + 1) * P], w0[:, 1, c, :],
                                       start=(c == 0), stop=(c == DC - 1))
                mm.then_inc(gate_projected, 1)
                pe.wait_ge(any_ready, 1)
                pe.matmul(bank[0][0:NT, 0:1], const("before")[0:NT, 0:NT], tile_any[0:NT, :], start=True, stop=True)\
                  .then_inc(any_turned, 1)
                pe.wait_ge(tile_hot_ready, 1)
                for k in range(2):
                    pe.matmul(bank[1][0:1, k * (NT + 1):(k + 1) * (NT + 1)], const("tile")[0:NT, k:k + 1], tile_hot[0:NT, :],
                              start=True, stop=True)
                pe.matmul(bank[1][0:1, COUNT_AT:COUNT_AT + 1], tile_any[0:NT, :], tile_any[0:NT, :], start=True, stop=True)\
                  .then_inc(plan_turned, 1)
                pe.wait_ge(ones_ready, 1)
                pe.wait_ge(gate_exp, 1)
                pe.wait_ge(plan_ready, 1)
                n_tiles = pe.value_load(plan[0:1, COUNT_AT:COUNT_AT + 1], min_val=1, max_val=NT)

                def project(i):
                    pe.wait_ge(ctx_loaded, 16 * (i + 1))
                    for m in range(DC):
                        for c in range(DC):
                            pe.matmul(bank[0][:, m * P:(m + 1) * P], w0[:, 2, c, m * P:(m + 1) * P],
                                      ctx_tile[:, c, :], start=(c == 0), stop=(c == DC - 1))
                    for c in range(DC):
                        mm = pe.matmul(bank[1][:, 0:D], ctx_tile[:, c, :], w0[:, 3, c, :],
                                       start=(c == 0), stop=(c == DC - 1))
                    mm.then_inc(kv_projected, 1)

                def scores(i):
                    pe.wait_ge(q0bd_ready, i + 1)
                    pe.wait_ge(bias_ready, i + 1)
                    pe.wait_ge(k0_ready, i + 1)
                    for m in range(DC):
                        pe.matmul(bank[2 + m], ones_row[:], tile_bias[:].rearrange("p g k -> p (g k)"),
                                  start=True, stop=False, skip_group_check=True)
                        for g in range(4):
                            mm = pe.matmul(bank[2 + m][:, g * P:(g + 1) * P],
                                           q0bd[:, m, 2 * g:2 * g + 2, :].rearrange("p h q -> p (h q)"),
                                           k0T[:, m, :], start=False, stop=True, skip_group_check=True)
                    mm.then_inc(scored, 1)

                project(0)
                scores(0)
                with pe.Fori(0, n_tiles) as i:
                    pe.wait_ge(v0_ready, i + 1)
                    project(i + 1)
                    pe.wait_ge(exped, i + 1)
                    for g in range(G0):
                        mm = pe.transpose(bank[4 + g // 4][:, (g % 4) * P:(g % 4 + 1) * P], probs0[:, g, :], ident)
                    mm.then_inc(turned, 1)
                    scores(i + 1)
                    pe.wait_ge(pT_act, i + 1)
                    pe.wait_ge(pT_dve, i + 1)
                    for g in range(G0):
                        w = 2 * HD0 + 1
                        mm = pe.matmul(bank[6][:, g * w:(g + 1) * w], probs0T[:, g, :], v0[:, g, :], start=True, stop=True)
                    mm.then_inc(attended, 1)
                pe.wait_ge(o_norm_ready, 1)
                for c in range(DC):
                    for b in range(B):
                        mm = pe.matmul(bank[c][:, b * S:(b + 1) * S],
                                       o_norm[:, b, 4 * c:4 * c + 4, :].rearrange("p g j -> p (g j)"), const("fold"),
                                       start=True, stop=True)
                mm.then_inc(o_folded, 1)
                pe.wait_ge(o0T_ready, 2)
                for i in range(TT):
                    for c in range(DC):
                        mm = pe.matmul(bank[4 + i][:, 0:D], o0T[:, c, i * P:(i + 1) * P], w0[:, 4, c, :],
                                       start=(c == 0), stop=(c == DC - 1))
                mm.then_inc(out0_projected, 1)

            def l0_attn():
                with pe.Fori(0, HA // 4) as i:
                    for k in range(2):
                        n = i * 2 + k
                        w = wa[k]
                        pe.wait_ge(wa_loaded[k], 16 * (i + 1))
                        for u in range(2):
                            for j in range(2):
                                for c in range(DC):
                                    o = ((u * 2 + j) * DC + c) * HDA
                                    mm = pe.matmul(bank[3 * u + j], w[:, o:o + HDA], xnT[:, c, :],
                                                   start=(c == 0), stop=(c == DC - 1))
                            mm.then_inc(kqa_projected, 1)
                        pe.wait_ge(a_added, n + 1)
                        for t in range(TT):
                            for c in range(DC):
                                o = 4 * D + c * D
                                mm = pe.matmul(bank[2 + 3 * (t // 2)][:, (t % 2) * D:(t % 2 + 1) * D],
                                               xnT[:, c, t * P:(t + 1) * P], w[:, o:o + D], start=(c == 0), stop=(c == DC - 1))
                        mm.then_inc(va_projected, 1)
                        for u in range(2):
                            pe.wait_ge(kqa_ready, 2 * n + u + 1)
                            for t in range(TT):
                                mm = pe.matmul(bank[6 + u][:, t * P:(t + 1) * P], qaT[:, u, t * P:(t + 1) * P],
                                               kaT[:, u, t * P:(t + 1) * P], start=True, stop=True)
                            mm.then_inc(a_scored, 1)
                        for u in range(2):
                            pe.wait_ge(a_normed, 2 * n + u + 1)
                            for t in range(TT):
                                mm = pe.transpose(bank[3 * u][:, t * P:(t + 1) * P], pa[:, u, t, :], ident)
                            mm.then_inc(a_turned, 1)
                        pe.wait_ge(va_ready, n + 1)
                        for u in range(2):
                            pe.wait_ge(paT_ready, 2 * n + u + 1)
                            for t in range(TT):
                                mm = pe.matmul(bank[1 + 3 * u][:, t * P:(t + 1) * P], va[:, t, u * HDA:(u + 1) * HDA],
                                               paT[:, u, t, :], start=True, stop=True)
                            mm.then_inc(a_mixed, 1)
                        pe.wait_ge(zaT_ready, 2 * n + 2)
                        for t in range(TT):
                            for u in range(2):
                                o = 6 * D + u * D
                                mm = pe.matmul(bank[2 + 3 * (t // 2)][:, (t % 2) * D:(t % 2 + 1) * D],
                                               zaT[:, u, t * P:(t + 1) * P], w[:, o:o + D], start=(u == 0), stop=(u == 1))
                        mm.then_inc(a_out, 1)

            def router(r, w, ne):
                for t in range(TT):
                    for c in range(DC):
                        mm = pe.matmul(bank[7][:, t * ne:(t + 1) * ne], xnT[:, c, t * P:(t + 1) * P], w[:, c, :],
                                       start=(c == 0), stop=(c == DC - 1))
                mm.then_inc(r_scored, 1)

            def up(k, n, width, loaded):
                pe.wait_ge(we_loaded[k], loaded)
                for j in range(2):
                    for c in range(DC):
                        mm = pe.matmul(bank[2 * (k % 2) + j][0:width, :], wgu[k][:, c, j, 0:width], xnT[:, c, :],
                                       start=(c == 0), stop=(c == DC - 1))
                mm.then_inc(e_projected, 1)

            def down(k, n, width):
                pe.wait_ge(hid_ready, n + 1)
                for t in range(TT):
                    mm = pe.matmul(bank[4 + 2 * (k % 2) + t // 2][:, (t % 2) * D:(t % 2 + 1) * D],
                                   hid[k][0:width, t * P:(t + 1) * P], wdn[k][0:width, :], start=True, stop=True)
                mm.then_inc(e_down, 1)

            def experts(n0, first, count, width, one_more):
                with pe.Fori(0, count // NB) as i:
                    for k in range(0, NB, 2):
                        n = n0 + i * NB + k
                        up(k, n, width, 32 * (first + i + 1))
                        up(k + 1, n + 1, width, 32 * (first + i + 1))
                        pe.wait_ge(e_added, n + 1)
                        down(k, n, width)
                        down(k + 1, n + 1, width)
                if one_more:
                    n = n0 + count
                    up(0, n, width, 32 * (first + count // NB + 1))
                    pe.wait_ge(e_added, n + 1)
                    down(0, n, width)

            def l0_ffn():
                pe.wait_ge(router_loaded, 80)
                router(0, wr0, E0)
                pe.wait_ge(sel_ready, 1)
                for t in range(TT):
                    mm = pe.transpose(bank[6][0:E0, t * P:(t + 1) * P], pr[:, t, :], ident)
                mm.then_inc(sel_turned, 1)
                pe.wait_ge(selT_ready, 1)
                for t in range(TT):
                    mm = pe.matmul(bank[5][:, t * G:(t + 1) * G], selT[:, t * P:(t + 1) * P], onehot[:], start=True, stop=True)
                mm.then_inc(w_summed, 1)
                pe.wait_ge(we_ready, 1)
                experts(0, 0, G, I0, False)

            def l1_ffn():
                pe.wait_ge(router_loaded, 80)
                router(1, wr1, E1)
                pe.wait_ge(we_ready, R1 + 1)
                experts(N1, N1 // NB, E1, I1, True)

            def l1_xattn():
                pe.wait_ge(w1_loaded, 16)
                for m in range(DC):
                    for c in range(DC):
                        mm = pe.matmul(bank[2 + m], w1[:, 0, c, m * P:(m + 1) * P], xnT[:, c, :],
                                       start=(c == 0), stop=(c == DC - 1))
                mm.then_inc(q1_projected, 1)
                pe.wait_ge(q1_squared, 1)
                for m in range(DC):
                    mm = pe.matmul(bank[4 + m], const("mean8"), sq1[:, m, :], start=True, stop=True)
                mm.then_inc(q1_meaned, 1)
                pe.wait_ge(q1_r, 1)

                def project_keys(b, j):
                    k, w = j % 2, CHUNK[j + 1] - CHUNK[j]
                    pe.wait_ge(ctxc_loaded[k], 16 * (b * (NCH // 2) + j // 2 + 1))
                    for m in range(DC):
                        for c in range(DC):
                            mm = pe.matmul(bank[m][:, 0:w * P], w1[:, 1, c, m * P:(m + 1) * P], ctxc[k][:, 0:w, c, :],
                                           start=(c == 0), stop=(c == DC - 1))
                    mm.then_inc(k1_projected, 1)

                def mean_squares(b, j):
                    w = CHUNK[j + 1] - CHUNK[j]
                    pe.wait_ge(k1_squared, b * NCH + j + 1)
                    if j == 1:
                        pe.wait_ge(o1T_ready, b + 1)
                    for m in range(DC):
                        mm = pe.matmul(bank[m][:, 0:w * P], const("mean8"), sq1[:, m, 0:w * P], start=True, stop=True)
                    mm.then_inc(k1_meaned, 1)

                def project_values(b, j, t):
                    if not (isinstance(b, int) and b * KT + t == 0):
                        pe.wait_ge(v1_copied, b * KT + t)
                    for c in range(DC):
                        mm = pe.matmul(bank[2][:, 0:D], ctxc[j % 2][:, t - CHUNK[j], c, :], w1[:, 2, c, :],
                                       start=(c == 0), stop=(c == DC - 1))
                    mm.then_inc(v1_projected, 1)

                def scores(b, j, t):
                    keys, o = min(P, S2 - t * P), (t - CHUNK[j]) * P
                    if t == CHUNK[j]:
                        pe.wait_ge(k1_ready, b * NCH + j + 1)
                    if t == 0:
                        pe.wait_ge(q1bd_ready, b + 1)
                        pe.wait_ge(q1bd_low, b + 1)
                    for m in range(DC):
                        if not (isinstance(b, int) and b * KT + t == 0):
                            pe.wait_ge(p1_ready, b * 2 * KT + 2 * t + m - 1)
                        for h in range(2):
                            for part in range(2):
                                mm = pe.matmul(bank[4 + 2 * m + h][0:keys, :], k1s[j % 2][:, m, h, o:o + keys],
                                               q1bd[part][:, m, h, :, :].rearrange("p h q -> p (h q)"),
                                               start=(part == 0), stop=(part == 1))
                        mm.then_inc(s1_scored, 1)

                def mix(b, j, t):
                    keys = min(P, S2 - t * P)
                    pe.wait_ge(v1_copied, b * KT + t + 1)
                    pe.wait_ge(p1_ready, b * 2 * KT + 2 * t + 2)
                    if t == 0:
                        pe.wait_ge(acc1_copied, b + 1)
                    for g in range(G1):
                        q, s = g % 4, g // 4
                        mm = pe.matmul(bank[3][32 * q:32 * q + 32, s * P:(s + 1) * P], v1[0:keys, j % 2, t - CHUNK[j], g, :],
                                       p1[t % 2][0:keys, g * P:(g + 1) * P], start=(t == 0 and s == 0), stop=(t == KT - 1),
                                       skip_group_check=True)
                    mm.then_inc(p1_used, 1)

                project_keys(0, 0)
                mean_squares(0, 0)
                for t in range(CHUNK[1]):
                    project_values(0, 0, t)
                project_keys(0, 1)
                scores(0, 0, 0)
                with pe.Fori(0, B) as b:
                    for j in range(NCH):
                        b1, j1 = (b, j + 1) if j + 1 < NCH else (b + 1, 0)
                        b2, j2 = (b, j + 2) if j + 2 < NCH else (b + 1, j + 2 - NCH)
                        values = list(range(CHUNK[j1], CHUNK[j1 + 1]))
                        for t in range(CHUNK[j], CHUNK[j + 1]):
                            if t == CHUNK[j]:
                                mean_squares(b1, j1)
                            elif t + 1 == CHUNK[j + 1]:
                                project_keys(b2, j2)
                            if t + 1 < KT:
                                scores(b, j if t + 1 < CHUNK[j + 1] else j + 1, t + 1)
                            for _ in range(2 if t == CHUNK[j] + 1 else 1):
                                if values:
                                    project_values(b1, j1, values.pop(0))
                            mix(b, j, t)
                        assert not values
                    scores(b + 1, 0, 0)
                    pe.wait_ge(acc1_copied, b + 2)
                    pe.wait_ge(k1_copied, (b + 1) * NCH + 2)
                    for s in range(4):
                        mm = pe.transpose(bank[0][:, s * P:(s + 1) * P], acc1[:, s * P:(s + 1) * P], ident)
                    mm.then_inc(acc1_turned, 1)
                    pe.wait_ge(on1_ready, b + 1)
                    for c in range(DC):
                        mm = pe.matmul(bank[1][:, c * S:(c + 1) * S],
                                       on1[:, 8 * c:8 * c + 8, :].rearrange("p g j -> p (g j)"), const("fold"),
                                       start=True, stop=True)
                    mm.then_inc(o1_folded, 1)
                pe.wait_ge(o1T_ready, B + 1)
                pe.wait_ge(v1_copied, B * KT + CHUNK[1])
                for c in range(DC):
                    for i in range(TT):
                        mm = pe.transpose(bank[i][:, c * P:(c + 1) * P], o1T[:, c, i * P:(i + 1) * P], ident)
                mm.then_inc(o1_turned, 1)

            def l1_attn():
                pe.wait_ge(wb_loaded, 32)
                for t in range(TT):
                    for c in range(DC):
                        mm = pe.matmul(bank[2 + t][:, 0:QKV], xnT[:, c, t * P:(t + 1) * P], wqkv[:, c, :],
                                       start=(c == 0), stop=(c == DC - 1))
                    mm.then_inc(qkv_projected, 1)

                def turn_qk(t):
                    pe.wait_ge(rotated, t + 1)
                    if t >= 1:
                        pe.wait_ge(qbT_ready, t)
                        pe.wait_ge(kbd_ready, t)
                    qk = rot[:, t, 0:HB, :].rearrange("p h d -> p (h d)")
                    for m in range(DC):
                        pe.transpose(bank[0][:, m * P:(m + 1) * P], qk[:, m * P:(m + 1) * P], ident)
                    pe.transpose(bank[0][:, 2 * P:3 * P], krep[:, t, :, :].rearrange("p h d -> p (h d)"), ident)\
                      .then_inc(qk_turned, 1)

                def scores(j):
                    t, m, h = j // 4, j // 2 % 2, j % 2
                    if j % 4 == 0:
                        pe.wait_ge(qbT_ready, t + 1)
                        pe.wait_ge(kbd_ready, t + 1)
                    if j >= 2:
                        pe.wait_ge(b_maxed, j - 1)
                    pe.matmul(bank[6 + j % 2], qbT[:, m, t * P:(t + 1) * P],
                              kbd[t % 2][:, 4 * h:4 * h + 4, :].rearrange("p h k -> p (h k)"), start=True, stop=True)\
                      .then_inc(b_scored, 1)

                def mix(j):
                    t = j // 4
                    pe.wait_ge(b_normed, j + 1)
                    if j >= 1:
                        pe.wait_ge(pbT_ready, j)
                    for h in range(4):
                        mm = pe.transpose(bank[1][:, h * P:(h + 1) * P], pa[:, j % 2, h, :], ident)
                    mm.then_inc(b_turned, 1)
                    pe.wait_ge(pbT_ready, j + 1)
                    if j >= 4 and j % 4 == 0:
                        pe.wait_ge(ob_ready, t)
                    for h in range(4):
                        k = (j % 4 * 4 + h) * HDB
                        mm = pe.matmul(bank[2][:, k:k + HDB], paT[:, j % 2, h, :], vb[:, t, :], start=True, stop=True)
                    mm.then_inc(b_mixed, 1)

                def project(t):
                    pe.wait_ge(ob_ready, t + 1)
                    if t >= 1:
                        pe.wait_ge(b_added, t)
                    for c in range(DC):
                        mm = pe.transpose(bank[3][:, c * P:(c + 1) * P], ob[:, t, c * P:(c + 1) * P], ident)
                    mm.then_inc(ob_turned, 1)
                    pe.wait_ge(obT_ready, t + 1)
                    for c in range(DC):
                        mm = pe.matmul(bank[4][:, 0:D], obT[:, c, t * P:(t + 1) * P], wout[:, c, :],
                                       start=(c == 0), stop=(c == DC - 1))
                    mm.then_inc(b_out, 1)

                pe.wait_ge(rotated, TT)
                turn_qk(0)
                for j in range(4 * TT + 1):
                    if j < 4 * TT:
                        scores(j)
                    if j % 4 == 1 and j // 4 + 1 < TT:
                        turn_qk(j // 4 + 1)
                    if j >= 1:
                        mix(j - 1)
                    if j >= 4 and j % 4 == 0:
                        project(j // 4 - 1)

            pe.wait_ge(consts_loaded, 16)
            if 1 in stages:
                layernorm(1)
                l0_xattn()
            if 2 in stages:
                layernorm(2)
                l0_attn()
            if 3 in stages:
                layernorm(3)
                l0_ffn()
            if 4 in stages:
                layernorm(4)
                l1_xattn()
            if 5 in stages:
                layernorm(5)
                l1_attn()
            if 6 in stages:
                layernorm(6)
                l1_ffn()

        @block.scalar
        def _(act):
            chain = Chain(act, act_chain)

            def rsqrt(dst, src, bias, scale=1.0):
                chain(act.activation(lnv[:], src, ACT.Ln, bias=bias, scale=scale))
                return act.activation(dst, lnv[:], ACT.Exp, scale=-0.5)

            def layernorm(stage):
                s = LN_AT[stage]
                act.wait_ge(var_ready, s + 1)
                rsqrt(rstd[:], mv[:, :, 1], eps[:, 0:1]).then_inc(rstd_ready, 1)
                if stage == 1:
                    act.wait_ge(sumsq_ready, 1)
                    rsqrt(rstd[:], ms[:], eps[:, 1:2], 1.0 / D).then_inc(rrms_ready, 1)
                act.wait_ge(xn_turned, s + 1)
                if stage == 1:
                    act.wait_ge(w0_loaded, 32)
                    act.activation(xnT[:, 0, :], bank[0], ACT.Copy, scale=normw[:, 0:1]).then_inc(xnT_act, 1)
                else:
                    act.activation(xnT[:, 0, :], bank[0], ACT.Copy).then_inc(xnT_act, 1)

            def l0_xattn():
                act.wait_ge(q0_projected, 1)
                for m in range(DC):
                    act.activation(q0T[:, m, :], bank[2 + m], ACT.Copy, scale=HD0 ** -0.5).then_inc(q0T_ready, 1)
                act.wait_ge(gate_projected, 1)
                for i in range(TT):
                    e = act.activation(gate[:, i, :], bank[4 + i][:, 0:D], ACT.Exp, scale=-1.0)
                e.then_inc(gate_exp, 1)
                act.wait_ge(plan_ready, 1)
                n_tiles = act.value_load(plan[0:1, COUNT_AT:COUNT_AT + 1], min_val=1, max_val=NT)

                def copy_k(i):
                    act.wait_ge(kv_projected, i + 1)
                    act.activation(k0T[:].rearrange("p m k -> p (m k)"), bank[0][:, 0:D], ACT.Copy).then_inc(k0_ready, 1)

                copy_k(0)
                with act.Fori(0, n_tiles) as i:
                    act.wait_ge(shifted, i + 1)
                    act.activation(probs0[:], probs0[:], ACT.Exp).then_inc(exped, 1)
                    act.activation(alpha[:], m_step[:], ACT.Exp).then_inc(alpha_ready, 1)
                    copy_k(i + 1)
                    act.wait_ge(turned, i + 1)
                    act.activation(probs0T[:, 0:4, :].rearrange("p g k -> p (g k)"), bank[4], ACT.Copy).then_inc(pT_act, 1)
                act.wait_ge(o_folded, 1)
                act.activation(o0T[:, 0, :], bank[0], ACT.Copy).then_inc(o0T_ready, 1)

            def l0_attn():
                with act.Fori(0, HA // 4) as i:
                    for k in range(2):
                        n = i * 2 + k
                        for u in range(2):
                            act.wait_ge(kqa_projected, 2 * n + u + 1)
                            act.activation(kaT[:, u, :], bank[3 * u], ACT.Copy)
                            act.activation(qaT[:, u, :], bank[3 * u + 1], ACT.Copy).then_inc(kqa_ready, 1)
                        for u in range(2):
                            act.wait_ge(a_maxed, 2 * n + u + 1)
                            for t in range(TT):
                                e = act.activation(pa[:, u, t, :], pa[:, u, t, :], ACT.Exp, bias=maxa[:, u, t:t + 1],
                                                   scale=HDA ** -0.5, accum_out=suma[:, u, t:t + 1])
                            e.then_inc(a_exped, 1)
                        for u in range(2):
                            act.wait_ge(a_turned, 2 * n + u + 1)
                            act.activation(paT[:, u, :, :].rearrange("p t q -> p (t q)"), bank[3 * u], ACT.Copy).then_inc(paT_ready, 1)

            def router(r):
                act.wait_ge(r_shifted, r * R1 + 1)
                ne = (E0, E1)[r]
                act.activation(pr[:, :, 0:ne], pr[:, :, 0:ne], ACT.Exp).then_inc(r_exped, 1)

            def experts(n0, count, width, one_more):
                def silu(k, n):
                    act.wait_ge(e_projected, n + 1)
                    act.activation(hid[k][0:width, :], bank[2 * (k % 2)][0:width, :], ACT.Silu).then_inc(silu_ready, 1)
                with act.Fori(0, count // NB) as i:
                    for k in range(NB):
                        silu(k, n0 + i * NB + k)
                if one_more:
                    silu(0, n0 + count)

            def l1_xattn():
                def mean_rsqrt(first, w, n):
                    for m in range(DC):
                        act.activation(r1[:, m, 0:w], bank[first + m][:, 0:w], ACT.Ln, bias=eps[:, 1:2]).then_inc(r1_ln, 1)
                    act.wait_ge(r1_ln, n)
                    return act.activation(r1[:, :, 0:w], r1[:, :, 0:w], ACT.Exp, scale=-0.5)

                act.wait_ge(q1_projected, 1)
                for m in range(DC):
                    e = act.activation(sq1[:, m, :], bank[2 + m], ACT.Square)
                e.then_inc(q1_squared, 1)
                act.wait_ge(q1_meaned, 1)
                mean_rsqrt(4, 512, 2).then_inc(q1_r, 1)

                def square(b, j):
                    w = (CHUNK[j + 1] - CHUNK[j]) * P
                    act.wait_ge(k1_copied, b * NCH + j + 1)
                    act.activation(sq1[:, :, 0:w], k1f[:, :, 0:w], ACT.Square).then_inc(k1_squared, 1)

                def norm(b, j):
                    act.wait_ge(k1_meaned, b * NCH + j + 1)
                    mean_rsqrt(0, (CHUNK[j + 1] - CHUNK[j]) * P, 2 * (b * NCH + j) + 4).then_inc(r1_ready, 1)

                def high_k(b, j):
                    w = (CHUNK[j + 1] - CHUNK[j]) * P
                    act.wait_ge(k1_normed, b * NCH + j + 1)
                    for half in range(2):
                        own = slice(S * half, S * half + S)
                        act.activation(k1s[j % 2][own, :, half, 0:w], k1f[own, :, 0:w], ACT.Copy).then_inc(k1_high, 1)

                def exp(b, t):
                    keys = min(P, S2 - t * P)
                    act.wait_ge(p1_used, b * KT + max(t, 1))
                    for m in range(DC):
                        act.wait_ge(s1_scored, b * 2 * KT + 2 * t + m + 1)
                        act.activation(p1[t % 2][0:keys, m * 1024:(m + 1) * 1024], pair[2 + m][0:keys, :], ACT.Exp,
                                       scale=HD1 ** -0.5).then_inc(p1_ready, 1)

                square(0, 0)
                norm(0, 0)
                high_k(0, 0)
                square(0, 1)
                exp(0, 0)
                with act.Fori(0, B) as b:
                    for j in range(NCH):
                        b1, j1 = (b, j + 1) if j + 1 < NCH else (b + 1, 0)
                        b2, j2 = (b, j + 2) if j + 2 < NCH else (b + 1, j + 2 - NCH)
                        for t in range(CHUNK[j], CHUNK[j + 1]):
                            if t == CHUNK[j]:
                                norm(b1, j1)
                            if t + 1 < KT:
                                exp(b, t + 1)
                            if t == CHUNK[j]:
                                high_k(b1, j1)
                        square(b2, j2)
                    exp(b + 1, 0)

            def l1_attn():
                for j in range(4 * TT + 1):
                    if j < 4 * TT:
                        t = j // 4
                        if j % 4 == 0:
                            act.wait_ge(qk_turned, t + 1)
                            act.activation(qbT[:, :, t * P:(t + 1) * P], bank[0][:, 0:D].rearrange("p (m q) -> p m q", m=DC), ACT.Copy)\
                               .then_inc(qbT_ready, 1)
                        act.wait_ge(b_maxed, j + 1)
                        for h in range(4):
                            e = act.activation(pa[:, j % 2, h, :], pa[:, j % 2, h, :], ACT.Exp, bias=maxa[:, j % 2, h:h + 1],
                                               scale=HDB ** -0.5, accum_out=suma[:, j % 2, h:h + 1])
                        e.then_inc(b_exped, 1)
                    if j >= 1:
                        act.wait_ge(b_turned, j)
                        act.activation(paT[:, (j - 1) % 2, :, :].rearrange("p t q -> p (t q)"), bank[1], ACT.Copy).then_inc(pbT_ready, 1)

            act.sem_inc(p1_used, 1)
            act.preload_act_table_set("natural_log_exp_and_others")
            act.wait_ge(eps_ready, 2)
            if 1 in stages:
                layernorm(1)
                l0_xattn()
            if 2 in stages:
                layernorm(2)
                l0_attn()
            if 3 in stages:
                layernorm(3)
                router(0)
                experts(0, G, I0, False)
            if 4 in stages:
                act.preload_act_table_set("natural_log_exp_and_others")
                layernorm(4)
                l1_xattn()
            if 5 in stages:
                layernorm(5)
                l1_attn()
            if 6 in stages:
                layernorm(6)
                router(1)
                experts(N1, E1, I1, True)

        @block.gpsimd
        def _(pool):
            def l0_xattn():
                pool.wait_ge(consts_loaded, 16)
                pool.wait_ge(q0T_ready, 2)
                pool.wait_ge(plan_ready, 1)
                n_tiles = pool.value_load(plan[0:1, COUNT_AT:COUNT_AT + 1], min_val=1, max_val=NT)

                def queries(i):
                    b = pool.value_load(plan[0:1, bass.ds(i + NT + 1, 1)], min_val=0, max_val=B - 1)
                    for m in range(DC):
                        ins = pool.tensor_tensor(q0bd[:, m, :, :], const("head16").unsqueeze(2).broadcast_to([P, 8, S]),
                                                 q0T[:, m, bass.ds(b * S, S)].unsqueeze(1).broadcast_to([P, 8, S]), ALU.mult)
                    ins.then_inc(q0bd_ready, 1)
                queries(0)
                with pool.Fori(0, n_tiles) as i:
                    pool.wait_ge(scored, i + 1)
                    queries(i + 1)

            def l1_xattn():
                pool.wait_ge(consts_loaded, 16)
                pool.wait_ge(q1_split, 1)

                def queries(bb):
                    for m in range(DC):
                        for h in range(2):
                            ins = pool.tensor_tensor(q1bd[1][:, m, h, :, :], const("head8s").unsqueeze(2).broadcast_to([P, 8, S]),
                                                     q1s[1][:, m, h, bass.ds(bb * S, S)].unsqueeze(1).broadcast_to([P, 8, S]), ALU.mult)
                    ins.then_inc(q1bd_low, 1)

                queries(0)
                with pool.Fori(0, B) as b:
                    pool.wait_ge(s1_scored, (b + 1) * 2 * KT)
                    queries((b + 1) % B)

            if 1 in stages:
                l0_xattn()
            if 4 in stages:
                l1_xattn()

        @block.vector
        def _(v):
            chain = Chain(v, dve_chain)

            def layernorm(stage):
                s = LN_AT[stage]
                for i in range(TT):
                    ins = v.bn_stats(stats[:, i, :], x[:, i, :])
                chain(ins)
                for i in range(TT):
                    ins = v.bn_aggr(mv[:, i, :], stats[:, i, :])
                ins.then_inc(var_ready, 1)
                v.wait_ge(var_ready, s + 1)
                v.wait_ge(rstd_ready, s + 1)
                if stage == 1:
                    for i in range(TT):
                        chain(v.tensor_scalar(xn[:, i, :], x[:, i, :], mv[:, i, 0:1], rstd[:, i:i + 1],
                                              ALU.subtract, ALU.mult))
                    for i in range(TT):
                        ins = v.tensor_tensor_reduce(scratch[:, i, :], xn[:, i, :], xn[:, i, :], 1.0, 0.0,
                                                     ALU.mult, ALU.add, ms[:, i:i + 1])
                    ins.then_inc(sumsq_ready, 1)
                    v.wait_ge(rrms_ready, 1)
                    for i in range(TT):
                        v.tensor_scalar(xn[:, i, :], xn[:, i, :], rstd[:, i:i + 1], None, ALU.mult).then_inc(xn_ready, 1)
                    v.wait_ge(w0_loaded, 32)
                    v.wait_ge(xn_turned, 1)
                    v.tensor_scalar(xnT[:, 1, :], bank[1], normw[:, 1:2], None, ALU.mult).then_inc(xnT_dve, 1)
                else:
                    for i in range(TT):
                        v.tensor_scalar(xn[:, i, :], x[:, i, :], mv[:, i, 0:1], rstd[:, i:i + 1],
                                        ALU.subtract, ALU.mult).then_inc(xn_ready, 1)
                    v.wait_ge(xn_turned, s + 1)
                    v.tensor_copy(xnT[:, 1, :], bank[1]).then_inc(xnT_dve, 1)

            def l0_xattn():
                v.memset(ones_row[:], 1.0).then_inc(ones_ready, 1)
                v.wait_ge(mask_loaded, 16)
                v.tensor_reduce(tile_any[0:B * KT, :], mask_tiles[:], AX.X, ALU.max).then_inc(any_ready, 1)
                v.wait_ge(any_turned, 1)
                v.tensor_copy(tile_at[0:NT, :], bank[0][0:NT, 0:1]).then_inc(tile_at_ready, 1)
                v.wait_ge(tile_at_ready, 1)
                v.wait_ge(any_ready, 1)
                v.tensor_scalar(tile_hot[0:NT, :], const("count")[0:NT, :], tile_at[0:NT, 0:1], tile_any[0:NT, 0:1],
                                ALU.is_equal, ALU.mult).then_inc(tile_hot_ready, 1)
                v.wait_ge(plan_turned, 1)
                v.tensor_copy(plan[:, 0:COUNT_AT], bank[1][0:1, 0:COUNT_AT])
                v.tensor_scalar(plan[:, COUNT_AT:], bank[1][0:1, COUNT_AT:COUNT_AT + 1], 1.0, None, ALU.max).then_inc(plan_ready, 1)
                v.wait_ge(gate_exp, 1)
                chain(v.tensor_scalar(gate[:], gate[:], 1.0, None, ALU.add))
                chain(v.reciprocal(gate[:], gate[:]))
                v.memset(m_run[:], NEG)
                v.memset(v0[:, :, 2 * HD0:], 1.0)
                chain(v.memset(o_run[:], 0.0))
                v.wait_ge(plan_ready, 1)
                n_tiles = v.value_load(plan[0:1, COUNT_AT:COUNT_AT + 1], min_val=1, max_val=NT)
                steps = Chain(v, tile_chain)

                def batch_of(i):
                    return v.value_load(plan[0:1, bass.ds(i + NT + 1, 1)], min_val=0, max_val=B - 1)

                def mask_bias(i):
                    v.wait_ge(mask_tile_loaded, 16 * (i + 1))
                    v.tensor_scalar(tile_bias[:], mask_tile[:].unsqueeze(1).broadcast_to([1, 4, P]),
                                    1.0, -NEG, ALU.subtract, ALU.mult).then_inc(bias_ready, 1)

                def copy_v(i):
                    v.wait_ge(kv_projected, i + 1)
                    v.tensor_copy(v0[:, :, 0:2 * HD0], bank[1][:, 0:D].rearrange("p (g j) -> p g j", g=G0)).then_inc(v0_ready, 1)

                def shift(i, b):
                    m_old = m_run[:, bass.ds(b, 1), :].rearrange("p o g -> p (o g)")
                    v.wait_ge(scored, i + 1)
                    for m in range(DC):
                        ins = v.tensor_reduce(m_tile[:, 4 * m:4 * m + 4], bank[2 + m].rearrange("p (g k) -> p g k", g=4),
                                              AX.X, ALU.max)
                    steps(ins)
                    steps(v.tensor_tensor(m_new[:], m_old, m_tile[:], ALU.max))
                    steps(v.tensor_tensor(m_step[:], m_old, m_new[:], ALU.subtract))
                    v.tensor_tensor(m_old, m_old, m_tile[:], ALU.max)
                    for m in range(DC):
                        ins = v.tensor_tensor(probs0[:, 4 * m:4 * m + 4, :], bank[2 + m].rearrange("p (g k) -> p g k", g=4),
                                              m_new[:, 4 * m:4 * m + 4].unsqueeze(2).broadcast_to([P, 4, P]), ALU.subtract)
                    ins.then_inc(shifted, 1)
                    v.wait_ge(shifted, i + 1)

                mask_bias(0)
                copy_v(0)
                shift(0, batch_of(0))
                with v.Fori(0, n_tiles) as i:
                    PER_TILE = 5
                    began = steps.enter(i, PER_TILE)
                    b = batch_of(i)
                    o = o_run[:, bass.ds(b, 1), :, :].rearrange("p o g j -> p (o g) j")
                    mask_bias(i + 1)
                    v.wait_ge(alpha_ready, i + 1)
                    steps(v.tensor_tensor(o, o, alpha[:].unsqueeze(2).broadcast_to([P, G0, 2 * HD0 + 1]), ALU.mult))
                    v.wait_ge(turned, i + 1)
                    v.tensor_copy(probs0T[:, 4:8, :].rearrange("p g k -> p (g k)"), bank[5]).then_inc(pT_dve, 1)
                    shift(i + 1, batch_of(i + 1))
                    v.wait_ge(attended, i + 1)
                    steps(v.tensor_tensor(o, o, bank[6][:, 0:G0 * (2 * HD0 + 1)].rearrange("p (g j) -> p g j", g=G0), ALU.add))
                    copy_v(i + 1)
                    steps.leave(began, 1)
                chain(v.tensor_scalar(l_inv[:], o_run[:, :, :, 2 * HD0], 1e-30, None, ALU.max))
                chain(v.reciprocal(l_inv[:], l_inv[:]))
                chain(v.tensor_scalar(m_run[:], m_run[:], 0.1 * NEG, None, ALU.is_gt))
                chain(v.tensor_tensor(l_inv[:], l_inv[:], m_run[:], ALU.mult))
                flat_o = o_norm.rearrange("p b g j -> p (b g) j")
                chain(v.tensor_tensor(flat_o, o_run[:].rearrange("p b g j -> p (b g) j")[:, :, 0:2 * HD0],
                                      l_inv[:].rearrange("p b g -> p (b g)").unsqueeze(2).broadcast_to([P, B * G0, 2 * HD0]), ALU.mult))
                v.tensor_tensor(flat_o, flat_o, const("own16").unsqueeze(1).broadcast_to([P, B * G0, 2 * HD0]), ALU.mult)\
                 .then_inc(o_norm_ready, 1)
                v.wait_ge(o_folded, 1)
                v.tensor_copy(o0T[:, 1, :], bank[1]).then_inc(o0T_ready, 1)
                v.wait_ge(out0_projected, 1)
                for i in range(TT):
                    ins = v.tensor_tensor(scratch[:, i, :], bank[4 + i][:, 0:D], gate[:, i, :], ALU.mult)
                chain(ins)
                chain(v.tensor_tensor(x[:], x[:], scratch[:], ALU.add))

            def l0_attn():
                PER_PAIR = 4
                with v.Fori(0, HA // 4) as i:
                    began = chain.enter(i, 2 * PER_PAIR)
                    for k in range(2):
                        n = i * 2 + k
                        v.wait_ge(va_projected, n + 1)
                        for j in range(2):
                            ins = v.tensor_copy(va[:, 2 * j:2 * j + 2, :].rearrange("p t f -> p (t f)"), bank[2 + 3 * j])
                        ins.then_inc(va_ready, 1)
                        for u in range(2):
                            v.wait_ge(a_scored, 2 * n + u + 1)
                            chain(v.tensor_tensor(pa[:, u, :, :], bank[6 + u].rearrange("p (t k) -> p t k", t=TT),
                                                  const("causal").unsqueeze(1).broadcast_to([P, TT, P]), ALU.add))
                            chain(v.tensor_reduce(maxa[:, u, :], pa[:, u, :, :], AX.X, ALU.max))
                            v.tensor_scalar(maxa[:, u, :], maxa[:, u, :], -HDA ** -0.5, None, ALU.mult).then_inc(a_maxed, 1)
                        for u in range(2):
                            v.wait_ge(a_exped, 2 * n + u + 1)
                            v.reciprocal(suma[:, u, :], suma[:, u, :]).then_inc(a_summed, 1)
                            v.wait_ge(a_summed, 2 * n + u + 1)
                            v.tensor_tensor(pa[:, u, :, :], pa[:, u, :, :],
                                            suma[:, u, :].unsqueeze(2).broadcast_to([P, TT, P]), ALU.mult).then_inc(a_normed, 1)
                        for u in range(2):
                            v.wait_ge(a_mixed, 2 * n + u + 1)
                            v.tensor_copy(zaT[:, u, :], bank[1 + 3 * u]).then_inc(zaT_ready, 1)
                        v.wait_ge(a_out, n + 1)
                        for j in range(2):
                            ins = v.tensor_tensor(x[:, 2 * j:2 * j + 2, :], x[:, 2 * j:2 * j + 2, :],
                                                  bank[2 + 3 * j].rearrange("p (t f) -> p t f", t=2), ALU.add)
                        ins.then_inc(a_added, 1)
                        v.wait_ge(a_added, n + 2)
                    chain.leave(began, HA // 4)

            def l1_xattn():
                chain(v.memset(v1[:, :, :, :, 2 * HD1:], 1.0))
                v.wait_ge(q1_squared, 1)
                for m in range(DC):
                    ins = v.tensor_copy(q1T[:, m, :], bank[2 + m])
                ins.then_inc(q1_copied, 1)
                v.wait_ge(q1_copied, 1)
                v.wait_ge(q1_r, 1)
                chain(v.tensor_tensor(q1T[:], q1T[:], r1[:], ALU.mult))
                for half in range(2):
                    own = slice(S * half, S * half + S)
                    for to in range(2):
                        ins = v.tensor_copy(q1s[0][S * to:S * to + S, :, half, :], q1T[own, :, :])
                    chain(ins)
                    for to in range(2):
                        ins = v.tensor_tensor(q1s[1][S * to:S * to + S, :, half, :], q1T[own, :, :],
                                              q1s[0][own, :, half, :], ALU.subtract)
                ins.then_inc(q1_split, 1)
                v.wait_ge(q1_split, 1)

                def queries(bb):
                    for m in range(DC):
                        for h in range(2):
                            ins = v.tensor_tensor(q1bd[0][:, m, h, :, :], const("head8s").unsqueeze(2).broadcast_to([P, 8, S]),
                                                  q1s[0][:, m, h, bass.ds(bb * S, S)].unsqueeze(1).broadcast_to([P, 8, S]), ALU.mult)
                    ins.then_inc(q1bd_ready, 1)

                def copy_k(b, j):
                    w = (CHUNK[j + 1] - CHUNK[j]) * P
                    v.wait_ge(k1_projected, b * NCH + j + 1)
                    v.tensor_copy(k1f[:, :, 0:w], pair[0][:].rearrange("p (m k) -> p m k", m=DC)[:, :, 0:w]).then_inc(k1_copied, 1)

                def norm_k(b, j):
                    w = (CHUNK[j + 1] - CHUNK[j]) * P
                    v.wait_ge(k1_copied, b * NCH + j + 1)
                    v.wait_ge(r1_ready, b * NCH + j + 1)
                    v.tensor_tensor(k1f[:, :, 0:w], k1f[:, :, 0:w], r1[:, :, 0:w], ALU.mult).then_inc(k1_normed, 1)
                    v.wait_ge(k1_normed, b * NCH + j + 1)

                def low_k(b, j):
                    w = (CHUNK[j + 1] - CHUNK[j]) * P
                    k = k1s[j % 2]
                    for half in range(2):
                        v.wait_ge(k1_high, 2 * (b * NCH + j) + half + 1)
                        own, other = slice(S * half, S * half + S), slice(S - S * half, P - S * half)
                        ins = v.tensor_tensor(k[other, :, half, 0:w], k1f[own, :, 0:w], k[own, :, half, 0:w], ALU.subtract)
                    ins.then_inc(k1_ready, 1)

                def copy_v(b, j, t):
                    v.wait_ge(v1_projected, b * KT + t + 1)
                    v.tensor_copy(v1[:, j % 2, t - CHUNK[j], :, 0:2 * HD1], bank[2][:, 0:D].rearrange("p (g j) -> p g j", g=G1))\
                     .then_inc(v1_copied, 1)

                copy_k(0, 0)
                queries(0)
                norm_k(0, 0)
                low_k(0, 0)
                for t in range(CHUNK[1]):
                    copy_v(0, 0, t)
                copy_k(0, 1)
                PER_BATCH = 2
                with v.Fori(0, B) as b:
                    began = chain.enter(b, PER_BATCH)
                    for j in range(NCH):
                        b1, j1 = (b, j + 1) if j + 1 < NCH else (b + 1, 0)
                        b2, j2 = (b, j + 2) if j + 2 < NCH else (b + 1, j + 2 - NCH)
                        norm_k(b1, j1)
                        values = list(range(CHUNK[j1], CHUNK[j1 + 1]))
                        copy_v(b1, j1, values[0])
                        low_k(b1, j1)
                        for t in values[1:3]:
                            copy_v(b1, j1, t)
                        if j == NCH - 1:
                            v.wait_ge(s1_scored, (b + 1) * 2 * KT)
                            queries((b + 1) % B)
                        for t in values[3:]:
                            copy_v(b1, j1, t)
                        copy_k(b2, j2)
                        if j == NCH - 1:
                            v.wait_ge(p1_used, (b + 1) * KT + 1)
                            v.tensor_copy(acc1, bank[3]).then_inc(acc1_copied, 1)
                    v.wait_ge(acc1_turned, b + 1)
                    o = bank[0].rearrange("p (g r) -> p g r", g=G1)
                    chain(v.reciprocal(rden1[:], o[:, :, 2 * HD1]))
                    chain(v.tensor_tensor(on1[:], o[:, :, 0:2 * HD1], rden1[:].unsqueeze(2).broadcast_to([P, G1, 2 * HD1]), ALU.mult))
                    v.tensor_tensor(on1[:], on1[:], const("own8").unsqueeze(1).broadcast_to([P, G1, 2 * HD1]), ALU.mult)\
                     .then_inc(on1_ready, 1)
                    v.wait_ge(o1_folded, b + 1)
                    v.tensor_copy(o1T[:, :, bass.ds(b * S, S)], bank[1][:, 0:DC * S].rearrange("p (c q) -> p c q", c=DC))\
                     .then_inc(o1T_ready, 1)
                    chain.leave(began, B)
                v.wait_ge(o1_turned, 1)
                for i in range(TT):
                    ins = v.tensor_tensor(x[:, i, :], x[:, i, :], bank[i][:, 0:D], ALU.add)
                chain(ins)

            def l1_attn():
                for t in range(TT):
                    v.wait_ge(qkv_projected, t + 1)
                    z = bank[2 + t][:, 0:NR * HDB].rearrange("p (h d) -> p h d", h=NR)
                    hd = HDB // 2
                    cos, sin = const("cos"), const("sin")
                    v.tensor_tensor(rot[:, t, :, :], z, cos.unsqueeze(1).broadcast_to([P, NR, HDB]), ALU.mult)
                    v.tensor_tensor(rot2[:, t, :, 0:hd], z[:, :, hd:], sin[:, 0:hd].unsqueeze(1).broadcast_to([P, NR, hd]), ALU.mult)
                    v.tensor_tensor(rot2[:, t, :, hd:], z[:, :, 0:hd], sin[:, hd:].unsqueeze(1).broadcast_to([P, NR, hd]), ALU.mult)
                    chain(v.tensor_copy(vb[:, t, :], bank[2 + t][:, NR * HDB:QKV]))
                    chain(v.tensor_tensor(rot[:, t, :, :], rot[:, t, :, :], rot2[:, t, :, :], ALU.add))
                    v.tensor_copy(krep[:, t, :, :], rot[:, t, HB:NR, :].broadcast_to([P, 8, HDB])).then_inc(rotated, 1)
                for j in range(4 * TT + 1):
                    t = j // 4
                    if j < 4 * TT:
                        if j % 4 == 0:
                            v.wait_ge(qk_turned, t + 1)
                            v.wait_ge(qbT_ready, t + 1)
                            v.tensor_tensor(kbd[t % 2][:], const("head16").unsqueeze(2).broadcast_to([P, 8, P]),
                                            bank[0][:, 2 * P:3 * P].unsqueeze(1).broadcast_to([P, 8, P]), ALU.mult).then_inc(kbd_ready, 1)
                        v.wait_ge(b_scored, j + 1)
                        if j >= 2:
                            v.wait_ge(b_turned, j - 1)
                        chain(v.tensor_tensor(pa[:, j % 2, :, :], bank[6 + j % 2].rearrange("p (h k) -> p h k", h=4),
                                              const("block").unsqueeze(1).broadcast_to([P, 4, P]), ALU.add))
                        chain(v.tensor_reduce(maxa[:, j % 2, :], pa[:, j % 2, :, :], AX.X, ALU.max))
                        v.tensor_scalar(maxa[:, j % 2, :], maxa[:, j % 2, :], -HDB ** -0.5, None, ALU.mult).then_inc(b_maxed, 1)
                        v.wait_ge(b_exped, j + 1)
                        v.reciprocal(suma[:, j % 2, :], suma[:, j % 2, :]).then_inc(b_summed, 1)
                        v.wait_ge(b_summed, j + 1)
                        v.tensor_tensor(pa[:, j % 2, :, :], pa[:, j % 2, :, :],
                                        suma[:, j % 2, :].unsqueeze(2).broadcast_to([P, 4, P]), ALU.mult).then_inc(b_normed, 1)
                    if j >= 4 and j % 4 == 0:
                        t = j // 4 - 1
                        v.wait_ge(b_mixed, j)
                        v.tensor_copy(ob[:, t, :], bank[2][:, 0:D]).then_inc(ob_ready, 1)
                        v.wait_ge(ob_turned, t + 1)
                        v.tensor_copy(obT[:, :, t * P:(t + 1) * P], bank[3][:, 0:D].rearrange("p (c q) -> p c q", c=DC)).then_inc(obT_ready, 1)
                        v.wait_ge(b_out, t + 1)
                        v.tensor_tensor(x[:, t, :], x[:, t, :], bank[4][:, 0:D], ALU.add).then_inc(b_added, 1)
                v.wait_ge(b_added, TT)

            def softmax_rows(r, ne):
                v.wait_ge(r_scored, r * R1 + 1)
                p = pr[:, :, 0:ne]
                logits = bank[7][:, 0:TT * ne].rearrange("p (t e) -> p t e", t=TT)
                if r == 1:
                    chain(v.tensor_tensor(p, logits, bias1[:].unsqueeze(1).broadcast_to([P, TT, E1]), ALU.add))
                    logits = p
                chain(v.tensor_reduce(rmax[:], logits, AX.X, ALU.max))
                v.tensor_tensor(p, logits, rmax[:].unsqueeze(2).broadcast_to([P, TT, ne]), ALU.subtract).then_inc(r_shifted, 1)
                v.wait_ge(r_exped, r * R1 + 1)
                chain(v.tensor_reduce(rmax[:], p, AX.X, ALU.add))
                chain(v.reciprocal(rmax[:], rmax[:]))
                chain(v.tensor_tensor(p, p, rmax[:].unsqueeze(2).broadcast_to([P, TT, ne]), ALU.mult))
                for t in range(TT):
                    ins = v.max(mx8[:, t, :], pr[:, t, 0:ne])
                chain(ins)

            def router0():
                chain(v.tensor_copy(merge_f[:], merge_i[:]))
                chain(v.tensor_scalar(onehot[:], const("group")[0:E0, :], merge_f[:, 0:1], None, ALU.is_equal))
                softmax_rows(0, E0)
                for t in range(TT):
                    ins = v.match_replace(rep[:, t, :], mx8[:, t, :], pr[:, t, :], 0.0)
                chain(ins)
                chain(v.tensor_tensor(pr[:], pr[:], rep[:], ALU.subtract))
                chain(v.tensor_reduce(rmax[:], mx8[:], AX.X, ALU.add))
                chain(v.reciprocal(rmax[:], rmax[:]))
                v.tensor_tensor(pr[:], pr[:], rmax[:].unsqueeze(2).broadcast_to([P, TT, E0]), ALU.mult).then_inc(sel_ready, 1)
                v.wait_ge(sel_turned, 1)
                v.tensor_copy(selT[:], bank[6][0:E0, :]).then_inc(selT_ready, 1)
                v.wait_ge(w_summed, 1)
                v.tensor_copy(we[:, :, 0:G], bank[5][:, 0:TT * G].rearrange("p (t g) -> p t g", t=TT)).then_inc(we_ready, 1)
                v.wait_ge(we_ready, 1)

            def router1():
                chain(v.memset(pr[:, :, E1:E1 + 8], -1.0))
                chain(v.memset(pick[:], -1.0))
                softmax_rows(1, E1)
                chain(v.tensor_copy(pick[:, :, 0:2], mx8[:, :, 0:2]))
                for t in range(TT):
                    ins = v.match_replace(rep[:, t, 0:E1 + 8], pick[:, t, :], pr[:, t, 0:E1 + 8], 0.0)
                chain(ins)
                chain(v.tensor_tensor(we[:, :, 0:E1], pr[:, :, 0:E1], rep[:, :, 0:E1], ALU.subtract))
                chain(v.tensor_reduce(rmax[:], mx8[:, :, 0:2], AX.X, ALU.add))
                chain(v.tensor_scalar(rmax[:], rmax[:], 1e-9, None, ALU.add))
                chain(v.reciprocal(rmax[:], rmax[:]))
                chain(v.tensor_tensor(we[:, :, 0:E1], we[:, :, 0:E1], rmax[:].unsqueeze(2).broadcast_to([P, TT, E1]), ALU.mult))
                v.memset(we[:, :, E1:NX], 1.0).then_inc(we_ready, 1)
                v.wait_ge(we_ready, R1 + 1)

            def experts(n0, count, width, one_more):
                def hidden(k, n):
                    v.wait_ge(silu_ready, n + 1)
                    v.tensor_tensor(hid[k][0:width, :], hid[k][0:width, :], bank[2 * (k % 2) + 1][0:width, :], ALU.mult)\
                     .then_inc(hid_ready, 1)

                def add(k, n, e):
                    v.wait_ge(e_down, n + 1)
                    for t in range(TT):
                        ins = v.scalar_tensor_tensor(x[:, t, :], bank[4 + 2 * (k % 2) + t // 2][:, (t % 2) * D:(t % 2 + 1) * D],
                                                     we[:, t, bass.ds(e, 1)], x[:, t, :], ALU.mult, ALU.add)
                    ins.then_inc(e_added, 1)
                    v.wait_ge(e_added, n + 2)
                with v.Fori(0, count // NB) as i:
                    for k in range(0, NB, 2):
                        n = n0 + i * NB + k
                        hidden(k, n)
                        hidden(k + 1, n + 1)
                        add(k, n, i * NB + k)
                        add(k + 1, n + 1, i * NB + k + 1)
                if one_more:
                    hidden(0, n0 + count)
                    add(0, n0 + count, count)

            for free in (a_added, e_added, o1T_ready, acc1_copied):
                v.sem_inc(free, 1)
            v.memset(eps[:, 0:1], LN_EPS).then_inc(eps_ready, 1)
            v.memset(eps[:, 1:2], RMS_EPS).then_inc(eps_ready, 1)
            v.wait_ge(x_loaded, 16)
            v.wait_ge(consts_loaded, 16)
            if 1 in stages:
                layernorm(1)
                l0_xattn()
            if 2 in stages:
                layernorm(2)
                l0_attn()
            if 3 in stages:
                layernorm(3)
                v.wait_ge(router_loaded, 80)
                router0()
                experts(0, G, I0, False)
            if 4 in stages:
                layernorm(4)
                l1_xattn()
            if 5 in stages:
                layernorm(5)
                l1_attn()
            if 6 in stages:
                layernorm(6)
                v.wait_ge(router_loaded, 80)
                router1()
                experts(N1, E1, I1, True)
            v.sem_inc(dve_done, 1)



def layout(inputs):
    f = {k: np.asarray(v) for k, v in inputs.items()}

    def wide(w):
        return w.reshape(DC, P, -1).transpose(1, 0, 2)

    ctxT = np.zeros((B, D, S2P), np.float32)
    ctxT[:, :, :S2] = f["ctx_2048"].transpose(0, 2, 1)
    mask = np.zeros((B, S2P), bool)
    mask[:, :S2] = f["mask_BxS2_bk0"]
    kv1 = np.concatenate([f["L1_xattn_Wk"], f["L1_xattn_Wv"]], 0)
    r = {
        "x": f["x"],
        "const": CONST,
        "w0": np.stack([wide(f[f"L0_xattn_{n}"].T) for n in ("wq", "wg", "wk", "wv", "wo")], 1),
        "norm_w": f["L0_xattn_norm_w"].reshape(DC, P).T,
        "wa": np.concatenate([
            np.stack([f["L0_attn_W_K"], f["L0_attn_W_Q"]], 1).reshape(HA // 2, 2, 2, HDA, DC, P)
              .transpose(0, 5, 1, 2, 4, 3).reshape(HA // 2, P, -1),
            f["L0_attn_W_V"].reshape(HA // 2, 2 * HDA, DC, P).transpose(0, 3, 2, 1).reshape(HA // 2, P, -1),
            f["L0_attn_W_O"].reshape(D, HA // 2, 2, HDA).transpose(1, 3, 2, 0).reshape(HA // 2, P, -1)], 2),
        "w1": np.stack([wide(w.T) for w in (f["L1_xattn_Wq"], kv1[0::2], kv1[1::2])], 1),
        "wqkv": wide(f["L1_attn_w_attn"]),
        "wout": wide(f["L1_attn_w_out"]),
        "gu0": f["L0_ffn_gate_up_proj"].reshape(E0, 2, I0, DC, P).transpose(0, 4, 3, 1, 2),
        "dn0": f["L0_ffn_down_proj"].transpose(0, 2, 1),
        "wr0": wide(f["L0_ffn_gate_weight"].T),
        "merge": f["L0_ffn_merge_groups"].reshape(E0, 1),
        "dom": f["L0_ffn_dominant_experts"].reshape(1, G),
        "gu1": np.stack([np.concatenate([f["L1_ffn_W" + n], f["L1_ffn_sW" + n][None]], 0) for n in "gu"], 1)
                 .reshape(NX, 2, DC, P, I1).transpose(0, 3, 2, 1, 4),
        "dn1": np.concatenate([f["L1_ffn_Wd"], f["L1_ffn_sWd"][None]], 0),
        "wr1": wide(f["L1_ffn_Wr"].T),
        "bias1": f["L1_ffn_bias"].reshape(1, E1),
        "mask": mask.reshape(B * KT, P),
        "ctxT": ctxT.reshape(B, DC, P, KT, P).transpose(0, 3, 2, 1, 4).reshape(B * KT, P, DC, P),
    }
    return {k: np.ascontiguousarray(v) for k, v in r.items()}


def kernel(**inputs):
    import concourse.bacc as _bacc
    from concourse.bass_utils import run_bass_kernel_spmd as _run

    nc = _bacc.Bacc("TRN2", target_bir_lowering=False, num_devices=1)
    arrays = layout(inputs)
    aps = {k: nc.dram_tensor(f"in_{k}", v.shape, mybir.dt.from_np(v.dtype), kind="ExternalInput").ap()
           for k, v in arrays.items()}
    out = nc.dram_tensor("out_x", (B, S, D), F32, kind="ExternalOutput").ap()
    build(nc, aps, out)
    r = _run(nc, [{f"in_{k}": v for k, v in arrays.items()}], core_ids=[0])
    return r.results[0]["out_x"]
```

```python
from contextlib import ExitStack

import concourse.bass as bass
import numpy as np
from concourse import mybir

ALU = mybir.AluOpType
ACT = mybir.ActivationFunctionType
AX = mybir.AxisListType
F32 = mybir.dt.float32
U8 = mybir.dt.uint8
BF16 = mybir.dt.bfloat16
F16 = mybir.dt.float16
I32 = mybir.dt.int32

P = 128
B, S, D = 8, 64, 256
T = B * S
TT = T // P
DC = D // P
S2 = 1601
KT = -(-S2 // P)
S2P = KT * P
NT = B * KT
PLAN = NT + 2
H0, HD0 = 16, 16
G0 = H0 // 2
HA, HDA = 16, 128
E0, G, I0 = 32, 8, 96
H1, HD1 = 32, 8
G1 = H1 // 2
QR = P // 4
QG, QH = D // QR, QR // HD1
HB, HDB = 16, 16
QKV = (HB + 2) * HDB
E1, I1 = 16, 128
NX = E1 + 1
NCH = 4
CHUNK = [KT * j // NCH + (KT * j % NCH > 0) for j in range(NCH + 1)]
NEG = -1e30
LN_EPS, RMS_EPS = 1e-5, 1e-6



def constants():
    p = np.arange(P)[:, None]
    f = np.arange(P)[None, :]
    same = p // S == f // S
    pos = (np.arange(P) % S).astype(np.float32)
    freq = (np.float32(10000.0) ** ((-2.0 * np.arange(0, HDB, 2, dtype=np.float32) - 1.0) / HDB)).astype(np.float32)
    ang = pos[:, None] * freq[None, :]
    ang = np.concatenate([ang, ang], 1).astype(np.float32)
    sin = np.sin(ang)
    sin[:, :HDB // 2] *= -1
    parts = {
        "ident": (p == f),
        "head16": (p // HD0 == np.arange(P // HD0)[None, :]),
        "head8q": (p % QR // HD1 == np.arange(QR // HD1)[None, :]),
        "mean8": (p // HD1 == f // HD1) / HD1,
        "fold": (p % S == np.arange(S)[None, :]),
        "own16": (np.arange(2 * HD0)[None, :] // HD0 == p // S),
        "own8": (np.arange(2 * HD1)[None, :] // HD1 == p // S),
        "causal": np.where(same & (f <= p), 0.0, -1e10),
        "block": np.where(same, 0.0, NEG),
        "cos": np.cos(ang),
        "sin": sin,
        "before": (p < f),
        "count": np.arange(PLAN)[None, :] * np.ones((P, 1)),
        "tile": np.concatenate([p, p // KT], 1),
        "group": np.ones((P, 1)) * np.arange(G)[None, :],
    }
    at, cols, n = {}, [], 0
    for k, v in parts.items():
        v = np.asarray(v, np.float32).reshape(P, -1)
        at[k] = (n, n + v.shape[1])
        n += v.shape[1]
        cols.append(v)
    return np.ascontiguousarray(np.concatenate(cols, 1)), at


CONST, CONST_AT = constants()


class Chain:

    def __init__(self, eng, sem):
        self.eng, self.sem, self.n, self.loops = eng, sem, 0, []

    def value(self):
        v = self.n
        for var, per in self.loops:
            v = v + var * per
        return v

    def __call__(self, ins):
        ins.then_inc(self.sem, 1)
        self.n += 1
        self.eng.wait_ge(self.sem, self.value())

    def enter(self, var, per):
        self.loops.append((var, per))
        return self.n

    def leave(self, began, count):
        _, per = self.loops.pop()
        assert self.n - began == per, (self.n - began, per)
        self.n = began + per * count


def build(nc, a, out, stages=(1, 2, 3, 4, 5, 6)):
    with ExitStack() as ctx:
        def sb(name, shape, dt=F32):
            return ctx.enter_context(nc.sbuf_tensor(name, shape, dt))

        def sem(name):
            return ctx.enter_context(nc.semaphore(name))

        pair = [ctx.enter_context(nc.psum_tensor(f"banks{2 * i}", [P, 1024], F32)) for i in range(4)]
        bank = [pair[i // 2][:, i % 2 * 512:(i % 2 + 1) * 512] for i in range(8)]

        cst = sb("cst", [P, CONST.shape[1]])

        def const(name):
            lo, hi = CONST_AT[name]
            return cst[:, lo:hi]

        ident = const("ident")
        x = sb("x_sb", [P, TT, D])
        xn = sb("xn", [P, TT, D])
        xnT = sb("xnT", [P, DC, T])
        stats = sb("stats", [P, TT, 6])
        mv = sb("mv", [P, TT, 2])
        lnv = sb("lnv", [P, TT])
        rstd = sb("rstd", [P, TT])
        ms = sb("ms", [P, TT])
        eps = sb("eps", [P, 2])
        w0 = sb("w0", [P, 5, DC, D])
        w1 = sb("w1", [P, 3, DC, D])
        normw = sb("normw", [P, DC])

        consts_loaded = sem("consts_loaded")
        x_loaded = sem("x_loaded")
        w0_loaded = sem("w0_loaded")
        eps_ready = sem("eps_ready")
        var_ready = sem("var_ready")
        rstd_ready = sem("rstd_ready")
        sumsq_ready = sem("sumsq_ready")
        rrms_ready = sem("rrms_ready")
        xn_ready = sem("xn_ready")
        xn_turned = sem("xn_turned")
        xnT_act = sem("xnT_act")
        xnT_dve = sem("xnT_dve")
        act_chain = sem("act_chain")
        dve_chain = sem("dve_chain")

        scratch = sb("scratch", [P, TT, D])
        gate = sb("gate", [P, TT, D])
        q0T = sb("q0T", [P, DC, T])
        q0bd = sb("q0bd", [P, DC, 8, S])
        ctx_tile = sb("ctx_tile", [P, DC, P])
        mask_tiles = sb("mask_tiles", [B * KT, P], U8)
        tile_any = sb("tile_any", [P, 1])
        tile_at = sb("tile_at", [P, 1])
        tile_hot = sb("tile_hot", [P, PLAN])
        plan = sb("plan", [1, 2 * PLAN + 1], I32)
        tile_bias = sb("tile_bias", [1, P], BF16)
        ones_row = sb("ones_row", [1, P], BF16)
        bias_tiles = sb("bias_tiles", [NT, P], BF16)
        k0T = sb("k0T", [P, DC, P])
        v0 = sb("v0", [P, G0, 2 * HD0 + 1])
        probs0 = sb("probs0", [P, G0, P])
        probs0T = sb("probs0T", [P, G0, P])
        m_run = sb("m_run", [P, B, G0])
        m_new = sb("m_new", [P, G0])
        m_tile = sb("m_tile", [P, G0])
        m_step = sb("m_step", [P, G0])
        alpha = sb("alpha", [P, G0])
        o_run = sb("o_run", [P, B, G0, 2 * HD0 + 1])
        l_inv = sb("l_inv", [P, B, G0])
        o0T = sb("o0T", [P, DC, T])

        q0_projected = sem("q0_projected")
        gate_projected = sem("gate_projected")
        gate_exp = sem("gate_exp")
        o_scaled = sem("o_scaled")
        q0T_ready = sem("q0T_ready")
        ones_ready = sem("ones_ready")
        mask_loaded = sem("mask_loaded")
        bias_tiles_ready = sem("bias_tiles_ready")
        bias_row_loaded = sem("bias_row_loaded")
        any_ready = sem("any_ready")
        any_turned = sem("any_turned")
        tile_at_ready = sem("tile_at_ready")
        tile_hot_ready = sem("tile_hot_ready")
        plan_turned = sem("plan_turned")
        plan_ready = sem("plan_ready")
        tile_chain = sem("tile_chain")
        ctx_loaded = sem("ctx_loaded")
        bias_ready = sem("bias_ready")
        kv_projected = sem("kv_projected")
        k0_ready = sem("k0_ready")
        v0_ready = sem("v0_ready")
        q0bd_ready = sem("q0bd_ready")
        scored = sem("scored")
        shifted = sem("shifted")
        exped = sem("exped")
        alpha_ready = sem("alpha_ready")
        turned = sem("turned")
        pT_act = sem("pT_act")
        pT_dve = sem("pT_dve")
        attended = sem("attended")
        o_norm_ready = sem("o_norm_ready")
        o_folded = sem("o_folded")
        o0T_ready = sem("o0T_ready")
        out0_projected = sem("out0_projected")

        wa = [sb(f"wa{k}", [P, 8 * D]) for k in range(2)]
        kaT = sb("kaT", [P, 2, T])
        qaT = sb("qaT", [P, 2, T])
        va = sb("va", [P, TT, 2 * HDA])
        pa = sb("pa", [P, 2, TT, P])
        paT = sb("paT", [P, 2, TT, P])
        zaT = sb("zaT", [P, 2, T])
        maxa = sb("maxa", [P, 2, TT])
        suma = sb("suma", [P, 2, TT])
        wa_loaded = [sem(f"wa_loaded{k}") for k in range(2)]
        kqa_projected = sem("kqa_projected")
        va_projected = sem("va_projected")
        ka_ready = sem("ka_ready")
        qa_ready = sem("qa_ready")
        va_ready = sem("va_ready")
        a_scored = sem("a_scored")
        a_maxed = sem("a_maxed")
        a_exped = sem("a_exped")
        a_normed = sem("a_normed")
        a_summed = sem("a_summed")
        a_turned = sem("a_turned")
        paT_ready = sem("paT_ready")
        a_mixed = sem("a_mixed")
        zaT_ready = sem("zaT_ready")
        a_out = sem("a_out")
        a_added = sem("a_added")

        CTXC, V1 = 4 * DC * P, 2 * 4 * G1 * 4 * HD1
        big = sb("big", [P, 2 * CTXC + V1 + DC * T])
        ctxc = [big[:, k * CTXC:(k + 1) * CTXC].rearrange("p (t c k) -> p t c k", t=4, c=DC) for k in range(2)]
        v1 = big[:, 2 * CTXC:2 * CTXC + V1].rearrange("p (u t g j) -> p u t g j", u=2, t=4, g=G1)
        o_norm = v1.rearrange("p u t g j -> p (u t g j)")[:, 0:B * D].rearrange("p (b g j) -> p b g j", b=B, g=G0)
        bias_row = big[:].bitcast(BF16)[0:1, 0:NT * P]
        q1T = big[:, 2 * CTXC + V1:].rearrange("p (c q) -> p c q", c=DC)
        q1s = sb("q1s", [P, QG, T], F16)
        q1bd = sb("q1bd", [P, 2, QG, QH, S], F16)
        k1s = [sb(f"k1s{k}", [P, QG, 4 * P], F16) for k in range(2)]
        parts = pa[:].rearrange("p u t k -> p (u t k)").bitcast(F16).rearrange("p (h m k) -> p h m k", h=2, m=DC)
        q1parts = probs0[:].rearrange("p g k -> p (g k)").bitcast(F16).rearrange("p (h m k) -> p h m k", h=2, m=DC)
        q1sq = va[:].rearrange("p t f -> p (t f)").rearrange("p (m q) -> p m q", m=DC)
        q1r = zaT
        p1 = [[wa[k][:, m * 1024:(m + 1) * 1024] for m in range(DC)] for k in range(2)]
        p1.append([q[:].rearrange("p g k -> p (g k)") for q in (probs0, probs0T)])
        k1f = paT[:].rearrange("p u t k -> p u (t k)")
        sq1, r1 = kaT, qaT
        acc1 = zaT[:, 0, :]
        rden1 = sb("rden1", [P, G1])
        on1 = sb("on1", [P, G1, 2 * HD1])
        o1T = sb("o1T", [P, DC, T])
        w1_loaded = sem("w1_loaded")
        ctxc_loaded = [sem(f"ctxc_loaded{k}") for k in range(2)]
        q1_projected = sem("q1_projected")
        q1_squared = sem("q1_squared")
        q1_copied = sem("q1_copied")
        q1_meaned = sem("q1_meaned")
        q1_r = sem("q1_r")
        q1bd_ready = sem("q1bd_ready")
        q1_split = sem("q1_split")
        k1_projected = sem("k1_projected")
        k1_copied = sem("k1_copied")
        k1_squared = sem("k1_squared")
        k1_meaned = sem("k1_meaned")
        r1_ready = sem("r1_ready")
        k1_normed = sem("k1_normed")
        k1_high = sem("k1_high")
        k1_split = sem("k1_split")
        k1_stacked = sem("k1_stacked")
        k1_stacked_act = sem("k1_stacked_act")
        v1_projected = sem("v1_projected")
        s1_scored = sem("s1_scored")
        p1_ready = sem("p1_ready")
        p1_used = sem("p1_used")
        acc1_copied = sem("acc1_copied")
        acc1_turned = sem("acc1_turned")
        on1_ready = sem("on1_ready")
        o1_folded = sem("o1_folded")
        o1T_ready = sem("o1T_ready")
        o1_turned = sem("o1_turned")
        r1_ln = sem("r1_ln")
        v1_copied = sem("v1_copied")
        q1bd_pool = sem("q1bd_pool")
        q1_high = sem("q1_high")
        q1_stacked = sem("q1_stacked")
        q1_stacked_act = sem("q1_stacked_act")
        v1_ones = sem("v1_ones")
        q1s_loaded = sem("q1s_loaded")
        k1s_loaded = sem("k1s_loaded")

        def spread_queries(eng, b, groups):
            for g in groups:
                ins = eng.tensor_tensor(q1bd[:, bass.ds(b % 2, 1), g, :, :].rearrange("p o h q -> p (o h) q"),
                                        const("head8q").unsqueeze(2).broadcast_to([P, QH, S]),
                                        q1s[:, g, bass.ds(b % B * S, S)].unsqueeze(1).broadcast_to([P, QH, S]), ALU.mult)
            return ins

        def piece(to, i, q, w):
            return to[i * QR:(i + 1) * QR, :, 0:w].rearrange("r (m q) k -> r m q k", m=DC)[:, :, q, :]

        def part_rows(of, part, q, w):
            return of[q * QR:(q + 1) * QR, part, :, 0:w]

        def p1_half(t, m):
            return p1[2 if t == KT - 1 else t % 2][m]

        def after(b, j, n):
            return (b, j + n) if j + n < NCH else (b + 1, j + n - NCH)

        wqkv = sb("wqkv", [P, DC, QKV])
        wout = sb("wout", [P, DC, D])
        NR = HB + 1
        flat = v1.rearrange("p u t g j -> p (u t g j)")
        rot, rot2 = (flat[:, k * TT * NR * HDB:(k + 1) * TT * NR * HDB].rearrange("p (t h d) -> p t h d", t=TT, h=NR)
                     for k in range(2))
        krep = sb("krep", [P, TT, 8, HDB])
        vb = sb("vb", [P, TT, HDB])
        qbT, kbd, ob, obT = q0T, [probs0, probs0T], scratch, o0T
        NJ = 4 * TT
        maxb = sb("maxb", [P, NJ, 4])
        sumb = sb("sumb", [P, NJ, 4])
        ident_b = sb("ident_b", [P, P], BF16)
        block_b = sb("block_b", [P, P], BF16)
        causal_b = sb("causal_b", [P, P], BF16)
        masks_ready = sem("masks_ready")

        def score_bank(j):
            return bank[(6, 7, 5)[j % 3]]

        wb_loaded = sem("wb_loaded")
        qkv_projected = sem("qkv_projected")
        rotated = sem("rotated")
        qk_turned = sem("qk_turned")
        qbT_ready = sem("qbT_ready")
        kbd_ready = sem("kbd_ready")
        b_scored = sem("b_scored")
        b_maxed = sem("b_maxed")
        b_exped = sem("b_exped")
        b_turned = sem("b_turned")
        pbT_ready = sem("pbT_ready")
        b_mixed = sem("b_mixed")
        ob_ready = sem("ob_ready")
        ob_turned = sem("ob_turned")
        obT_ready = sem("obT_ready")
        b_out = sem("b_out")
        b_added = sem("b_added")
        b_summed = sem("b_summed")

        NB = 4
        wgu = [sb(f"wgu{k}", [P, DC, 2, P]) for k in range(NB)]
        wdn = [sb(f"wdn{k}", [P, D]) for k in range(NB)]
        hid = [kaT[:, 0, :], kaT[:, 1, :], qaT[:, 0, :], qaT[:, 1, :]]
        wr0 = sb("wr0", [P, DC, E0])
        wr1 = sb("wr1", [P, DC, E1])
        bias1 = sb("bias1", [P, E1])
        merge_i = sb("merge_i", [E0, 1], I32)
        merge_f = sb("merge_f", [E0, 1])
        onehot = sb("onehot", [E0, G])
        dom = sb("dom", [1, G], I32)
        pr = sb("pr", [P, TT, E0])
        rep = sb("rep", [P, TT, E0])
        mx8 = sb("mx8", [P, TT, 8])
        pick = sb("pick", [P, TT, 8])
        rmax = sb("rmax", [P, TT])
        selT = sb("selT", [E0, T])
        we = sb("we", [P, TT, NX])
        router_loaded = sem("router_loaded")
        we_loaded = [sem(f"we_loaded{k}") for k in range(NB)]
        r_scored = sem("r_scored")
        r_shifted = sem("r_shifted")
        r_exped = sem("r_exped")
        sel_ready = sem("sel_ready")
        sel_turned = sem("sel_turned")
        selT_ready = sem("selT_ready")
        w_summed = sem("w_summed")
        e_projected = sem("e_projected")
        silu_ready = sem("silu_ready")
        hid_ready = sem("hid_ready")
        e_down = sem("e_down")
        e_added = sem("e_added")
        we_ready = sem("we_ready")
        stored = sem("stored")
        dve_done = sem("dve_done")

        COUNT_AT = 2 * PLAN
        LN_AT = {st: k for k, st in enumerate(stages)}
        N1 = G if 3 in stages else 0
        R1 = 1 if 3 in stages else 0
        block = ctx.enter_context(nc.Block())
        xd = a["x"].rearrange("b s d -> (b s) d").rearrange("(t p) d -> p t d", p=P)
        od = out.rearrange("b s d -> (b s) d").rearrange("(t p) d -> p t d", p=P)

        @block.sync
        def _(sp):
            sp.dma_start(mask_tiles[:], a["mask"]).then_inc(mask_loaded, 16)
            sp.dma_start(x[:], xd).then_inc(x_loaded, 16)
            sp.dma_start(cst[:], a["const"]).then_inc(consts_loaded, 16)
            sp.dma_start(w0[:], a["w0"]).then_inc(w0_loaded, 16)
            sp.dma_start(normw[:], a["norm_w"]).then_inc(w0_loaded, 16)

            def l0_xattn():
                def load_ctx(i):
                    n = sp.value_load(plan[0:1, bass.ds(i, 1)], min_val=0, max_val=NT - 1)
                    sp.dma_start(ctx_tile[:], a["ctxT"][bass.ds(n, 1), :, :, :].rearrange("n p c k -> p (n c) k"))\
                      .then_inc(ctx_loaded, 16)

                sp.wait_ge(bias_tiles_ready, 1)
                sp.dma_start(bias_row.rearrange("p (n k) -> p n k", n=NT), bias_tiles[:]).then_inc(bias_row_loaded, 16)
                sp.wait_ge(plan_ready, 1)
                n_tiles = sp.value_load(plan[0:1, COUNT_AT:COUNT_AT + 1], min_val=1, max_val=NT)
                load_ctx(0)
                sp.wait_ge(kv_projected, 1)
                load_ctx(1)
                with sp.Fori(0, n_tiles) as i:
                    sp.wait_ge(kv_projected, i + 2)
                    load_ctx(i + 2)

            def l0_attn():
                def load(n, k):
                    sp.dma_start(wa[k][:], a["wa"][bass.ds(n, 1), :, :].rearrange("n p f -> p (n f)")).then_inc(wa_loaded[k], 16)
                for k in range(2):
                    load(k, k)
                with sp.Fori(0, HA // 4 - 1) as i:
                    for k in range(2):
                        n = i * 2 + k
                        sp.wait_ge(a_out, n + 1)
                        load(n + 2, k)

            def load_expert(gu, dn, width, index, k):
                sp.dma_start(wgu[k][:, :, :, 0:width], gu[bass.ds(index, 1), :, :, :, :].rearrange("n p c u i -> p (n c) u i"))\
                  .then_inc(we_loaded[k], 16)
                sp.dma_start(wdn[k][0:width, :], dn[bass.ds(index, 1), :, :].rearrange("n p f -> p (n f)"))\
                  .then_inc(we_loaded[k], 16)

            def l0_ffn():
                def load(n, k):
                    e = sp.value_load(dom[0:1, bass.ds(n, 1)], min_val=0, max_val=E0 - 1)
                    load_expert(a["gu0"], a["dn0"], I0, e, k)
                for k in range(NB):
                    load(k, k)
                with sp.Fori(0, G // NB - 1) as i:
                    for k in range(NB):
                        n = i * NB + k
                        sp.wait_ge(e_down, n + 1)
                        load(n + NB, k)

            def l1_xattn():
                sp.dma_start(w1[:], a["w1"]).then_inc(w1_loaded, 16)

                def load(first, n, k):
                    sp.dma_start(ctxc[k][:, 0:n, :, :].rearrange("p t c k -> p t (c k)"),
                                 a["ctxT"][bass.ds(first, n), :, :, :].rearrange("t p c k -> p t (c k)")).then_inc(ctxc_loaded[k], 16)

                def stack(to, of, i, part, rows, w, loaded):
                    for q in rows:
                        sp.dma_start(piece(to, i, q, w), part_rows(of, part, q, w)).then_inc(loaded, 16)

                def stack_k(b, j):
                    w = (CHUNK[j + 1] - CHUNK[j]) * P
                    sp.wait_ge(k1_high, b * NCH + j + 1)
                    stack(k1s[j % 2], parts, 2, 0, range(4), w, k1s_loaded)
                    sp.wait_ge(k1_split, b * NCH + j + 1)
                    stack(k1s[j % 2], parts, 3, 1, range(2), w, k1s_loaded)

                for j in range(2):
                    load(CHUNK[j], CHUNK[j + 1] - CHUNK[j], j)
                sp.wait_ge(q1_high, 1)
                stack(q1s, q1parts, 0, 0, range(4), T, q1s_loaded)
                stack_k(0, 0)
                with sp.Fori(0, B) as b:
                    for j in range(NCH):
                        jj = (j + 2) % NCH
                        bb = b if j + 2 < NCH else (b + 1) % B
                        sp.wait_ge(v1_projected, b * KT + CHUNK[j + 1])
                        load(bb * KT + CHUNK[jj], CHUNK[jj + 1] - CHUNK[jj], j % 2)
                        b1, j1 = after(b, j, 1)
                        stack_k(b1, j1)

            def l1_attn():
                sp.dma_start(wqkv[:], a["wqkv"]).then_inc(wb_loaded, 16)
                sp.dma_start(wout[:], a["wout"]).then_inc(wb_loaded, 16)

            def l1_ffn():
                for k in range(NB):
                    if N1:
                        sp.wait_ge(e_down, N1 - NB + k + 1)
                    load_expert(a["gu1"], a["dn1"], I1, k, k)
                with sp.Fori(0, E1 // NB - 1) as i:
                    for k in range(NB):
                        n = i * NB + k
                        sp.wait_ge(e_down, N1 + n + 1)
                        load_expert(a["gu1"], a["dn1"], I1, n + NB, k)
                sp.wait_ge(e_down, N1 + E1 - NB + 1)
                load_expert(a["gu1"], a["dn1"], I1, E1, 0)

            sp.dma_start(wr0[:], a["wr0"]).then_inc(router_loaded, 16)
            sp.dma_start(wr1[:], a["wr1"]).then_inc(router_loaded, 16)
            sp.dma_start(bias1[:], a["bias1"].broadcast_to([P, E1])).then_inc(router_loaded, 16)
            sp.dma_start(merge_i[:], a["merge"]).then_inc(router_loaded, 16)
            sp.dma_start(dom[:], a["dom"]).then_inc(router_loaded, 16)
            if 1 in stages:
                l0_xattn()
            if 2 in stages:
                l0_attn()
            if 3 in stages:
                sp.wait_ge(router_loaded, 80)
                l0_ffn()
            if 4 in stages:
                l1_xattn()
            if 5 in stages:
                l1_attn()
            if 6 in stages:
                l1_ffn()
            sp.wait_ge(dve_done, 1)
            sp.dma_start(od, x[:]).then_inc(stored, 16)
            sp.wait_ge(mask_loaded, 16)
            sp.wait_ge(router_loaded, 80)
            sp.wait_ge(w0_loaded, 32)
            sp.wait_ge(stored, 16)

        @block.tensor
        def _(pe):
            def layernorm(stage):
                s = LN_AT[stage]
                for i in range(TT):
                    pe.wait_ge(xn_ready, TT * s + i + 1)
                    for c in range(DC):
                        mm = pe.transpose(bank[c][:, i * P:(i + 1) * P], xn[:, i, c * P:(c + 1) * P], ident)
                mm.then_inc(xn_turned, 1)
                pe.wait_ge(xnT_act, s + 1)
                pe.wait_ge(xnT_dve, s + 1)

            def plan_tiles():
                pe.wait_ge(any_ready, 1)
                pe.matmul(bank[0][0:NT, 0:1], const("before")[0:NT, 0:NT], tile_any[0:NT, :], start=True, stop=True)\
                  .then_inc(any_turned, 1)
                pe.wait_ge(tile_hot_ready, 1)
                for k in range(2):
                    pe.matmul(bank[1][0:1, k * PLAN:(k + 1) * PLAN], const("tile")[0:NT, k:k + 1], tile_hot[0:NT, :],
                              start=True, stop=True)
                pe.matmul(bank[1][0:1, COUNT_AT:COUNT_AT + 1], tile_any[0:NT, :], tile_any[0:NT, :], start=True, stop=True)\
                  .then_inc(plan_turned, 1)

            def l0_xattn():
                pe.wait_ge(w0_loaded, 32)
                for m in range(DC):
                    for c in range(DC):
                        mm = pe.matmul(bank[2 + m], w0[:, 0, c, m * P:(m + 1) * P], xnT[:, c, :],
                                       start=(c == 0), stop=(c == DC - 1))
                mm.then_inc(q0_projected, 1)
                n_tiles = pe.value_load(plan[0:1, COUNT_AT:COUNT_AT + 1], min_val=1, max_val=NT)

                def project(i):
                    pe.wait_ge(ctx_loaded, 16 * (i + 1))
                    for m in range(DC):
                        for c in range(DC):
                            pe.matmul(bank[0][:, m * P:(m + 1) * P], w0[:, 2, c, m * P:(m + 1) * P],
                                      ctx_tile[:, c, :], start=(c == 0), stop=(c == DC - 1))
                    if not (isinstance(i, int) and i == 0):
                        pe.wait_ge(v0_ready, i)
                    for c in range(DC):
                        mm = pe.matmul(bank[1][:, 0:D], ctx_tile[:, c, :], w0[:, 3, c, :],
                                       start=(c == 0), stop=(c == DC - 1))
                    mm.then_inc(kv_projected, 1)

                def scores(i):
                    pe.wait_ge(q0bd_ready, i + 1)
                    pe.wait_ge(bias_ready, i + 1)
                    pe.wait_ge(k0_ready, i + 1)
                    for m in range(DC):
                        pe.matmul(bank[2 + m], ones_row[:], tile_bias[:].unsqueeze(1).broadcast_to([1, 4, P]),
                                  start=True, stop=False, skip_group_check=True)
                        for g in range(4):
                            mm = pe.matmul(bank[2 + m][:, g * P:(g + 1) * P],
                                           q0bd[:, m, 2 * g:2 * g + 2, :].rearrange("p h q -> p (h q)"),
                                           k0T[:, m, :], start=False, stop=True, skip_group_check=True)
                        mm.then_inc(scored, 1)

                pe.wait_ge(ones_ready, 1)
                project(0)
                pe.wait_ge(q0T_ready, 2)
                scores(0)
                project(1)
                with pe.Fori(0, n_tiles) as i:
                    for m in range(DC):
                        pe.wait_ge(exped, 2 * i + m + 1)
                        for g in range(4):
                            mm = pe.transpose(bank[4 + m][:, g * P:(g + 1) * P], probs0[:, 4 * m + g, :], ident)
                        mm.then_inc(turned, 1)
                    scores(i + 1)
                    pe.wait_ge(pT_act, i + 1)
                    pe.wait_ge(pT_dve, i + 1)
                    for g in range(G0):
                        w = 2 * HD0 + 1
                        mm = pe.matmul(bank[6][:, g * w:(g + 1) * w], probs0T[:, g, :], v0[:, g, :], start=True, stop=True)
                    mm.then_inc(attended, 1)
                    project(i + 2)
                for i in range(TT):
                    for c in range(DC):
                        mm = pe.matmul(bank[4 + i // 2][:, i % 2 * D:(i % 2 + 1) * D], xnT[:, c, i * P:(i + 1) * P], w0[:, 1, c, :],
                                       start=(c == 0), stop=(c == DC - 1))
                mm.then_inc(gate_projected, 1)
                for b in range(B):
                    if b % (B // 2) == 0:
                        pe.wait_ge(o_norm_ready, 2 * b // B + 1)
                    for c in range(DC):
                        mm = pe.matmul(bank[c][:, b * S:(b + 1) * S],
                                       o_norm[:, b, 4 * c:4 * c + 4, :].rearrange("p g j -> p (g j)"), const("fold"),
                                       start=True, stop=True)
                mm.then_inc(o_folded, 1)
                pe.wait_ge(gate_exp, 1)
                pe.wait_ge(o0T_ready, 2)
                for i in range(TT):
                    for c in range(DC):
                        mm = pe.matmul(bank[4 + i][:, 0:D], o0T[:, c, i * P:(i + 1) * P], w0[:, 4, c, :],
                                       start=(c == 0), stop=(c == DC - 1))
                mm.then_inc(out0_projected, 1)

            def l0_attn():
                pe.wait_ge(masks_ready, 1)
                with pe.Fori(0, HA // 4) as i:
                    for k in range(2):
                        n = i * 2 + k
                        w = wa[k]
                        pe.wait_ge(wa_loaded[k], 16 * (i + 1))
                        for u in range(2):
                            for j in range(2):
                                for c in range(DC):
                                    o = ((u * 2 + j) * DC + c) * HDA
                                    mm = pe.matmul(bank[3 * u + j], w[:, o:o + HDA], xnT[:, c, :],
                                                   start=(c == 0), stop=(c == DC - 1))
                            mm.then_inc(kqa_projected, 1)
                        pe.wait_ge(a_added, n + 1)
                        for u in range(2):
                            pe.wait_ge(ka_ready, 2 * n + u + 1)
                            pe.wait_ge(qa_ready, 2 * n + u + 1)
                            pe.matmul(bank[6 + u], ident_b[:], causal_b[:].unsqueeze(1).broadcast_to([P, TT, P]),
                                      start=True, stop=False, skip_group_check=True)
                            for t in range(TT):
                                mm = pe.matmul(bank[6 + u][:, t * P:(t + 1) * P], qaT[:, u, t * P:(t + 1) * P],
                                               kaT[:, u, t * P:(t + 1) * P], start=False, stop=True, skip_group_check=True)
                            mm.then_inc(a_scored, 1)
                        for u in range(2):
                            for t in (2 * u, 2 * u + 1):
                                for c in range(DC):
                                    o = 4 * D + c * D
                                    mm = pe.matmul(bank[2 + 3 * u][:, (t % 2) * D:(t % 2 + 1) * D],
                                                   xnT[:, c, t * P:(t + 1) * P], w[:, o:o + D], start=(c == 0), stop=(c == DC - 1))
                            mm.then_inc(va_projected, 1)
                        for u in range(2):
                            pe.wait_ge(a_normed, 2 * n + u + 1)
                            for t in range(TT):
                                mm = pe.transpose(bank[3 * u][:, t * P:(t + 1) * P], pa[:, u, t, :], ident)
                            mm.then_inc(a_turned, 1)
                        pe.wait_ge(va_ready, 2 * n + 2)
                        for u in range(2):
                            pe.wait_ge(paT_ready, 2 * n + u + 1)
                            for t in range(TT):
                                mm = pe.matmul(bank[1 + 3 * u][:, t * P:(t + 1) * P], va[:, t, u * HDA:(u + 1) * HDA],
                                               paT[:, u, t, :], start=True, stop=True)
                            mm.then_inc(a_mixed, 1)
                        for u in range(2):
                            pe.wait_ge(zaT_ready, 2 * n + u + 1)
                            for t in range(TT):
                                o = 6 * D + u * D
                                mm = pe.matmul(bank[2 + 3 * (t // 2)][:, (t % 2) * D:(t % 2 + 1) * D],
                                               zaT[:, u, t * P:(t + 1) * P], w[:, o:o + D], start=(u == 0 and t % 2 == 0), stop=(u == 1),
                                               skip_group_check=True)
                        mm.then_inc(a_out, 1)

            def router(r, w, ne):
                for t in range(TT):
                    for c in range(DC):
                        mm = pe.matmul(bank[7][:, t * ne:(t + 1) * ne], xnT[:, c, t * P:(t + 1) * P], w[:, c, :],
                                       start=(c == 0), stop=(c == DC - 1))
                mm.then_inc(r_scored, 1)

            def up(k, n, width, loaded):
                pe.wait_ge(we_loaded[k], loaded)
                for j in range(2):
                    for c in range(DC):
                        mm = pe.matmul(bank[2 * (k % 2) + j][0:width, :], wgu[k][:, c, j, 0:width], xnT[:, c, :],
                                       start=(c == 0), stop=(c == DC - 1))
                mm.then_inc(e_projected, 1)

            def down(k, n, width):
                pe.wait_ge(hid_ready, n + 1)
                for t in range(TT):
                    mm = pe.matmul(bank[4 + 2 * (k % 2) + t // 2][:, (t % 2) * D:(t % 2 + 1) * D],
                                   hid[k][0:width, t * P:(t + 1) * P], wdn[k][0:width, :], start=True, stop=True)
                mm.then_inc(e_down, 1)

            def experts(n0, first, count, width, one_more, weigh):
                def group(i, between=None):
                    for k in range(0, NB, 2):
                        n = n0 + i * NB + k
                        up(k, n, width, 32 * (first + i + 1))
                        up(k + 1, n + 1, width, 32 * (first + i + 1))
                        if between:
                            between()
                            between = None
                        pe.wait_ge(e_added, n + 1)
                        down(k, n, width)
                        down(k + 1, n + 1, width)

                group(0, weigh)
                with pe.Fori(1, count // NB) as i:
                    group(i)
                if one_more:
                    n = n0 + count
                    up(0, n, width, 32 * (first + count // NB + 1))
                    pe.wait_ge(e_added, n + 1)
                    down(0, n, width)

            def l0_ffn():
                pe.wait_ge(router_loaded, 80)
                router(0, wr0, E0)

                def weigh():
                    pe.wait_ge(sel_ready, 1)
                    for t in range(TT):
                        mm = pe.transpose(bank[6][0:E0, t * P:(t + 1) * P], pr[:, t, :], ident)
                    mm.then_inc(sel_turned, 1)
                    pe.wait_ge(selT_ready, 1)
                    for t in range(TT):
                        mm = pe.matmul(bank[5][:, t * G:(t + 1) * G], selT[:, t * P:(t + 1) * P], onehot[:], start=True, stop=True)
                    mm.then_inc(w_summed, 1)
                    pe.wait_ge(we_ready, 1)

                experts(0, 0, G, I0, False, weigh)

            def l1_ffn():
                pe.wait_ge(router_loaded, 80)
                router(1, wr1, E1)
                experts(N1, N1 // NB, E1, I1, True, lambda: pe.wait_ge(we_ready, R1 + 1))

            def l1_xattn():
                pe.wait_ge(w1_loaded, 16)
                for m in range(DC):
                    for c in range(DC):
                        mm = pe.matmul(bank[4 + m], w1[:, 0, c, m * P:(m + 1) * P], xnT[:, c, :],
                                       start=(c == 0), stop=(c == DC - 1))
                mm.then_inc(q1_projected, 1)

                def project_keys(b, j):
                    k, w = j % 2, CHUNK[j + 1] - CHUNK[j]
                    pe.wait_ge(ctxc_loaded[k], 16 * (b * (NCH // 2) + j // 2 + 1))
                    for m in range(DC):
                        for c in range(DC):
                            mm = pe.matmul(bank[m][:, 0:w * P], w1[:, 1, c, m * P:(m + 1) * P], ctxc[k][:, 0:w, c, :],
                                           start=(c == 0), stop=(c == DC - 1))
                    mm.then_inc(k1_projected, 1)

                def mean_squares(b, j):
                    w = CHUNK[j + 1] - CHUNK[j]
                    pe.wait_ge(k1_squared, b * NCH + j + 1)
                    for m in range(DC):
                        mm = pe.matmul(bank[m][:, 0:w * P], const("mean8"), sq1[:, m, 0:w * P], start=True, stop=True)
                    mm.then_inc(k1_meaned, 1)

                def project_values(b, j, t):
                    if not (isinstance(b, int) and b * KT + t == 0):
                        pe.wait_ge(v1_copied, b * KT + t)
                    for c in range(DC):
                        mm = pe.matmul(bank[2][:, 0:D], ctxc[j % 2][:, t - CHUNK[j], c, :], w1[:, 2, c, :],
                                       start=(c == 0), stop=(c == DC - 1))
                    mm.then_inc(v1_projected, 1)

                def scores(b, j, t):
                    keys, o = min(P, S2 - t * P), (t - CHUNK[j]) * P
                    if t == CHUNK[j]:
                        pe.wait_ge(k1s_loaded, 6 * 16 * (b * NCH + j + 1))
                        pe.wait_ge(k1_stacked_act, b * NCH + j + 1)
                        pe.wait_ge(k1_stacked, b * NCH + j + 1)
                    if t == 0:
                        pe.wait_ge(q1bd_ready, b + 1)
                        pe.wait_ge(q1bd_pool, b + 1)
                    for m in range(DC):
                        if not (isinstance(b, int) and b * KT + t == 0):
                            pe.wait_ge(p1_ready, b * 2 * KT + 2 * t + m - 1)
                        for q in range(QG // 2):
                            g = m * QG // 2 + q
                            w = QH * S
                            mm = pe.matmul(bank[4 + g // 2][0:keys, g % 2 * w:(g % 2 + 1) * w], k1s[j % 2][:, g, o:o + keys],
                                           q1bd[:, bass.ds(b % 2, 1), g, :, :].rearrange("p o h q -> p (o h q)"),
                                           start=True, stop=True)
                        mm.then_inc(s1_scored, 1)

                def mix(b, j, t):
                    keys = min(P, S2 - t * P)
                    pe.wait_ge(v1_copied, b * KT + t + 1)
                    pe.wait_ge(p1_ready, b * 2 * KT + 2 * t + 2)
                    if t == 0:
                        pe.wait_ge(o1T_ready, b + 1)
                    for g in range(G1):
                        q, s = g % 4, g // 4
                        mm = pe.matmul(bank[3][32 * q:32 * q + 32, s * P:(s + 1) * P], v1[0:keys, j % 2, t - CHUNK[j], g, :],
                                       p1_half(t, g // 8)[0:keys, g % 8 * P:(g % 8 + 1) * P], start=(t == 0 and s == 0),
                                       stop=(t == KT - 1), skip_group_check=True)
                    mm.then_inc(p1_used, 1)

                project_keys(0, 0)
                pe.wait_ge(q1_squared, 1)
                for m in range(DC):
                    mm = pe.matmul(bank[6 + m], const("mean8"), q1sq[:, m, :], start=True, stop=True)
                mm.then_inc(q1_meaned, 1)
                project_values(0, 0, 0)
                mean_squares(0, 0)
                project_values(0, 0, 1)
                pe.wait_ge(r1_ready, 1)
                project_keys(0, 1)
                for t in range(2, CHUNK[1]):
                    project_values(0, 0, t)
                mean_squares(0, 1)
                pe.wait_ge(v1_ones, 1)
                scores(0, 0, 0)
                with pe.Fori(0, B) as b:
                    for j in range(NCH):
                        b1, j1 = after(b, j, 1)
                        b2, j2 = after(b, j, 2)
                        values = list(range(CHUNK[j1], CHUNK[j1 + 1]))
                        for t in range(CHUNK[j], CHUNK[j + 1]):
                            if t + 1 < KT:
                                scores(b, j if t + 1 < CHUNK[j + 1] else j + 1, t + 1)
                            if t == CHUNK[j] + 1:
                                pe.wait_ge(r1_ready, b1 * NCH + j1 + 1)
                                project_keys(b2, j2)
                            if values:
                                project_values(b1, j1, values.pop(0))
                            mix(b, j, t)
                        mean_squares(b2, j2)
                    scores(b + 1, 0, 0)
                    pe.wait_ge(acc1_copied, b + 1)
                    for s in range(4):
                        mm = pe.transpose(bank[3][:, s * P:(s + 1) * P], acc1[:, s * P:(s + 1) * P], ident)
                    mm.then_inc(acc1_turned, 1)
                    project_values(b1, j1, values.pop(0))
                    assert not values
                    pe.wait_ge(on1_ready, b + 1)
                    for c in range(DC):
                        mm = pe.matmul(bank[3][:, c * S:(c + 1) * S],
                                       on1[:, 8 * c:8 * c + 8, :].rearrange("p g j -> p (g j)"), const("fold"),
                                       start=True, stop=True)
                    mm.then_inc(o1_folded, 1)
                pe.wait_ge(r1_ready, B * NCH + 2)
                pe.wait_ge(o1T_ready, B + 1)
                pe.wait_ge(v1_copied, B * KT + CHUNK[1])
                for c in range(DC):
                    for i in range(TT):
                        mm = pe.transpose(bank[i][:, c * P:(c + 1) * P], o1T[:, c, i * P:(i + 1) * P], ident)
                mm.then_inc(o1_turned, 1)

            def l1_attn():
                pe.wait_ge(wb_loaded, 32)
                def turn_qk(t):
                    if t >= 1:
                        pe.wait_ge(qbT_ready, t)
                        pe.wait_ge(kbd_ready, t)
                    qk = rot[:, t, 0:HB, :].rearrange("p h d -> p (h d)")
                    for m in range(DC):
                        pe.transpose(bank[0][:, m * P:(m + 1) * P], qk[:, m * P:(m + 1) * P], ident)
                    pe.transpose(bank[0][:, 2 * P:3 * P], krep[:, t, :, :].rearrange("p h d -> p (h d)"), ident)\
                      .then_inc(qk_turned, 1)

                def scores(j):
                    t, m, h = j // 4, j // 2 % 2, j % 2
                    if j % 4 == 0:
                        pe.wait_ge(qbT_ready, t + 1)
                        pe.wait_ge(kbd_ready, t + 1)
                    if j >= 3:
                        pe.wait_ge(b_exped, j - 2)
                    pe.matmul(score_bank(j), ident_b[:], block_b[:].unsqueeze(1).broadcast_to([P, 4, P]),
                              start=True, stop=False, skip_group_check=True)
                    pe.matmul(score_bank(j), qbT[:, m, t * P:(t + 1) * P],
                              kbd[t % 2][:, 4 * h:4 * h + 4, :].rearrange("p h k -> p (h k)"), start=False, stop=True,
                              skip_group_check=True).then_inc(b_scored, 1)

                def turn(j):
                    pe.wait_ge(b_exped, j + 1)
                    if j >= 2:
                        pe.wait_ge(pbT_ready, j - 1)
                    for h in range(4):
                        mm = pe.transpose(bank[1 + 2 * (j % 2)][:, h * P:(h + 1) * P], pa[:, j % 2, h, :], ident)
                    mm.then_inc(b_turned, 1)

                def mix(j):
                    t = j // 4
                    pe.wait_ge(pbT_ready, j + 1)
                    if j >= 4 and j % 4 == 0:
                        pe.wait_ge(ob_ready, t)
                    for h in range(4):
                        k = (j % 4 * 4 + h) * HDB
                        mm = pe.matmul(bank[2][:, k:k + HDB], paT[:, j % 2, h, :], vb[:, t, :], start=True, stop=True)
                    mm.then_inc(b_mixed, 1)

                def turn_out(t):
                    pe.wait_ge(ob_ready, t + 1)
                    if t >= 1:
                        pe.wait_ge(b_added, t)
                    for c in range(DC):
                        mm = pe.transpose(bank[4][:, c * P:(c + 1) * P], ob[:, t, c * P:(c + 1) * P], ident)
                    mm.then_inc(ob_turned, 1)

                def project(t):
                    pe.wait_ge(obT_ready, t + 1)
                    for c in range(DC):
                        mm = pe.matmul(bank[4][:, D:2 * D], obT[:, c, t * P:(t + 1) * P], wout[:, c, :],
                                       start=(c == 0), stop=(c == DC - 1))
                    mm.then_inc(b_out, 1)

                for t in range(TT):
                    for c in range(DC):
                        mm = pe.matmul(bank[2 + t][:, 0:QKV], xnT[:, c, t * P:(t + 1) * P], wqkv[:, c, :],
                                       start=(c == 0), stop=(c == DC - 1))
                    mm.then_inc(qkv_projected, 1)
                    if t == 2:
                        pe.wait_ge(rotated, 1)
                        turn_qk(0)
                pe.wait_ge(masks_ready, 1)
                scores(0)
                scores(1)
                pe.wait_ge(rotated, TT)
                for j in range(NJ + 3):
                    if j + 2 < NJ:
                        scores(j + 2)
                    if j % 4 == 0 and j // 4 + 1 < TT:
                        turn_qk(j // 4 + 1)
                    if j < NJ:
                        turn(j)
                    if 1 <= j <= NJ:
                        mix(j - 1)
                    if j >= 5 and j % 4 == 1:
                        turn_out(j // 4 - 1)
                    if j >= 6 and j % 4 == 2:
                        project(j // 4 - 1)

            pe.wait_ge(consts_loaded, 16)
            if 1 in stages:
                plan_tiles()
                layernorm(1)
                l0_xattn()
            if 2 in stages:
                layernorm(2)
                l0_attn()
            if 3 in stages:
                layernorm(3)
                l0_ffn()
            if 4 in stages:
                layernorm(4)
                l1_xattn()
            if 5 in stages:
                layernorm(5)
                l1_attn()
            if 6 in stages:
                layernorm(6)
                l1_ffn()

        @block.scalar
        def _(act):
            chain = Chain(act, act_chain)

            def rsqrt(dst, src, bias, scale=1.0):
                chain(act.activation(lnv[:], src, ACT.Ln, bias=bias, scale=scale))
                return act.activation(dst, lnv[:], ACT.Exp, scale=-0.5)

            def layernorm(stage):
                s = LN_AT[stage]
                act.wait_ge(var_ready, s + 1)
                rsqrt(rstd[:], mv[:, :, 1], eps[:, 0:1]).then_inc(rstd_ready, 1)
                if stage == 1:
                    act.wait_ge(sumsq_ready, 1)
                    rsqrt(rstd[:], ms[:], eps[:, 1:2], 1.0 / D).then_inc(rrms_ready, 1)
                act.wait_ge(xn_turned, s + 1)
                if stage == 1:
                    act.wait_ge(w0_loaded, 32)
                    act.activation(xnT[:, 0, :], bank[0], ACT.Copy, scale=normw[:, 0:1]).then_inc(xnT_act, 1)
                else:
                    act.activation(xnT[:, 0, :], bank[0], ACT.Copy).then_inc(xnT_act, 1)

            def l0_xattn():
                act.wait_ge(q0_projected, 1)
                for m in range(DC):
                    act.activation(q0T[:, m, :], bank[2 + m], ACT.Copy, scale=HD0 ** -0.5).then_inc(q0T_ready, 1)
                act.wait_ge(plan_ready, 1)
                n_tiles = act.value_load(plan[0:1, COUNT_AT:COUNT_AT + 1], min_val=1, max_val=NT)

                def copy_k(i):
                    act.wait_ge(kv_projected, i + 1)
                    act.activation(k0T[:].rearrange("p m k -> p (m k)"), bank[0][:, 0:D], ACT.Copy).then_inc(k0_ready, 1)

                def copy_v(i):
                    act.activation(v0[:, :, 0:2 * HD0], bank[1][:, 0:D].rearrange("p (g j) -> p g j", g=G0), ACT.Copy)\
                       .then_inc(v0_ready, 1)

                copy_k(0)
                copy_v(0)
                act.sem_inc(o_scaled, 1)
                with act.Fori(0, n_tiles) as i:
                    for m in range(DC):
                        act.wait_ge(shifted, 2 * i + m + 1)
                        act.activation(probs0[:, 4 * m:4 * m + 4, :], probs0[:, 4 * m:4 * m + 4, :], ACT.Exp).then_inc(exped, 1)
                    act.wait_ge(o_scaled, i + 1)
                    act.activation(alpha[:], m_step[:], ACT.Exp).then_inc(alpha_ready, 1)
                    copy_k(i + 1)
                    act.wait_ge(turned, 2 * i + 1)
                    act.activation(probs0T[:, 0:4, :].rearrange("p g k -> p (g k)"), bank[4], ACT.Copy).then_inc(pT_act, 1)
                    act.wait_ge(attended, i + 1)
                    copy_v(i + 1)
                act.wait_ge(gate_projected, 1)
                for i in range(2):
                    e = act.activation(gate[:, 2 * i:2 * i + 2, :].rearrange("p t f -> p (t f)"), bank[4 + i], ACT.Exp, scale=-1.0)
                e.then_inc(gate_exp, 1)
                act.wait_ge(o_folded, 1)
                for c in range(DC):
                    act.activation(o0T[:, c, :], bank[c], ACT.Copy).then_inc(o0T_ready, 1)

            def l0_attn():
                with act.Fori(0, HA // 4) as i:
                    for k in range(2):
                        n = i * 2 + k
                        for u in range(2):
                            act.wait_ge(kqa_projected, 2 * n + u + 1)
                            act.activation(kaT[:, u, :], bank[3 * u], ACT.Copy).then_inc(ka_ready, 1)
                        for u in range(2):
                            act.wait_ge(a_maxed, 2 * n + u + 1)
                            for t in range(TT):
                                e = act.activation(pa[:, u, t, :], bank[6 + u][:, t * P:(t + 1) * P], ACT.Exp, bias=maxa[:, u, t:t + 1],
                                                   scale=HDA ** -0.5, accum_out=suma[:, u, t:t + 1])
                            e.then_inc(a_exped, 1)
                        for u in range(2):
                            act.wait_ge(a_turned, 2 * n + u + 1)
                            act.activation(paT[:, u, :, :].rearrange("p t q -> p (t q)"), bank[3 * u], ACT.Copy).then_inc(paT_ready, 1)

            def router(r):
                act.wait_ge(r_shifted, r * R1 + 1)
                ne = (E0, E1)[r]
                act.activation(pr[:, :, 0:ne], pr[:, :, 0:ne], ACT.Exp).then_inc(r_exped, 1)

            def experts(n0, count, width, one_more):
                def silu(k, n):
                    act.wait_ge(e_projected, n + 1)
                    act.activation(hid[k][0:width, :], bank[2 * (k % 2)][0:width, :], ACT.Silu).then_inc(silu_ready, 1)
                with act.Fori(0, count // NB) as i:
                    for k in range(NB):
                        silu(k, n0 + i * NB + k)
                if one_more:
                    silu(0, n0 + count)

            def l1_xattn():
                def mean_rsqrt(to, first, w, n):
                    for m in range(DC):
                        act.activation(to[:, m, 0:w], bank[first + m][:, 0:w], ACT.Ln, bias=eps[:, 1:2]).then_inc(r1_ln, 1)
                    act.wait_ge(r1_ln, n)
                    return act.activation(to[:, :, 0:w], to[:, :, 0:w], ACT.Exp, scale=-0.5)

                def square(b, j):
                    w = (CHUNK[j + 1] - CHUNK[j]) * P
                    act.wait_ge(k1_copied, b * NCH + j + 1)
                    act.activation(sq1[:, :, 0:w], k1f[:, :, 0:w], ACT.Square).then_inc(k1_squared, 1)

                def norm(b, j):
                    act.wait_ge(k1_meaned, b * NCH + j + 1)
                    mean_rsqrt(r1, 0, (CHUNK[j + 1] - CHUNK[j]) * P, 2 * (b * NCH + j) + 4).then_inc(r1_ready, 1)

                def exp(b, t):
                    keys = min(P, S2 - t * P)
                    act.wait_ge(p1_used, b * KT + t + 1)
                    for m in range(DC):
                        act.wait_ge(s1_scored, b * 2 * KT + 2 * t + m + 1)
                        act.activation(p1_half(t, m)[0:keys, :], pair[2 + m][0:keys, :], ACT.Exp,
                                       scale=HD1 ** -0.5).then_inc(p1_ready, 1)

                def stack_k(b, j):
                    w = (CHUNK[j + 1] - CHUNK[j]) * P
                    act.wait_ge(k1_split, b * NCH + j + 1)
                    for q in range(2, 4):
                        e = act.activation(piece(k1s[j % 2], 3, q, w), part_rows(parts, 1, q, w), ACT.Copy)
                    e.then_inc(k1_stacked_act, 1)

                act.wait_ge(q1_projected, 1)
                for m in range(DC):
                    e = act.activation(q1sq[:, m, :], bank[4 + m], ACT.Square)
                e.then_inc(q1_squared, 1)
                square(0, 0)
                act.wait_ge(q1_meaned, 1)
                mean_rsqrt(q1r, 6, T, 2).then_inc(q1_r, 1)
                norm(0, 0)
                act.wait_ge(q1_split, 1)
                for q in range(4):
                    e = act.activation(piece(q1s, 3, q, T), part_rows(q1parts, 1, q, T), ACT.Copy)
                e.then_inc(q1_stacked_act, 1)
                square(0, 1)
                stack_k(0, 0)
                norm(0, 1)
                exp(0, 0)
                with act.Fori(0, B) as b:
                    for j in range(NCH):
                        b1, j1 = after(b, j, 1)
                        b2, j2 = after(b, j, 2)
                        for t in range(CHUNK[j], CHUNK[j + 1]):
                            if t + 1 < KT:
                                exp(b, t + 1)
                            if t == CHUNK[j] + 1:
                                stack_k(b1, j1)
                                square(b2, j2)
                        norm(b2, j2)
                    exp(b + 1, 0)

            def l1_attn():
                def copy_q(t):
                    act.wait_ge(qk_turned, t + 1)
                    act.activation(qbT[:, :, t * P:(t + 1) * P], bank[0][:, 0:D].rearrange("p (m q) -> p m q", m=DC), ACT.Copy)\
                       .then_inc(qbT_ready, 1)

                copy_q(0)
                for j in range(NJ):
                    act.wait_ge(b_maxed, j + 1)
                    if j >= 2:
                        act.wait_ge(b_turned, j - 1)
                    for h in range(4):
                        e = act.activation(pa[:, j % 2, h, :], score_bank(j)[:, h * P:(h + 1) * P], ACT.Exp,
                                           bias=maxb[:, j, h:h + 1], scale=HDB ** -0.5, accum_out=sumb[:, j, h:h + 1])
                    e.then_inc(b_exped, 1)
                    if j % 4 == 0 and j // 4 + 1 < TT:
                        copy_q(j // 4 + 1)

            act.sem_inc(p1_used, 2)
            act.preload_act_table_set("natural_log_exp_and_others")
            act.wait_ge(eps_ready, 2)
            if 1 in stages:
                layernorm(1)
                l0_xattn()
            if 2 in stages:
                layernorm(2)
                l0_attn()
            if 3 in stages:
                layernorm(3)
                router(0)
                experts(0, G, I0, False)
            if 4 in stages:
                act.preload_act_table_set("natural_log_exp_and_others")
                layernorm(4)
                l1_xattn()
            if 5 in stages:
                layernorm(5)
                l1_attn()
            if 6 in stages:
                layernorm(6)
                router(1)
                experts(N1, E1, I1, True)

        @block.gpsimd
        def _(pool):
            def l0_xattn():
                pool.wait_ge(consts_loaded, 16)
                pool.wait_ge(plan_ready, 1)
                n_tiles = pool.value_load(plan[0:1, COUNT_AT:COUNT_AT + 1], min_val=1, max_val=NT)

                def tile_of(i):
                    return (pool.value_load(plan[0:1, bass.ds(i, 1)], min_val=0, max_val=NT - 1),
                            pool.value_load(plan[0:1, bass.ds(i + PLAN, 1)], min_val=0, max_val=B - 1))

                def queries(n, b):
                    pool.tensor_tensor(tile_bias[:], bias_row[:, bass.ds(n * P, P)], ones_row[:], ALU.mult).then_inc(bias_ready, 1)
                    for m in range(DC):
                        ins = pool.tensor_tensor(q0bd[:, m, :, :], const("head16").unsqueeze(2).broadcast_to([P, 8, S]),
                                                 q0T[:, m, bass.ds(b * S, S)].unsqueeze(1).broadcast_to([P, 8, S]), ALU.mult)
                    ins.then_inc(q0bd_ready, 1)
                pool.wait_ge(bias_row_loaded, 16)
                pool.wait_ge(ones_ready, 1)
                n, b = tile_of(0)
                pool.wait_ge(q0T_ready, 2)
                queries(n, b)
                with pool.Fori(0, n_tiles) as i:
                    n, b = tile_of(i + 1)
                    pool.wait_ge(scored, 2 * i + 2)
                    queries(n, b)

            def l1_xattn():
                pool.wait_ge(xn_ready, TT * LN_AT[4] + 1)
                pool.memset(v1[:, :, :, :, 2 * HD1:], 1.0).then_inc(v1_ones, 1)
                pool.wait_ge(consts_loaded, 16)
                pool.wait_ge(q1s_loaded, 4 * 16)
                pool.wait_ge(q1_stacked, 1)
                pool.wait_ge(q1_stacked_act, 1)

                def queries(b):
                    spread_queries(pool, b, range(QG // 2, QG)).then_inc(q1bd_pool, 1)

                queries(0)
                with pool.Fori(0, B) as b:
                    pool.wait_ge(s1_scored, b * 2 * KT + 2)
                    queries(b + 1)

            if 1 in stages:
                l0_xattn()
            if 4 in stages:
                l1_xattn()

        @block.vector
        def _(v):
            chain = Chain(v, dve_chain)

            def layernorm(stage):
                s = LN_AT[stage]
                for i in range(TT):
                    ins = v.bn_stats(stats[:, i, :], x[:, i, :])
                chain(ins)
                for i in range(TT):
                    ins = v.bn_aggr(mv[:, i, :], stats[:, i, :])
                ins.then_inc(var_ready, 1)
                v.wait_ge(var_ready, s + 1)
                v.wait_ge(rstd_ready, s + 1)
                if stage == 1:
                    for i in range(TT):
                        chain(v.tensor_scalar(xn[:, i, :], x[:, i, :], mv[:, i, 0:1], rstd[:, i:i + 1],
                                              ALU.subtract, ALU.mult))
                    for i in range(TT):
                        ins = v.tensor_tensor_reduce(scratch[:, i, :], xn[:, i, :], xn[:, i, :], 1.0, 0.0,
                                                     ALU.mult, ALU.add, ms[:, i:i + 1])
                    ins.then_inc(sumsq_ready, 1)
                    v.wait_ge(rrms_ready, 1)
                    for i in range(TT):
                        v.tensor_scalar(xn[:, i, :], xn[:, i, :], rstd[:, i:i + 1], None, ALU.mult).then_inc(xn_ready, 1)
                    v.wait_ge(w0_loaded, 32)
                    v.wait_ge(xn_turned, 1)
                    v.tensor_scalar(xnT[:, 1, :], bank[1], normw[:, 1:2], None, ALU.mult).then_inc(xnT_dve, 1)
                else:
                    for i in range(TT):
                        v.tensor_scalar(xn[:, i, :], x[:, i, :], mv[:, i, 0:1], rstd[:, i:i + 1],
                                        ALU.subtract, ALU.mult).then_inc(xn_ready, 1)
                    v.wait_ge(xn_turned, s + 1)
                    v.tensor_copy(xnT[:, 1, :], bank[1]).then_inc(xnT_dve, 1)

            def plan_tiles():
                v.memset(ones_row[:], 1.0).then_inc(ones_ready, 1)
                v.wait_ge(mask_loaded, 16)
                v.tensor_reduce(tile_any[0:B * KT, :], mask_tiles[:], AX.X, ALU.max).then_inc(any_ready, 1)
                v.tensor_scalar(bias_tiles[:], mask_tiles[:], 1.0, -NEG, ALU.subtract, ALU.mult).then_inc(bias_tiles_ready, 1)
                v.wait_ge(consts_loaded, 16)
                v.wait_ge(any_turned, 1)
                v.tensor_copy(tile_at[0:NT, :], bank[0][0:NT, 0:1]).then_inc(tile_at_ready, 1)
                v.wait_ge(tile_at_ready, 1)
                v.wait_ge(any_ready, 1)
                v.tensor_scalar(tile_hot[0:NT, :], const("count")[0:NT, :], tile_at[0:NT, 0:1], tile_any[0:NT, 0:1],
                                ALU.is_equal, ALU.mult).then_inc(tile_hot_ready, 1)
                v.wait_ge(plan_turned, 1)
                v.tensor_copy(plan[:, 0:COUNT_AT], bank[1][0:1, 0:COUNT_AT])
                v.tensor_scalar(plan[:, COUNT_AT:], bank[1][0:1, COUNT_AT:COUNT_AT + 1], 1.0, None, ALU.max).then_inc(plan_ready, 1)

            def l0_xattn():
                v.wait_ge(plan_ready, 1)
                n_tiles = v.value_load(plan[0:1, COUNT_AT:COUNT_AT + 1], min_val=1, max_val=NT)
                v.memset(m_run[:], NEG)
                v.memset(v0[:, :, 2 * HD0:], 1.0)
                chain(v.memset(o_run[:], 0.0))
                steps = Chain(v, tile_chain)

                def batch_of(i):
                    return v.value_load(plan[0:1, bass.ds(i + PLAN, 1)], min_val=0, max_val=B - 1)

                def shift(i, b):
                    m_old = m_run[:, bass.ds(b, 1), :].rearrange("p o g -> p (o g)")
                    for m in range(DC):
                        v.wait_ge(scored, 2 * i + m + 1)
                        ins = v.tensor_reduce(m_tile[:, 4 * m:4 * m + 4], bank[2 + m].rearrange("p (g k) -> p g k", g=4),
                                              AX.X, ALU.max)
                    steps(ins)
                    steps(v.tensor_tensor(m_new[:], m_old, m_tile[:], ALU.max))
                    steps(v.tensor_tensor(m_step[:], m_old, m_new[:], ALU.subtract))
                    v.tensor_tensor(m_old, m_old, m_tile[:], ALU.max)
                    for m in range(DC):
                        v.tensor_tensor(probs0[:, 4 * m:4 * m + 4, :], bank[2 + m].rearrange("p (g k) -> p g k", g=4),
                                        m_new[:, 4 * m:4 * m + 4].unsqueeze(2).broadcast_to([P, 4, P]), ALU.subtract)\
                         .then_inc(shifted, 1)
                    v.wait_ge(shifted, 2 * i + 2)

                shift(0, batch_of(0))
                with v.Fori(0, n_tiles) as i:
                    PER_TILE = 4
                    began = steps.enter(i, PER_TILE)
                    v.wait_ge(turned, 2 * i + 2)
                    v.tensor_copy(probs0T[:, 4:8, :].rearrange("p g k -> p (g k)"), bank[5]).then_inc(pT_dve, 1)
                    b, b_next = batch_of(i), batch_of(i + 1)
                    o = o_run[:, bass.ds(b, 1), :, :].rearrange("p o g j -> p (o g) j")
                    shift(i + 1, b_next)
                    v.wait_ge(alpha_ready, i + 1)
                    v.tensor_tensor(o, o, alpha[:].unsqueeze(2).broadcast_to([P, G0, 2 * HD0 + 1]), ALU.mult)\
                     .then_inc(o_scaled, 1)
                    v.wait_ge(o_scaled, i + 2)
                    v.wait_ge(attended, i + 1)
                    steps(v.tensor_tensor(o, o, bank[6][:, 0:G0 * (2 * HD0 + 1)].rearrange("p (g j) -> p g j", g=G0), ALU.add))
                    steps.leave(began, 1)
                chain(v.tensor_scalar(l_inv[:], o_run[:, :, :, 2 * HD0], 1e-30, None, ALU.max))
                chain(v.reciprocal(l_inv[:], l_inv[:]))
                chain(v.tensor_scalar(m_run[:], m_run[:], 0.1 * NEG, None, ALU.is_gt))
                chain(v.tensor_tensor(l_inv[:], l_inv[:], m_run[:], ALU.mult))
                for half in range(2):
                    own = slice(half * B // 2, (half + 1) * B // 2)
                    n = B * G0 // 2
                    flat_o = o_norm[:, own].rearrange("p b g j -> p (b g) j")
                    chain(v.tensor_tensor(flat_o, o_run[:, own].rearrange("p b g j -> p (b g) j")[:, :, 0:2 * HD0],
                                          l_inv[:, own].rearrange("p b g -> p (b g)").unsqueeze(2).broadcast_to([P, n, 2 * HD0]), ALU.mult))
                    v.tensor_tensor(flat_o, flat_o, const("own16").unsqueeze(1).broadcast_to([P, n, 2 * HD0]), ALU.mult)\
                     .then_inc(o_norm_ready, 1)
                v.wait_ge(gate_exp, 1)
                chain(v.tensor_scalar(gate[:], gate[:], 1.0, None, ALU.add))
                chain(v.reciprocal(gate[:], gate[:]))
                v.wait_ge(out0_projected, 1)
                for i in range(TT):
                    ins = v.tensor_tensor(scratch[:, i, :], bank[4 + i][:, 0:D], gate[:, i, :], ALU.mult)
                chain(ins)
                chain(v.tensor_tensor(x[:], x[:], scratch[:], ALU.add))

            def l0_attn():
                PER_PAIR = 2
                with v.Fori(0, HA // 4) as i:
                    began = chain.enter(i, 2 * PER_PAIR)
                    for k in range(2):
                        n = i * 2 + k
                        for u in range(2):
                            v.wait_ge(kqa_projected, 2 * n + u + 1)
                            v.tensor_copy(qaT[:, u, :], bank[3 * u + 1]).then_inc(qa_ready, 1)
                        for u in range(2):
                            v.wait_ge(a_scored, 2 * n + u + 1)
                            chain(v.tensor_reduce(maxa[:, u, :], bank[6 + u].rearrange("p (t k) -> p t k", t=TT), AX.X, ALU.max))
                            v.tensor_scalar(maxa[:, u, :], maxa[:, u, :], -HDA ** -0.5, None, ALU.mult).then_inc(a_maxed, 1)
                        for u in range(2):
                            v.wait_ge(a_exped, 2 * n + u + 1)
                            v.reciprocal(suma[:, u, :], suma[:, u, :]).then_inc(a_summed, 1)
                            v.wait_ge(a_summed, 2 * n + u + 1)
                            v.tensor_tensor(pa[:, u, :, :], pa[:, u, :, :],
                                            suma[:, u, :].unsqueeze(2).broadcast_to([P, TT, P]), ALU.mult).then_inc(a_normed, 1)
                            v.wait_ge(va_projected, 2 * n + u + 1)
                            v.tensor_copy(va[:, 2 * u:2 * u + 2, :].rearrange("p t f -> p (t f)"), bank[2 + 3 * u]).then_inc(va_ready, 1)
                        for u in range(2):
                            v.wait_ge(a_mixed, 2 * n + u + 1)
                            v.tensor_copy(zaT[:, u, :], bank[1 + 3 * u]).then_inc(zaT_ready, 1)
                        v.wait_ge(a_out, n + 1)
                        for j in range(2):
                            ins = v.tensor_tensor(x[:, 2 * j:2 * j + 2, :], x[:, 2 * j:2 * j + 2, :],
                                                  bank[2 + 3 * j].rearrange("p (t f) -> p t f", t=2), ALU.add)
                        ins.then_inc(a_added, 1)
                        v.wait_ge(a_added, n + 2)
                    chain.leave(began, HA // 4)

            def l1_xattn():
                def queries(b):
                    spread_queries(v, b, range(QG // 2)).then_inc(q1bd_ready, 1)

                def copy_k(b, j):
                    w = (CHUNK[j + 1] - CHUNK[j]) * P
                    v.wait_ge(k1_projected, b * NCH + j + 1)
                    v.tensor_copy(k1f[:, :, 0:w], pair[0][:].rearrange("p (m k) -> p m k", m=DC)[:, :, 0:w]).then_inc(k1_copied, 1)

                def split_k(b, j, scored_before=None):
                    n = b * NCH + j
                    w = (CHUNK[j + 1] - CHUNK[j]) * P
                    v.wait_ge(k1_copied, n + 1)
                    v.wait_ge(r1_ready, n + 1)
                    v.tensor_tensor(k1f[:, :, 0:w], k1f[:, :, 0:w], r1[:, :, 0:w], ALU.mult).then_inc(k1_normed, 1)
                    v.wait_ge(k1_normed, n + 1)
                    if not (isinstance(n, int) and n == 0):
                        v.wait_ge(k1s_loaded, 6 * 16 * n)
                        v.wait_ge(k1_stacked_act, n)
                        v.wait_ge(s1_scored, scored_before)
                    v.tensor_copy(parts[:, 0, :, 0:w], k1f[:, :, 0:w]).then_inc(k1_high, 1)
                    v.wait_ge(k1_high, n + 1)
                    v.tensor_tensor(parts[:, 1, :, 0:w], k1f[:, :, 0:w], parts[:, 0, :, 0:w], ALU.subtract).then_inc(k1_split, 1)
                    v.wait_ge(k1_split, n + 1)
                    for i, part in ((0, 0), (1, 1)):
                        for q in range(P // QR):
                            ins = v.tensor_copy(piece(k1s[j % 2], i, q, w), part_rows(parts, part, q, w))
                    ins.then_inc(k1_stacked, 1)

                def copy_v(b, j, t):
                    v.wait_ge(v1_projected, b * KT + t + 1)
                    v.tensor_copy(v1[:, j % 2, t - CHUNK[j], :, 0:2 * HD1], bank[2][:, 0:D].rearrange("p (g j) -> p g j", g=G1))\
                     .then_inc(v1_copied, 1)

                v.wait_ge(q1_squared, 1)
                for m in range(DC):
                    ins = v.tensor_copy(q1T[:, m, :], bank[4 + m])
                ins.then_inc(q1_copied, 1)
                copy_k(0, 0)
                copy_v(0, 0, 0)
                v.wait_ge(q1_copied, 1)
                v.wait_ge(q1_r, 1)
                chain(v.tensor_tensor(q1T, q1T, q1r[:], ALU.mult))
                v.tensor_copy(q1parts[:, 0], q1T).then_inc(q1_high, 1)
                v.wait_ge(q1_high, 1)
                v.tensor_tensor(q1parts[:, 1], q1T, q1parts[:, 0], ALU.subtract).then_inc(q1_split, 1)
                copy_v(0, 0, 1)
                v.wait_ge(q1_split, 1)
                for i, part in ((1, 0), (2, 1)):
                    for q in range(4):
                        ins = v.tensor_copy(piece(q1s, i, q, T), part_rows(q1parts, part, q, T))
                ins.then_inc(q1_stacked, 1)
                split_k(0, 0)
                copy_k(0, 1)
                for t in range(2, CHUNK[1]):
                    copy_v(0, 0, t)
                v.wait_ge(q1s_loaded, 4 * 16)
                v.wait_ge(q1_stacked, 1)
                v.wait_ge(q1_stacked_act, 1)
                queries(0)
                PER_BATCH = 2
                with v.Fori(0, B) as b:
                    began = chain.enter(b, PER_BATCH)
                    for j in range(NCH):
                        b1, j1 = after(b, j, 1)
                        b2, j2 = after(b, j, 2)
                        values = list(range(CHUNK[j1], CHUNK[j1 + 1]))
                        copy_v(b1, j1, values[0])
                        split_k(b1, j1, (b * KT + CHUNK[j]) * 2 + 2)
                        copy_k(b2, j2)
                        for t in values[1:3]:
                            copy_v(b1, j1, t)
                        if j == 0:
                            v.wait_ge(s1_scored, b * 2 * KT + 2)
                            queries(b + 1)
                    v.wait_ge(p1_used, (b + 1) * KT + 2)
                    v.tensor_copy(acc1, bank[3]).then_inc(acc1_copied, 1)
                    v.wait_ge(acc1_turned, b + 1)
                    o = bank[3].rearrange("p (g r) -> p g r", g=G1)
                    chain(v.reciprocal(rden1[:], o[:, :, 2 * HD1]))
                    chain(v.tensor_tensor(on1[:], o[:, :, 0:2 * HD1], rden1[:].unsqueeze(2).broadcast_to([P, G1, 2 * HD1]), ALU.mult))
                    v.tensor_tensor(on1[:], on1[:], const("own8").unsqueeze(1).broadcast_to([P, G1, 2 * HD1]), ALU.mult)\
                     .then_inc(on1_ready, 1)
                    copy_v(b1, j1, values[3])
                    v.wait_ge(o1_folded, b + 1)
                    v.tensor_copy(o1T[:, :, bass.ds(b * S, S)], bank[3][:, 0:DC * S].rearrange("p (c q) -> p c q", c=DC))\
                     .then_inc(o1T_ready, 1)
                    chain.leave(began, B)
                v.wait_ge(o1_turned, 1)
                for i in range(TT):
                    ins = v.tensor_tensor(x[:, i, :], x[:, i, :], bank[i][:, 0:D], ALU.add)
                chain(ins)

            def l1_attn():
                def rotate(t):
                    v.wait_ge(qkv_projected, t + 1)
                    z = bank[2 + t][:, 0:NR * HDB].rearrange("p (h d) -> p h d", h=NR)
                    hd = HDB // 2
                    cos, sin = const("cos"), const("sin")
                    v.tensor_tensor(rot[:, t, :, :], z, cos.unsqueeze(1).broadcast_to([P, NR, HDB]), ALU.mult)
                    v.tensor_tensor(rot2[:, t, :, 0:hd], z[:, :, hd:], sin[:, 0:hd].unsqueeze(1).broadcast_to([P, NR, hd]), ALU.mult)
                    v.tensor_tensor(rot2[:, t, :, hd:], z[:, :, 0:hd], sin[:, hd:].unsqueeze(1).broadcast_to([P, NR, hd]), ALU.mult)
                    chain(v.tensor_copy(vb[:, t, :], bank[2 + t][:, NR * HDB:QKV]))
                    chain(v.tensor_tensor(rot[:, t, :, :], rot[:, t, :, :], rot2[:, t, :, :], ALU.add))
                    v.tensor_copy(krep[:, t, :, :], rot[:, t, HB:NR, :].broadcast_to([P, 8, HDB])).then_inc(rotated, 1)

                def copy_k(t):
                    v.wait_ge(qk_turned, t + 1)
                    v.wait_ge(qbT_ready, t + 1)
                    v.tensor_tensor(kbd[t % 2][:], const("head16").unsqueeze(2).broadcast_to([P, 8, P]),
                                    bank[0][:, 2 * P:3 * P].unsqueeze(1).broadcast_to([P, 8, P]), ALU.mult).then_inc(kbd_ready, 1)

                def maximum(j):
                    v.wait_ge(b_scored, j + 1)
                    chain(v.tensor_reduce(maxb[:, j, :], score_bank(j).rearrange("p (h k) -> p h k", h=4), AX.X, ALU.max))
                    v.tensor_scalar(maxb[:, j, :], maxb[:, j, :], -HDB ** -0.5, None, ALU.mult).then_inc(b_maxed, 1)

                rotate(0)
                rotate(1)
                copy_k(0)
                rotate(2)
                maximum(0)
                rotate(3)
                for j in range(NJ + 3):
                    if j + 1 < NJ:
                        maximum(j + 1)
                    if j % 4 == 0 and j // 4 + 1 < TT:
                        copy_k(j // 4 + 1)
                    if j < NJ:
                        v.wait_ge(b_turned, j + 1)
                        if j >= 2:
                            v.wait_ge(b_mixed, j - 1)
                        v.tensor_copy(paT[:, j % 2, :, :].rearrange("p t q -> p (t q)"), bank[1 + 2 * (j % 2)]).then_inc(pbT_ready, 1)
                    t = j // 4 - 1
                    if t >= 0 and j % 4 == 0:
                        v.wait_ge(b_mixed, 4 * t + 4)
                        sums = sumb[:, 4 * t:4 * t + 4, :].rearrange("p j h -> p (j h)")
                        v.reciprocal(sums, sums).then_inc(b_summed, 1)
                        v.wait_ge(b_summed, t + 1)
                        v.tensor_tensor(ob[:, t, :].rearrange("p (h d) -> p h d", h=HB),
                                        bank[2][:, 0:D].rearrange("p (h d) -> p h d", h=HB),
                                        sums.unsqueeze(2).broadcast_to([P, HB, HDB]), ALU.mult).then_inc(ob_ready, 1)
                    if t >= 0 and j % 4 == 1:
                        v.wait_ge(ob_turned, t + 1)
                        v.tensor_copy(obT[:, :, t * P:(t + 1) * P], bank[4][:, 0:D].rearrange("p (c q) -> p c q", c=DC)).then_inc(obT_ready, 1)
                    if t >= 0 and j % 4 == 2:
                        v.wait_ge(b_out, t + 1)
                        v.tensor_tensor(x[:, t, :], x[:, t, :], bank[4][:, D:2 * D], ALU.add).then_inc(b_added, 1)
                v.wait_ge(b_added, TT)

            def softmax_rows(r, ne):
                v.wait_ge(r_scored, r * R1 + 1)
                p = pr[:, :, 0:ne]
                logits = bank[7][:, 0:TT * ne].rearrange("p (t e) -> p t e", t=TT)
                if r == 1:
                    chain(v.tensor_tensor(p, logits, bias1[:].unsqueeze(1).broadcast_to([P, TT, E1]), ALU.add))
                    logits = p
                chain(v.tensor_reduce(rmax[:], logits, AX.X, ALU.max))
                v.tensor_tensor(p, logits, rmax[:].unsqueeze(2).broadcast_to([P, TT, ne]), ALU.subtract).then_inc(r_shifted, 1)
                v.wait_ge(r_exped, r * R1 + 1)
                chain(v.tensor_reduce(rmax[:], p, AX.X, ALU.add))
                chain(v.reciprocal(rmax[:], rmax[:]))
                chain(v.tensor_tensor(p, p, rmax[:].unsqueeze(2).broadcast_to([P, TT, ne]), ALU.mult))
                for t in range(TT):
                    ins = v.max(mx8[:, t, :], pr[:, t, 0:ne])
                chain(ins)

            def router0():
                chain(v.tensor_copy(merge_f[:], merge_i[:]))
                chain(v.tensor_scalar(onehot[:], const("group")[0:E0, :], merge_f[:, 0:1], None, ALU.is_equal))
                softmax_rows(0, E0)
                for t in range(TT):
                    ins = v.match_replace(rep[:, t, :], mx8[:, t, :], pr[:, t, :], 0.0)
                chain(ins)
                chain(v.tensor_tensor(pr[:], pr[:], rep[:], ALU.subtract))
                chain(v.tensor_reduce(rmax[:], mx8[:], AX.X, ALU.add))
                chain(v.reciprocal(rmax[:], rmax[:]))
                v.tensor_tensor(pr[:], pr[:], rmax[:].unsqueeze(2).broadcast_to([P, TT, E0]), ALU.mult).then_inc(sel_ready, 1)
                v.wait_ge(sel_turned, 1)
                v.tensor_copy(selT[:], bank[6][0:E0, :]).then_inc(selT_ready, 1)
                v.wait_ge(w_summed, 1)
                v.tensor_copy(we[:, :, 0:G], bank[5][:, 0:TT * G].rearrange("p (t g) -> p t g", t=TT)).then_inc(we_ready, 1)
                v.wait_ge(we_ready, 1)

            def router1():
                chain(v.memset(pr[:, :, E1:E1 + 8], -1.0))
                chain(v.memset(pick[:], -1.0))
                softmax_rows(1, E1)
                chain(v.tensor_copy(pick[:, :, 0:2], mx8[:, :, 0:2]))
                for t in range(TT):
                    ins = v.match_replace(rep[:, t, 0:E1 + 8], pick[:, t, :], pr[:, t, 0:E1 + 8], 0.0)
                chain(ins)
                chain(v.tensor_tensor(we[:, :, 0:E1], pr[:, :, 0:E1], rep[:, :, 0:E1], ALU.subtract))
                chain(v.tensor_reduce(rmax[:], mx8[:, :, 0:2], AX.X, ALU.add))
                chain(v.tensor_scalar(rmax[:], rmax[:], 1e-9, None, ALU.add))
                chain(v.reciprocal(rmax[:], rmax[:]))
                chain(v.tensor_tensor(we[:, :, 0:E1], we[:, :, 0:E1], rmax[:].unsqueeze(2).broadcast_to([P, TT, E1]), ALU.mult))
                v.memset(we[:, :, E1:NX], 1.0).then_inc(we_ready, 1)
                v.wait_ge(we_ready, R1 + 1)

            def experts(n0, count, width, one_more):
                def hidden(k, n):
                    v.wait_ge(silu_ready, n + 1)
                    v.tensor_tensor(hid[k][0:width, :], hid[k][0:width, :], bank[2 * (k % 2) + 1][0:width, :], ALU.mult)\
                     .then_inc(hid_ready, 1)

                def add(k, n, e):
                    v.wait_ge(e_down, n + 1)
                    for t in range(TT):
                        ins = v.scalar_tensor_tensor(x[:, t, :], bank[4 + 2 * (k % 2) + t // 2][:, (t % 2) * D:(t % 2 + 1) * D],
                                                     we[:, t, bass.ds(e, 1)], x[:, t, :], ALU.mult, ALU.add)
                    ins.then_inc(e_added, 1)
                    v.wait_ge(e_added, n + 2)
                with v.Fori(0, count // NB) as i:
                    for k in range(0, NB, 2):
                        n = n0 + i * NB + k
                        hidden(k, n)
                        hidden(k + 1, n + 1)
                        add(k, n, i * NB + k)
                        add(k + 1, n + 1, i * NB + k + 1)
                if one_more:
                    hidden(0, n0 + count)
                    add(0, n0 + count, count)

            for free in (a_added, e_added, o1T_ready):
                v.sem_inc(free, 1)
            v.memset(eps[:, 0:1], LN_EPS).then_inc(eps_ready, 1)
            v.memset(eps[:, 1:2], RMS_EPS).then_inc(eps_ready, 1)
            v.wait_ge(consts_loaded, 16)
            v.tensor_copy(ident_b[:], ident)
            v.tensor_copy(causal_b[:], const("causal"))
            v.tensor_copy(block_b[:], const("block")).then_inc(masks_ready, 1)
            v.wait_ge(x_loaded, 16)
            v.wait_ge(consts_loaded, 16)
            if 1 in stages:
                plan_tiles()
                layernorm(1)
                l0_xattn()
            if 2 in stages:
                layernorm(2)
                l0_attn()
            if 3 in stages:
                layernorm(3)
                v.wait_ge(router_loaded, 80)
                router0()
                experts(0, G, I0, False)
            if 4 in stages:
                layernorm(4)
                l1_xattn()
            if 5 in stages:
                layernorm(5)
                l1_attn()
            if 6 in stages:
                layernorm(6)
                v.wait_ge(router_loaded, 80)
                router1()
                experts(N1, E1, I1, True)
            v.sem_inc(dve_done, 1)



def layout(inputs):
    f = {k: np.asarray(v) for k, v in inputs.items()}

    def wide(w):
        return w.reshape(DC, P, -1).transpose(1, 0, 2)

    ctxT = np.zeros((B, D, S2P), np.float32)
    ctxT[:, :, :S2] = f["ctx_2048"].transpose(0, 2, 1)
    mask = np.zeros((B, S2P), bool)
    mask[:, :S2] = f["mask_BxS2_bk0"]
    kv1 = np.concatenate([f["L1_xattn_Wk"], f["L1_xattn_Wv"]], 0)
    r = {
        "x": f["x"],
        "const": CONST,
        "w0": np.stack([wide(f[f"L0_xattn_{n}"].T) for n in ("wq", "wg", "wk", "wv", "wo")], 1),
        "norm_w": f["L0_xattn_norm_w"].reshape(DC, P).T,
        "wa": np.concatenate([
            np.stack([f["L0_attn_W_K"], f["L0_attn_W_Q"]], 1).reshape(HA // 2, 2, 2, HDA, DC, P)
              .transpose(0, 5, 1, 2, 4, 3).reshape(HA // 2, P, -1),
            f["L0_attn_W_V"].reshape(HA // 2, 2 * HDA, DC, P).transpose(0, 3, 2, 1).reshape(HA // 2, P, -1),
            f["L0_attn_W_O"].reshape(D, HA // 2, 2, HDA).transpose(1, 3, 2, 0).reshape(HA // 2, P, -1)], 2),
        "w1": np.stack([wide(w.T) for w in (f["L1_xattn_Wq"], kv1[0::2], kv1[1::2])], 1),
        "wqkv": wide(f["L1_attn_w_attn"]),
        "wout": wide(f["L1_attn_w_out"]),
        "gu0": f["L0_ffn_gate_up_proj"].reshape(E0, 2, I0, DC, P).transpose(0, 4, 3, 1, 2),
        "dn0": f["L0_ffn_down_proj"].transpose(0, 2, 1),
        "wr0": wide(f["L0_ffn_gate_weight"].T),
        "merge": f["L0_ffn_merge_groups"].reshape(E0, 1),
        "dom": f["L0_ffn_dominant_experts"].reshape(1, G),
        "gu1": np.stack([np.concatenate([f["L1_ffn_W" + n], f["L1_ffn_sW" + n][None]], 0) for n in "gu"], 1)
                 .reshape(NX, 2, DC, P, I1).transpose(0, 3, 2, 1, 4),
        "dn1": np.concatenate([f["L1_ffn_Wd"], f["L1_ffn_sWd"][None]], 0),
        "wr1": wide(f["L1_ffn_Wr"].T),
        "bias1": f["L1_ffn_bias"].reshape(1, E1),
        "mask": mask.reshape(B * KT, P),
        "ctxT": ctxT.reshape(B, DC, P, KT, P).transpose(0, 3, 2, 1, 4).reshape(B * KT, P, DC, P),
    }
    return {k: np.ascontiguousarray(v) for k, v in r.items()}


def kernel(**inputs):
    import concourse.bacc as _bacc
    from concourse.bass_utils import run_bass_kernel_spmd as _run

    nc = _bacc.Bacc("TRN2", target_bir_lowering=False, num_devices=1)
    arrays = layout(inputs)
    aps = {k: nc.dram_tensor(f"in_{k}", v.shape, mybir.dt.from_np(v.dtype), kind="ExternalInput").ap()
           for k, v in arrays.items()}
    out = nc.dram_tensor("out_x", (B, S, D), F32, kind="ExternalOutput").ap()
    build(nc, aps, out)
    r = _run(nc, [{f"in_{k}": v for k, v in arrays.items()}], core_ids=[0])
    return r.results[0]["out_x"]
```
